# Optimizing a Trainium2 kernel written in Bass

```python
import numpy as np
import jax
import jax.numpy as jnp

def _softmax(x, axis=-1):
    return jax.nn.softmax(x, axis=axis)

def _gelu(x):
    return jax.nn.gelu(x, approximate=True)

def _silu(x):
    return jax.nn.silu(x)

def _sigmoid(x):
    return jax.nn.sigmoid(x)

def _layernorm(x, axis=-1, eps=1e-05):
    m = jnp.mean(x, axis=axis, keepdims=True)
    v = jnp.var(x, axis=axis, keepdims=True)
    return (x - m) / jnp.sqrt(v + eps)

def _scatter_add(tgt, idx, src, axis=0):
    return tgt.at[idx].add(src)

def _segment_sum(src, seg, n):
    return jax.ops.segment_sum(src, seg, n)
kernel_name = 'mk_decoder_postln_d1_seqx_r4_331bc4'

def setup_inputs(seed: int=0):
    np.random.seed(seed)
    _w = jnp.asarray

    def _rec_inputs():
        import jax
        import jax.numpy as jnp
        _rk = jax.random.key(seed)
        x = -7.109e-05 + 0.9999 * jax.random.normal(jax.random.fold_in(_rk, 1), (16, 112, 1024), jnp.float32)
        _lenS = 112 - jax.random.randint(jax.random.fold_in(_rk, 7), (16,), 0, max(1, 112 // 4) + 1, jnp.int32)
        _lenS2 = 375 - jax.random.randint(jax.random.fold_in(_rk, 8), (16,), 0, max(1, 375 // 4) + 1, jnp.int32)
        _ctx_4096P = jax.random.normal(jax.random.fold_in(_rk, 11), (16, 16, 1024), jnp.float32)
        _ctx_4096c = jax.random.dirichlet(jax.random.fold_in(_rk, 511), 0.3 * jnp.ones((16,), jnp.float32), (16, 375))
        _ctx_4096t = jnp.einsum('bsk,bkd->bsd', _ctx_4096c, _ctx_4096P)
        _ctx_4096t = _ctx_4096t * jax.lax.rsqrt(jnp.mean(jnp.square(_ctx_4096t)) + 1e-12) * 0.953939
        ctx_4096 = -2.6191e-05 + 0.999952 * (_ctx_4096t + 0.3 * jax.random.normal(jax.random.fold_in(_rk, 611), (16, 375, 1024), jnp.float32))
        return (x, ctx_4096)
    x, ctx_4096 = _rec_inputs()

    def _L0_attn_setup():
        import jax, jax.numpy as jnp
        import numpy as np
        H = 1024
        D = H // 4
        key = jax.random.key(seed)
        k1, k2, k3, k4, k5 = jax.random.split(key, 5)
        x = jax.random.normal(k1, (4, 1024, H), dtype=jnp.float32)
        s_in = 1.0 / np.sqrt(H)
        Wqkv = jax.random.normal(k2, (H, 3 * D), dtype=jnp.float32) * s_in
        bqkv = jax.random.normal(k3, (3 * D,), dtype=jnp.float32) * 0.01
        Wo = jax.random.normal(k4, (D, H), dtype=jnp.float32) * (1.0 / np.sqrt(D))
        bo = jax.random.normal(k5, (H,), dtype=jnp.float32) * 0.01
        return {'x': x, 'Wqkv': Wqkv, 'bqkv': bqkv, 'Wo': Wo, 'bo': bo}
    _L0_attn_all = _L0_attn_setup()
    _L0_attn_in = {k: v for k, v in _L0_attn_all.items() if k in ('Wqkv', 'bqkv', 'Wo', 'bo')}
    del _L0_attn_all

    def _L0_xattn_setup():
        import jax, jax.numpy as jnp
        import numpy as np
        TEXT_DIM = 1024
        FEATURE_DIM = 1024

        def _xavier_uniform(key, shape):
            fan_in, fan_out = (shape[1], shape[0])
            limit = float(np.sqrt(6.0 / (fan_in + fan_out)))
            return jax.random.uniform(key, shape, jnp.float32, -limit, limit)
        key = jax.random.key(seed)
        k1, k2, k3, k4 = jax.random.split(key, 4)
        text = jax.random.normal(k1, (8, 512, TEXT_DIM), jnp.float32)
        features = jax.random.normal(k2, (8, 144, FEATURE_DIM), jnp.float32)
        Wq = _xavier_uniform(k3, (FEATURE_DIM, TEXT_DIM))
        bq = jnp.zeros((FEATURE_DIM,), jnp.float32)
        Wk = _xavier_uniform(k4, (FEATURE_DIM, FEATURE_DIM))
        bk = jnp.zeros((FEATURE_DIM,), jnp.float32)
        return {'text': text, 'features': features, 'Wq': Wq, 'bq': bq, 'Wk': Wk, 'bk': bk}
    _L0_xattn_all = _L0_xattn_setup()
    _L0_xattn_in = {k: v for k, v in _L0_xattn_all.items() if k in ('Wq', 'bq', 'Wk', 'bk')}
    del _L0_xattn_all

    def _L0_ffn_setup():
        import jax, jax.numpy as jnp
        import numpy as np
        HID = 1024
        INTER = 2752
        BITS = 4
        PACK = 8
        MAXQ = 15
        GROUP = 128

        def _dequant(qweight, scales, qzeros, g_idx):
            shifts = jnp.arange(PACK, dtype=jnp.uint32) * BITS
            qw = qweight.astype(jnp.uint32)
            w = (qw[:, None, :] >> shifts[None, :, None] & MAXQ).reshape(-1, qweight.shape[1])
            qz = qzeros.astype(jnp.uint32)
            z = ((qz[:, :, None] >> shifts[None, None, :] & MAXQ) + 1).reshape(qzeros.shape[0], -1)
            s = scales[g_idx]
            return (w.astype(scales.dtype) - z[g_idx].astype(scales.dtype)) * s
        key = jax.random.key(seed)
        ks = jax.random.split(key, 16)

        def qw(k, K, N):
            return jax.random.randint(k, (K // PACK, N), 0, 2147483647, dtype=jnp.int32)

        def qz(k, G, N):
            return jax.random.randint(k, (G, N // PACK), 0, 2147483647, dtype=jnp.int32)

        def sc(k, G, N):
            return jax.random.uniform(k, (G, N), jnp.float32, 0.001, 0.01)
        Gk = HID // GROUP
        Gd = INTER // GROUP
        return {'x': jax.random.normal(ks[0], (4, 512, HID), jnp.float32), 'gate_qweight': qw(ks[1], HID, INTER), 'gate_scales': sc(ks[2], Gk, INTER), 'gate_qzeros': qz(ks[3], Gk, INTER), 'gate_g_idx': (jnp.arange(HID) // GROUP).astype(jnp.int32), 'up_qweight': qw(ks[4], HID, INTER), 'up_scales': sc(ks[5], Gk, INTER), 'up_qzeros': qz(ks[6], Gk, INTER), 'up_g_idx': (jnp.arange(HID) // GROUP).astype(jnp.int32), 'down_qweight': qw(ks[7], INTER, HID), 'down_scales': sc(ks[8], Gd, HID), 'down_qzeros': qz(ks[9], Gd, HID), 'down_g_idx': (jnp.arange(INTER) // GROUP).astype(jnp.int32)}
    _L0_ffn_all = _L0_ffn_setup()
    _L0_ffn_in = {k: v for k, v in _L0_ffn_all.items() if k in ('gate_qweight', 'gate_scales', 'gate_qzeros', 'gate_g_idx', 'up_qweight', 'up_scales', 'up_qzeros', 'up_g_idx', 'down_qweight', 'down_scales', 'down_qzeros', 'down_g_idx')}
    del _L0_ffn_all
    return {'x': x, 'ctx_4096': ctx_4096, 'L0_attn_Wqkv': _L0_attn_in['Wqkv'], 'L0_attn_bqkv': _L0_attn_in['bqkv'], 'L0_attn_Wo': _L0_attn_in['Wo'], 'L0_attn_bo': _L0_attn_in['bo'], 'L0_xattn_Wq': _L0_xattn_in['Wq'], 'L0_xattn_bq': _L0_xattn_in['bq'], 'L0_xattn_Wk': _L0_xattn_in['Wk'], 'L0_xattn_bk': _L0_xattn_in['bk'], 'L0_ffn_gate_qweight': _L0_ffn_in['gate_qweight'], 'L0_ffn_gate_scales': _L0_ffn_in['gate_scales'], 'L0_ffn_gate_qzeros': _L0_ffn_in['gate_qzeros'], 'L0_ffn_gate_g_idx': _L0_ffn_in['gate_g_idx'], 'L0_ffn_up_qweight': _L0_ffn_in['up_qweight'], 'L0_ffn_up_scales': _L0_ffn_in['up_scales'], 'L0_ffn_up_qzeros': _L0_ffn_in['up_qzeros'], 'L0_ffn_up_g_idx': _L0_ffn_in['up_g_idx'], 'L0_ffn_down_qweight': _L0_ffn_in['down_qweight'], 'L0_ffn_down_scales': _L0_ffn_in['down_scales'], 'L0_ffn_down_qzeros': _L0_ffn_in['down_qzeros'], 'L0_ffn_down_g_idx': _L0_ffn_in['down_g_idx']}

def reference(x, ctx_4096, L0_attn_Wqkv, L0_attn_bqkv, L0_attn_Wo, L0_attn_bo, L0_xattn_Wq, L0_xattn_bq, L0_xattn_Wk, L0_xattn_bk, L0_ffn_gate_qweight, L0_ffn_gate_scales, L0_ffn_gate_qzeros, L0_ffn_gate_g_idx, L0_ffn_up_qweight, L0_ffn_up_scales, L0_ffn_up_qzeros, L0_ffn_up_g_idx, L0_ffn_down_qweight, L0_ffn_down_scales, L0_ffn_down_qzeros, L0_ffn_down_g_idx):
    import jax
    import jax.numpy as jnp

    def _L0_attn_ref(x, Wqkv, bqkv, Wo, bo):
        import jax, jax.numpy as jnp
        import numpy as np
        H = 1024
        D = H // 4
        B, S, C = x.shape
        d = C // 4
        qkv = jnp.einsum('bsc,cf->bsf', x, Wqkv) + bqkv
        qkv = qkv.reshape(B, S, 3, d)
        q, k, v = (qkv[:, :, 0], qkv[:, :, 1], qkv[:, :, 2])
        scale = 1.0 / jnp.sqrt(jnp.float32(d)).astype(x.dtype)
        attn = jnp.einsum('bqd,bkd->bqk', q, k) * scale
        attn = jax.nn.softmax(attn, axis=-1)
        out = jnp.einsum('bqk,bkd->bqd', attn, v)
        return jnp.einsum('bqd,dc->bqc', out, Wo) + bo

    def _L0_xattn_ref(text, features, Wq, bq, Wk, bk):
        import jax, jax.numpy as jnp
        import numpy as np
        TEXT_DIM = 1024
        FEATURE_DIM = 1024

        def _xavier_uniform(key, shape):
            fan_in, fan_out = (shape[1], shape[0])
            limit = float(np.sqrt(6.0 / (fan_in + fan_out)))
            return jax.random.uniform(key, shape, jnp.float32, -limit, limit)
        Q = jnp.einsum('btx,dx->btd', text, Wq) + bq
        K = jnp.einsum('bpx,dx->bpd', features, Wk) + bk
        scale = 1.0 / jnp.sqrt(jnp.asarray(K.shape[-1], K.dtype))
        scores = jnp.einsum('btd,bpd->btp', Q, K) * scale
        attn = jax.nn.softmax(scores, axis=-1)
        attended = jnp.einsum('btp,bpd->btd', attn, features)
        return attended

    def _L0_ffn_ref(x, gate_qweight, gate_scales, gate_qzeros, gate_g_idx, up_qweight, up_scales, up_qzeros, up_g_idx, down_qweight, down_scales, down_qzeros, down_g_idx):
        import jax, jax.numpy as jnp
        import numpy as np
        HID = 1024
        INTER = 2752
        BITS = 4
        PACK = 8
        MAXQ = 15
        GROUP = 128

        def _dequant(qweight, scales, qzeros, g_idx):
            shifts = jnp.arange(PACK, dtype=jnp.uint32) * BITS
            qw = qweight.astype(jnp.uint32)
            w = (qw[:, None, :] >> shifts[None, :, None] & MAXQ).reshape(-1, qweight.shape[1])
            qz = qzeros.astype(jnp.uint32)
            z = ((qz[:, :, None] >> shifts[None, None, :] & MAXQ) + 1).reshape(qzeros.shape[0], -1)
            s = scales[g_idx]
            return (w.astype(scales.dtype) - z[g_idx].astype(scales.dtype)) * s
        Wg = _dequant(gate_qweight, gate_scales, gate_qzeros, gate_g_idx)
        Wu = _dequant(up_qweight, up_scales, up_qzeros, up_g_idx)
        Wd = _dequant(down_qweight, down_scales, down_qzeros, down_g_idx)
        xf = x.reshape(-1, x.shape[-1])
        h = jax.nn.silu(xf @ Wg) * (xf @ Wu)
        out = h @ Wd
        return out.reshape(x.shape[:-1] + (Wd.shape[1],))
    x = _layernorm(x + _L0_attn_ref(x, L0_attn_Wqkv, L0_attn_bqkv, L0_attn_Wo, L0_attn_bo), axis=-1)
    x = _layernorm(x + _L0_xattn_ref(x, ctx_4096, L0_xattn_Wq, L0_xattn_bq, L0_xattn_Wk, L0_xattn_bk), axis=-1)
    x = _layernorm(x + _L0_ffn_ref(x, L0_ffn_gate_qweight, L0_ffn_gate_scales, L0_ffn_gate_qzeros, L0_ffn_gate_g_idx, L0_ffn_up_qweight, L0_ffn_up_scales, L0_ffn_up_qzeros, L0_ffn_up_g_idx, L0_ffn_down_qweight, L0_ffn_down_scales, L0_ffn_down_qzeros, L0_ffn_down_g_idx), axis=-1)
    return x

_drawn_inputs = setup_inputs


def setup_inputs(seed=0):
    import zlib

    import numpy as np

    out = dict(_drawn_inputs(seed))
    spreads = {'L0_xattn_bq': (0.0, 0.294), 'L0_xattn_bk': (0.0, 0.8)}
    factors = {'L0_attn_bqkv': 4.899, 'L0_attn_bo': 5.218}
    for name, (base, spread) in spreads.items():
        noise = np.random.default_rng([zlib.crc32(name.encode()), seed]).standard_normal(out[name].shape)
        drawn = base * np.exp(spread * noise) if base else spread * noise
        out[name] = jnp.asarray(drawn.astype(out[name].dtype))
    for name, factor in factors.items():
        out[name] = (out[name] * factor).astype(out[name].dtype)
    return out
```

```python
from contextlib import ExitStack

import numpy as np

import concourse.bass as bass
from concourse import mybir

F32 = mybir.dt.float32
F16 = mybir.dt.float16
BF16 = mybir.dt.bfloat16
I32 = mybir.dt.int32
U32 = mybir.dt.uint32
ALU = mybir.AluOpType
ACT = mybir.ActivationFunctionType
AX = mybir.AxisListType
RMAX = bass.bass_isa.ReduceOp.max

P = 128
EPS = 1e-5
PASSES = ((0, 0), (0, 1), (1, 0))


def decoder_layer(nc, t_in, out):
    x_d, ctx_d = t_in["x"], t_in["ctx_4096"]
    NB, S, D = x_d.shape
    CTX = ctx_d.shape[1]
    HD = t_in["L0_attn_Wo"].shape[0]
    FF = t_in["L0_ffn_gate_qweight"].shape[1]
    GU = t_in["L0_ffn_gate_scales"].shape[0]
    GD = t_in["L0_ffn_down_scales"].shape[0]
    KC = D // P
    HC = HD // P
    GB = 4
    NG = NB // GB
    TG = GB * S
    NT = NB * S
    NI = -(-FF // P)
    FP = NI * P
    LASTC = FF - (NI - 1) * P
    TT = NT // P
    HALF = 512
    CP = [min(P, CTX - c * P) for c in range(-(-CTX // P))]
    CC = len(CP)
    XS = 1024.0
    assert NB % GB == 0 and TG <= 512 and D == 2 * HALF and NI % 2 == 0 and TT % 2 == 0 and KC == 8

    x1_d = nc.dram_tensor("x1_scratch", (NT, D), F32).ap()
    x2_d = nc.dram_tensor("x2_scratch", (NT, D), F32).ap()
    h_d = nc.dram_tensor("h_scratch", (TT, P, NI, 2, P), F16).ap()
    tab_d = nc.dram_tensor("table_scratch", (NI, P, 2, P), BF16).ap()

    with ExitStack() as ctx:
        def sem(name):
            return ctx.enter_context(nc.semaphore(name))

        def sb(name, shape, dt):
            return ctx.enter_context(nc.sbuf_tensor(name, shape, dt))

        ARENA = 203 * 1024
        arena = sb("arena", [P, ARENA // 4], F32)

        def carve(byte, shape, dt):
            size = {F32: 4, I32: 4, U32: 4, F16: 2, BF16: 2}[dt]
            n = int(np.prod(shape)) * size
            assert byte % 4 == 0 and n % 4 == 0 and byte + n <= ARENA, (byte, n)
            v = arena[:, byte // 4:(byte + n) // 4]
            if dt is not F32:
                v = v.bitcast(dt)
            if len(shape) == 2:
                v = v.rearrange("p (a b) -> p a b", b=shape[1])
            elif len(shape) == 3:
                v = v.rearrange("p (a b c) -> p a b c", b=shape[1], c=shape[2])
            elif len(shape) == 4:
                v = v.rearrange("p (a b c d) -> p a b c d", b=shape[1], c=shape[2], d=shape[3])
            return v

        at_x2t = 0
        at_tab = at_x2t + KC * NT * 4
        at_rest = at_tab + 4 * 2 * D + 2 * FP + 2 * 2 * D
        at_xs = at_rest
        at_xt = at_xs + GB * D * 4
        at_xr = at_xt + KC * TG * 4
        at_yo = at_xr + 2 * D * 4
        at_gt = at_yo + 2 * D * 4
        at_m = at_gt + KC * TG * 4
        at_ctx = at_m + KC * D * 4
        at_ctxt = at_ctx + 2 * CC * D * 4
        at_end = at_ctxt + KC * CTX * 4

        x2t = carve(at_x2t, [2, KC, NT], F16)
        wk = carve(at_x2t, [KC, D], F32)
        wq = [carve(at_x2t + KC * D * 4 + i * KC * P * 4, [KC, P], F32) for i in range(2)]
        sel_s = [carve(at_tab + m * 2 * D, [KC, P], BF16) for m in range(2)]
        sel_z = [carve(at_tab + (2 + m) * 2 * D, [KC, P], BF16) for m in range(2)]
        sel_d = carve(at_tab + 8 * D, [NI, P], BF16)
        tab_ds = carve(at_tab + 8 * D + 2 * FP, [D], BF16)
        tab_dz = carve(at_tab + 8 * D + 2 * FP + 2 * D, [D], BF16)

        xs = carve(at_xs, [GB, D], F32)
        xt = carve(at_xt, [KC, TG], F32)
        xr = carve(at_xr, [2, D], F32)
        yo = carve(at_yo, [2, D], F32)
        gt = carve(at_gt, [KC, TG], F32)
        qkt = carve(at_gt, [2 * HC, TG], F32)
        pr = carve(at_gt + 2 * HC * TG * 4, [GB, S], F32)
        pt = carve(at_gt + (2 * HC + 1) * TG * 4, [GB, S], F32)
        ot = carve(at_gt + (2 * HC + 2) * TG * 4, [HC, TG], F32)
        m_sb = carve(at_m, [KC, D], F32)
        wqkv = carve(at_m, [KC, 3 * HD], F32)
        wo = carve(at_m + KC * 3 * HD * 4, [HC, D], F32)
        cx = [carve(at_ctx + i * CC * D * 4, [CC, D], F32) for i in range(2)]
        v_sb = carve(at_ctx, [GB, HD], F32)
        bo_b = carve(at_ctx + GB * HD * 4, [D], F32)
        vb_b = carve(at_ctx + GB * HD * 4 + D * 4, [HD], F32)
        cxt = carve(at_ctxt, [KC, CTX], F32)
        at_tmp = at_ctx + CC * D * 4
        tmp = carve(at_tmp, [FP], F32)
        tmp_i = carve(at_tmp, [FP], I32)
        tab = carve(at_tmp + 4 * FP, [FP], BF16)
        qz = carve(at_tmp + 6 * FP, [FF // 8], U32)
        flat = [t_in[f"L0_ffn_{m}_scales"].shape[0] * t_in[f"L0_ffn_{m}_scales"].shape[1] // P
                for m in ("gate", "up", "down")]
        mid = carve(at_xt, [FP], BF16)
        s_flat = [carve(at_xt + 2 * FP + 4 * sum(flat[:m]), [flat[m]], F32) for m in range(3)]
        wd = carve(at_rest, [NI, 2, D], F16)
        at_b = at_rest + NI * 2 * D * 2
        wgu = [[carve(at_b + (s * 2 + m) * 4 * D, [2, KC, P], F16) for m in range(2)] for s in range(2)]
        at_b += 16 * D
        wbuf = [carve(at_b + i * 4 * D, [D], F32) for i in range(3)]
        at_b += 12 * D
        qw = [[carve(at_b + (s * 2 + m) * 4 * P, [P], U32) for m in range(2)] for s in range(2)]
        at_b += 16 * P
        tabc = [carve(at_b + s * 4 * P, [2, P], BF16) for s in range(2)]
        at_b += 8 * P
        h_st = carve(at_b, [2, NT], F16)
        at_b += NT * 4
        g_act = carve(at_b, [TG], F32)
        h_f = carve(at_b + TG * 4, [TG], F32)
        at_c = at_rest + NI * 2 * D * 2
        ht = [carve(at_c + i * NI * 4 * P, [NI, 2, P], F16) for i in range(2)]
        xf = [carve(at_x2t + i * D * 4, [D], F32) for i in range(2)]
        yf = [carve(at_x2t + (2 + i) * D * 4, [D], F32) for i in range(2)]

        ident = sb("ident", [P, P], F32)
        sp_ = sb("logits", [P, CTX + 1], F32)
        pt3 = carve(at_end, [CC, S], F32)
        small = sb("small", [P, 128], F32)
        small_i = small[:].bitcast(I32)
        c_ = {}
        used = [0]

        def col(name, n=1):
            c_[name] = small[:, used[0]:used[0] + n]
            used[0] += n
            return c_[name]

        bqk = col("bqk", 2 * HC)
        mx1, nm1, rs1, rc1 = col("mx1", GB), col("nm1", GB), col("rs1", GB), col("rc1", GB)
        st, mv, ve, rstd, mhalf = col("st", 12), col("mv", 2), col("ve"), col("rstd"), col("mhalf")
        bqc, bkc, u_c, v2, c0 = col("bqc", KC), col("bkc", KC), col("u", KC), col("v2", KC), col("c0")
        rr, nm3, rs3, rc3 = col("rr", GB), col("nm3"), col("rs3", GB), col("rc3", GB)
        amx, amr, pw, fac = col("amx", 3), col("amr", 3), col("pw", 4), col("fac", 3)
        inv_g, sc_u, inv_d, ghu = col("inv_g"), col("sc_u"), col("inv_d"), col("ghu")
        rowid, rowid_f, nib, four = col("rowid", 1), col("rowid_f"), col("nib", 3), col("masks", KC)
        assert used[0] <= 128

        psum = ctx.enter_context(nc.psum_tensor("psum", [P, 8 * 512], F32))
        bk = [psum[:, i * 512:(i + 1) * 512] for i in range(8)]

        s_const = sem("constants"); s_cc = sem("constant_step")
        s_w1 = sem("weights_stage1_in"); s_bias = sem("biases_in"); s_bo = sem("bo_in")
        s_xs = [sem(f"xs_in{b}") for b in range(GB)]
        s_xr = [sem(f"residual_in{i}") for i in range(2)]
        s_yout = [sem(f"rows_out{i}") for i in range(2)]
        s_xt = sem("xT_in_psum"); s_xte = sem("xT_copied")
        s_qk = sem("qk_in_psum"); s_qke = sem("qk_copied")
        s_s = sem("scores_in_psum"); s_v = sem("v_in_psum"); s_ve = sem("v_copied")
        s_mx = sem("max_ready"); s_nm = sem("neg_max_ready"); s_exp = sem("exp_done")
        s_rc = sem("recip_ready"); s_p = sem("probs_ready"); s_pt = sem("probsT_in_psum")
        s_pte = sem("probsT_copied"); s_o = sem("oT_in_psum"); s_oe = sem("oT_copied")
        s_w = sem("attn_in_psum"); s_xb = sem("residual_plus_bo"); s_y = sem("sum_ready")
        s_st = sem("stats_ready"); s_seen = sem("stats_seen"); s_ag = sem("mean_var_ready"); s_eps = sem("var_eps_ready")
        s_rstd = sem("rstd_ready"); s_n = sem("rows_normalised")
        s_wk = sem("wk_in"); s_wq = [sem(f"wq_in{i}") for i in range(2)]
        s_m = sem("m_in_psum"); s_me = sem("m_copied"); s_v2 = sem("v2_in_psum"); s_v2e = sem("v2_copied")
        s_tin = [sem(f"table_input{i}_in") for i in range(6)]; s_t = sem("table_step"); s_amx = sem("scale_max_all")
        s_tabo = sem("tables_out")
        s_cx = [sem(f"ctx_in{i}") for i in range(2)]
        s_ct = sem("ctxT_in_psum"); s_cte = sem("ctxT_copied")
        s_g = sem("g_in_psum"); s_ge = sem("g_copied"); s_r = sem("r_in_psum"); s_re = sem("r_copied")
        s_l = sem("logits_in_psum"); s_le = sem("logits_copied"); s_lm = sem("logit_max")
        s_ex3 = sem("exp3_done"); s_rc3 = sem("recip3_ready")
        s_pt3 = sem("p3T_in_psum"); s_pt3e = sem("p3T_copied"); s_at = sem("attended_in_psum")
        s_y3 = sem("sum3_ready"); s_x2t = sem("x2T_in_psum"); s_hi = sem("x2T_hi_ready"); s_lo = sem("x2T_lo_ready")
        s_qw = [sem(f"qw_in{i}") for i in range(2)]; s_tc = [sem(f"tabc_in{i}") for i in range(2)]
        s_qd = sem("qw_down_in")
        s_ga = sem("gather_in_psum"); s_wf = sem("weights_f32_ready"); s_dq = sem("dequant_step")
        s_wh = sem("weights_hi_ready"); s_wl = sem("weights_lo_ready")
        s_gp = sem("gate_in_psum"); s_up = sem("up_in_psum")
        s_si = sem("silu_ready"); s_hf = sem("h_f32_ready"); s_hh = sem("h_hi_ready"); s_hl = sem("h_lo_ready")
        s_ho = [sem(f"h_out{i}") for i in range(2)]
        s_ht = [sem(f"hT_in{i}") for i in range(2)]; s_xf = [sem(f"x2_in{i}") for i in range(2)]
        s_d = sem("down_in_psum"); s_y5 = sem("sum5_ready"); s_n5 = sem("rows5_normalised")
        s_fin = [sem(f"final_out{i}") for i in range(2)]

        block = ctx.enter_context(nc.Block())

        def rows(ap, n):
            return ap[bass.ds(n * S, S), :]

        x_rows = x_d.rearrange("b s d -> (b s) d")
        NLN = 2 * NB
        NGATHER = 3 * NI

        def down_no(i):
            return 3 * i + 4

        def wd_parts(i):
            if isinstance(i, int):
                return [wd[:, i, l, :] for l in range(2)]
            return [wd[:, bass.ds(i, 1), l, :].rearrange("p o c -> p (o c)") for l in range(2)]

        T = {}

        @block.vector
        def _(dve):
            for i in range(2):
                dve.sem_inc(s_yout[i], 16)
                dve.sem_inc(s_ho[i], 32)
                dve.sem_inc(s_fin[i], 16)
            dve.sem_inc(s_hf, 2)
            dve.sem_inc(s_hl, 1)
            dve.sem_inc(s_hh, 1)
            dve.sem_inc(s_lo, 1)
            dve.sem_inc(s_y5, 4)

            def layer_norm(y, k, summed, first, done):
                n = y.shape[0]
                for h in range(2):
                    dve.wait_ge(summed, first + h)
                    dve.bn_stats(st[0:n, 6 * h:6 * h + 6], y[:, h * HALF:(h + 1) * HALF]).then_inc(s_st, 1)
                dve.wait_ge(s_st, 2 * k + 2)
                dve.sem_inc(s_seen, 1)
                dve.bn_aggr(mv[0:n, :], st[0:n, :]).then_inc(s_ag, 1)
                dve.wait_ge(s_ag, k + 1)
                dve.tensor_scalar(ve[0:n, :], mv[0:n, 1:2], EPS, None, ALU.add).then_inc(s_eps, 1)
                dve.wait_ge(s_rstd, k + 1)
                dve.tensor_scalar(y, y, mv[0:n, 0:1], rstd[0:n, :], ALU.subtract, ALU.mult).then_inc(done, 1)

            with dve.Fori(0, NG) as g:
                dve.wait_ge(s_s, g + 1)
                dve.tensor_reduce(mx1[0:S, :], bk[2][0:S, 0:TG].rearrange("p (b k) -> p b k", b=GB), AX.X,
                                  ALU.max, negate=True).then_inc(s_mx, 1)
                dve.wait_ge(s_mx, g + 1)
                dve.tensor_scalar(nm1[0:S, :], mx1[0:S, :], HD ** -0.5, None, ALU.mult).then_inc(s_nm, 1)
                dve.wait_ge(s_bias, 32)
                for p in range(2):
                    dve.wait_ge(s_v, 2 * g + p + 1)
                    dve.tensor_tensor(v_sb[0:S, 2 * p:2 * p + 2, :],
                                      bk[4 + p][0:S, :].rearrange("p (b d) -> p b d", b=2),
                                      vb_b[0:S, :].unsqueeze(1).to_broadcast([S, 2, HD]), ALU.add).then_inc(s_ve, 1)
                dve.wait_ge(s_exp, GB * g + GB)
                dve.reciprocal(rc1[0:S, :], rs1[0:S, :]).then_inc(s_rc, 1)
                dve.wait_ge(s_rc, g + 1)
                dve.tensor_tensor(pr[0:S, :, :], pr[0:S, :, :], rc1[0:S, :].unsqueeze(2).to_broadcast([S, GB, S]),
                                  ALU.mult).then_inc(s_p, 1)
                dve.wait_ge(s_pt, g + 1)
                dve.tensor_copy(pt[0:S, :, :], bk[0][0:S, 0:TG].rearrange("p (b k) -> p b k", b=GB)).then_inc(s_pte, 1)
                for b in range(GB):
                    n = g * GB + b
                    dve.wait_ge(s_xb, n + 1)
                    dve.wait_ge(s_yout[b % 2], 16 * (2 * g + b // 2 + 1))
                    for h in range(2):
                        cols = slice(h * HALF, (h + 1) * HALF)
                        dve.wait_ge(s_w, 2 * n + h + 1)
                        dve.tensor_tensor(yo[0:S, b % 2, cols], bk[6 + h][0:S, :], xr[0:S, b % 2, cols],
                                          ALU.add).then_inc(s_y, 1)
                    layer_norm(yo[0:S, b % 2, :], n, s_y, 2 * n + 1, s_n)

            steps = [0]

            def step(ins):
                ins.then_inc(s_t, 1)
                steps[0] += 1
                dve.wait_ge(s_t, steps[0])

            dve.wait_ge(s_tin[0], 48)
            for m in range(3):
                step(dve.tensor_reduce(amx[:, m:m + 1], s_flat[m], AX.X, ALU.max, apply_absolute_value=True))
            T["amx"] = steps[0]
            dve.wait_ge(s_amx, 1)
            step(dve.tensor_scalar(amr, amr, 1e-15, None, ALU.max))
            step(dve.tensor_tensor(ghu, amr[:, 0:1], amr[:, 1:2], ALU.mult))
            step(dve.tensor_scalar(pw[:, 0:3].bitcast(I32), amr.bitcast(I32), 0x7F800000, None, ALU.bitwise_and))
            step(dve.tensor_scalar(pw[:, 3:4].bitcast(I32), ghu.bitcast(I32), 0x7F800000, None, ALU.bitwise_and))
            step(dve.reciprocal(fac, pw[:, 0:3]))
            step(dve.tensor_scalar(fac, fac, 1024.0, None, ALU.mult))
            step(dve.tensor_scalar(inv_g, pw[:, 0:1], 2.0 ** -10 / XS, None, ALU.mult))
            step(dve.reciprocal(sc_u, pw[:, 3:4]))
            step(dve.tensor_tensor(sc_u, sc_u, pw[:, 1:2], ALU.mult))
            step(dve.tensor_scalar(sc_u, sc_u, 2.0 ** -24 / XS, None, ALU.mult))
            step(dve.tensor_tensor(inv_d, pw[:, 3:4], pw[:, 2:3], ALU.mult))
            step(dve.tensor_scalar(inv_d, inv_d, 2.0 ** 4, None, ALU.mult))
            dve.wait_ge(s_const, 4)
            step(dve.tensor_scalar(nib[:, 0:1].bitcast(I32), rowid.bitcast(I32), 31, None, ALU.bitwise_and))
            step(dve.tensor_copy(rowid_f, nib[:, 0:1].bitcast(I32)))
            step(dve.memset(nib[:, 1:2].bitcast(U32), 15))
            step(dve.tensor_scalar(nib[:, 0:1].bitcast(I32), rowid.bitcast(I32), 7, 2, ALU.bitwise_and,
                                   ALU.arith_shift_left))
            step(dve.tensor_tensor(nib[:, 2:3].bitcast(U32), nib[:, 1:2].bitcast(U32), nib[:, 0:1].bitcast(U32),
                                   ALU.logical_shift_left))
            for j in range(8):
                step(dve.memset(four[:, j:j + 1].bitcast(U32), 15 << (4 * j)))

            def selection(idx, groups, width, put):
                step(dve.tensor_scalar(neg[:, 0:width], idx, 0, groups, ALU.is_lt, ALU.mult))
                step(dve.tensor_tensor(tmp[:, 0:width], idx, neg[:, 0:width], ALU.add))
                step(dve.tensor_scalar(tmp[:, 0:width], tmp[:, 0:width], 0, groups - 1, ALU.max, ALU.min))
                for j in range(8):
                    put(slice(0, 96), j, 2.0 ** (-4 * j), tmp[0:96, j:width:8])
                    put(slice(96, 128), j, 2.0 ** (4 * j), tmp[96:128, j:width:8])

            neg = carve(at_xs, [FP], F32)
            for m in range(2):
                step(dve.memset(sel_s[m].rearrange("p a b -> p (a b)").bitcast(U32), 0))
                step(dve.memset(sel_z[m].rearrange("p a b -> p (a b)").bitcast(U32), 0))
            step(dve.memset(sel_d.rearrange("p a b -> p (a b)").bitcast(U32), 0))
            step(dve.memset(tab_ds.bitcast(U32), 0))
            step(dve.memset(tab_dz.bitcast(U32), 0))
            for m, groups in enumerate((GU, GU, GD)):
                width = D if m < 2 else FF

                def put(r, j, factor, in0):
                    if m == 2:
                        dst = sel_d.rearrange("p a b -> p (a b)")[r, j:width:8]
                    else:
                        dst = (sel_s if r.start == 0 else sel_z)[m][r, j, :]
                    step(dve.tensor_scalar(dst, in0, rowid_f[r, :], factor, ALU.is_equal, ALU.mult))

                dve.wait_ge(s_tin[1], 16 * (m + 1))
                selection(tmp_i[:, 0:width], groups, width, put)
                T[f"idx{m}"] = steps[0]

            for m, groups in enumerate((GU, GU, GD)):
                width = FF if m < 2 else D
                s_to = tab if m < 2 else tab_ds
                z_to = tab if m < 2 else tab_dz
                if m == 0:
                    step(dve.memset(tab.bitcast(U32), 0))
                dve.wait_ge(s_tin[2], 16 * (m + 1))
                if m == 1:
                    dve.wait_ge(s_tabo, 16)
                s = tmp[0:groups, 0:width]
                step(dve.tensor_scalar(s, s, fac[0:groups, m:m + 1], None, ALU.mult))
                step(dve.tensor_copy(s_to[0:groups, 0:width], s))
                step(dve.tensor_tensor(s, s, s_to[0:groups, 0:width], ALU.subtract))
                step(dve.tensor_copy(mid[0:groups, 0:width], s))
                step(dve.tensor_copy(s_to[32:32 + groups, 0:width], s))
                step(dve.tensor_tensor(s, s, mid[0:groups, 0:width], ALU.subtract))
                step(dve.tensor_copy(s_to[64:64 + groups, 0:width], s))
                dve.wait_ge(s_tin[3], 16 * (m + 1))
                z = tmp_i[96:96 + groups, 0:width]
                for j in range(8):
                    step(dve.tensor_scalar(z[:, j:width:8].bitcast(U32), qz[96:96 + groups, 0:width // 8], 4 * j, 15,
                                           ALU.logical_shift_right, ALU.bitwise_and))
                step(dve.tensor_scalar(z_to[96:96 + groups, 0:width], z, 1, None, ALU.add))
                T[f"tab{m}"] = steps[0]

            def softmax_in(g, b):
                n = g * GB + b
                dve.wait_ge(s_l, n + 1)
                dve.tensor_scalar(sp_[0:S, 0:CTX], bk[5][0:S, 0:CTX], rr[0:S, b:b + 1], D ** -0.5,
                                  ALU.add, ALU.mult).then_inc(s_le, 1)
                dve.wait_ge(s_le, n + 1)
                dve.tensor_reduce(nm3[0:S, :], sp_[0:S, 0:CTX], AX.X, ALU.max, negate=True).then_inc(s_lm, 1)

            def probs_t(g, b):
                dve.wait_ge(s_pt3, g * GB + b + 1)
                for c in range(CC):
                    ins = dve.tensor_copy(pt3[0:CP[c], c, :], bk[4][0:CP[c], c * P:c * P + S])
                ins.then_inc(s_pt3e, 1)

            def attended(g, b):
                n = g * GB + b
                dve.wait_ge(s_ex3, n + 1)
                dve.reciprocal(rc3[0:S, b:b + 1], rs3[0:S, b:b + 1]).then_inc(s_rc3, 1)
                dve.wait_ge(s_xr[b % 2], 16 * (NB // 2 + 2 * g + b // 2 + 1))
                dve.wait_ge(s_yout[b % 2], 16 * (NB // 2 + 2 * g + b // 2 + 1))
                dve.wait_ge(s_rc3, n + 1)
                for h in range(2):
                    cols = slice(h * HALF, (h + 1) * HALF)
                    dve.wait_ge(s_at, 2 * n + h + 1)
                    dve.scalar_tensor_tensor(yo[0:S, b % 2, cols], bk[6 + h][0:S, :], rc3[0:S, b:b + 1],
                                             xr[0:S, b % 2, cols], ALU.mult, ALU.add).then_inc(s_y3, 1)

            def norm3(g, b):
                n = g * GB + b
                layer_norm(yo[0:S, b % 2, :], NB + n, s_y3, 2 * n + 1, s_n)

            def x2t_lo(g, b):
                n = g * GB + b
                for j in range(2):
                    dve.wait_ge(s_hi, 2 * n + j + 1)
                    dve.scalar_tensor_tensor(x2t[:, 1, 4 * j:4 * j + 4, bass.ds(n * S, S)],
                                             bk[2 + j][:, 0:TG].rearrange("p (a t) -> p a t", a=4), XS,
                                             x2t[:, 0, 4 * j:4 * j + 4, bass.ds(n * S, S)],
                                             ALU.mult, ALU.subtract).then_inc(s_lo, 1)

            dve.wait_ge(s_v2e, 1)
            with dve.Fori(0, NG) as g:
                dve.wait_ge(s_r, g + 1)
                dve.tensor_scalar(rr[0:S, :], bk[4][0:S, 0:GB], c0[0:S, :], None, ALU.add).then_inc(s_re, 1)
                dve.wait_ge(s_re, g + 1)
                softmax_in(g, 0)
                probs_t(g, 0)
                softmax_in(g, 1)
                attended(g, 0)
                norm3(g, 0)
                probs_t(g, 1)
                softmax_in(g, 2)
                attended(g, 1)
                norm3(g, 1)
                x2t_lo(g, 0)
                probs_t(g, 2)
                softmax_in(g, 3)
                attended(g, 2)
                probs_t(g, 3)
                norm3(g, 2)
                x2t_lo(g, 1)
                attended(g, 3)
                norm3(g, 3)
                x2t_lo(g, 2)
                x2t_lo(g, 3)

            def dequant(q, kind, s, e):
                w = wbuf[kind]
                if kind < 2:
                    dve.wait_ge(s_qw[s], 32 * (e + 1))
                    if not isinstance(q, int) or q >= 2:
                        dve.wait_ge(s_wh, q - 1)
                        dve.wait_ge(s_wl, q - 1)
                    dve.tensor_tensor(w.bitcast(U32).rearrange("p (j n) -> p j n", j=8),
                                      qw[s][kind].unsqueeze(1).to_broadcast([P, 8, P]),
                                      four.bitcast(U32).unsqueeze(2).to_broadcast([P, 8, P]),
                                      ALU.bitwise_and).then_inc(s_dq, 1)
                else:
                    dve.wait_ge(s_qd, 16 * (e + 1))
                    dve.tensor_scalar(w.bitcast(U32), w.bitcast(U32), nib[:, 2:3].bitcast(U32), None,
                                      ALU.bitwise_and).then_inc(s_dq, 1)
                dve.wait_ge(s_ga, q + 1)
                dve.wait_ge(s_dq, 2 * q + 1)
                dve.tensor_tensor(w, w.bitcast(U32), psum[:, 3072:4096], ALU.subtract).then_inc(s_dq, 1)
                dve.wait_ge(s_dq, 2 * q + 2)
                dve.tensor_tensor(w, w, psum[:, 2048:3072], ALU.mult).then_inc(s_wf, 1)

            def hidden(i, t):
                dve.wait_ge(s_si, 4 * i + t + 1)
                dve.wait_ge(s_up, 4 * i + t + 1)
                dve.wait_ge(s_hh, 4 * i + t + 1)
                dve.wait_ge(s_hl, 4 * i + t + 1)
                dve.scalar_tensor_tensor(h_f, bk[2 + t % 2][:, 0:TG], sc_u, g_act, ALU.mult, ALU.mult).then_inc(s_hf, 1)
                if t % 2 == 0:
                    dve.wait_ge(s_ho[t // 2], 32 * (i + 1))
                dve.wait_ge(s_hh, 4 * i + t + 2)
                cols = slice(t * TG, (t + 1) * TG)
                dve.tensor_tensor(h_st[:, 1, cols], h_f, h_st[:, 0, cols], ALU.subtract).then_inc(s_hl, 1)

            def chunk(i, s, e, more):
                hidden(i, 0)
                if more:
                    dequant(3 * i + 2, 0, 1 - s, e + s)
                hidden(i, 1)
                if more:
                    dequant(3 * i + 3, 1, 1 - s, e + s)
                hidden(i, 2)
                dequant(down_no(i) if more else NGATHER - 1, 2, s, i)
                hidden(i, 3)

            for m in range(2):
                dequant(m, m, 0, 0)
            with dve.Fori(0, NI // 2 - 1) as e:
                for s in range(2):
                    chunk(2 * e + s, s, e, True)
            chunk(NI - 2, 0, NI // 2 - 1, True)
            chunk(NI - 1, 1, NI // 2 - 1, False)

            with dve.Fori(0, TT // 2) as e:
                for s in range(2):
                    tile = 2 * e + s
                    dve.wait_ge(s_xf[s], 16 * (e + 1))
                    dve.wait_ge(s_fin[s], 16 * (e + 1))
                    for c in range(2):
                        cols = slice(c * HALF, (c + 1) * HALF)
                        dve.wait_ge(s_d, 2 * tile + c + 1)
                        dve.scalar_tensor_tensor(yf[s][:, cols], bk[2 * s + c], inv_d, xf[s][:, cols],
                                                 ALU.mult, ALU.add).then_inc(s_y5, 1)
                    layer_norm(yf[s], NLN + tile, s_y5, 2 * tile + 1 + 4, s_n5)

        @block.gpsimd
        def _(pool):
            pool.memset(ident[:], 1.0).then_inc(s_cc, 1)
            pool.memset(mhalf, -0.5).then_inc(s_const, 1)
            pool.iota(rowid.bitcast(I32), pattern=[[0, 1]], base=0, channel_multiplier=1).then_inc(s_const, 1)
            pool.memset(sp_[:], 0.0).then_inc(s_const, 1)
            pool.wait_ge(s_cc, 1)
            pool.affine_select(out=ident[:], in_=ident[:], compare_op=ALU.is_equal, fill=0.0, base=0,
                               pattern=[[-1, P]], channel_multiplier=1).then_inc(s_const, 1)
            pool.wait_ge(s_const, 4)
            pool.wait_ge(s_bo, 16)

            def inverse_std(k, n):
                pool.wait_ge(s_eps, k + 1)
                pool.tensor_tensor(rstd[0:n, :], ve[0:n, :], mhalf[0:n, :], ALU.pow).then_inc(s_rstd, 1)

            def add_bo(g, b):
                pool.wait_ge(s_xr[b % 2], 16 * (2 * g + b // 2 + 1))
                pool.tensor_tensor(xr[0:S, b % 2, :], xr[0:S, b % 2, :], bo_b[0:S, :], ALU.add).then_inc(s_xb, 1)

            def self_attention(g, more):
                for b in range(GB):
                    if b + 1 < GB:
                        add_bo(g, b + 1)
                    elif more:
                        add_bo(g + 1, 0)
                    inverse_std(g * GB + b, S)

            add_bo(0, 0)
            with pool.Fori(0, NG - 1) as g:
                self_attention(g, True)
            self_attention(NG - 1, False)
            pool.wait_ge(s_t, T["amx"])
            pool.partition_all_reduce(amr, amx, P, RMAX).then_inc(s_amx, 1)
            with pool.Fori(NB, NLN) as k:
                inverse_std(k, S)

            def low_part(q, dst, kind):
                pool.wait_ge(s_wh, q + 1)
                src = wbuf[kind]
                if kind < 2:
                    src = src.rearrange("p (j n) -> p j n", j=8)
                pool.tensor_tensor(dst[1], src, dst[0], ALU.subtract).then_inc(s_wl, 1)

            for m in range(2):
                low_part(m, [wgu[0][m][:, l, :, :] for l in range(2)], m)

            def chunk(i, s, more):
                if more:
                    for m in range(2):
                        low_part(3 * i + 2 + m, [wgu[1 - s][m][:, l, :, :] for l in range(2)], m)
                low_part(down_no(i) if more else NGATHER - 1, wd_parts(i), 2)

            with pool.Fori(0, NI // 2 - 1) as e:
                for s in range(2):
                    chunk(2 * e + s, s, True)
            chunk(NI - 2, 0, True)
            chunk(NI - 1, 1, False)
            with pool.Fori(NLN, NLN + TT) as k:
                inverse_std(k, P)

        @block.scalar
        def _(act):
            act.sem_inc(s_me, 2)

            def transposed_rows(gg):
                for c in range(KC):
                    act.wait_ge(s_xt, KC * gg + c + 1)
                    act.activation(xt[:, c, :], bk[c % 2][:, 0:TG], ACT.Identity).then_inc(s_xte, 1)

            act.wait_ge(s_bias, 32)
            with act.Fori(0, NG) as g:
                transposed_rows(g)
                for f in range(2 * HC):
                    act.wait_ge(s_qk, 2 * HC * g + f + 1)
                    act.activation(qkt[:, f, :], bk[2 + f % 2][:, 0:TG], ACT.Identity,
                                   bias=bqk[:, f:f + 1]).then_inc(s_qke, 1)
                act.wait_ge(s_nm, g + 1)
                for b in range(GB):
                    act.activation(pr[0:S, b, :], bk[2][0:S, b * S:(b + 1) * S], ACT.Exp, scale=HD ** -0.5,
                                   bias=nm1[0:S, b:b + 1], accum_out=rs1[0:S, b:b + 1]).then_inc(s_exp, 1)
                for c in range(HC):
                    act.wait_ge(s_o, HC * g + c + 1)
                    act.activation(ot[:, c, :], bk[3 - c][:, 0:TG], ACT.Identity).then_inc(s_oe, 1)

            with act.Fori(0, KC // 2) as e:
                for i in range(2):
                    act.wait_ge(s_m, 2 * e + i + 1)
                    act.activation(m_sb[:, bass.ds(2 * e + i, 1), :].rearrange("p a b -> p (a b)"),
                                   psum[:, i * 1024:(i + 1) * 1024], ACT.Identity)
                    act.activation(u_c[:, bass.ds(2 * e + i, 1)], bk[4 + i][:, 0:1], ACT.Identity).then_inc(s_me, 1)
            act.wait_ge(s_v2, 1)
            act.activation(v2, bk[6][:, 0:KC], ACT.Identity)
            act.activation(c0[0:S, :], bk[6][0:S, KC:KC + 1], ACT.Identity).then_inc(s_v2e, 1)

            act.wait_ge(s_v2e, 1)
            act.wait_ge(s_t, T["tab2"])
            act.wait_ge(s_tabo, 32)

            def context_t(g, b, part):
                n = g * GB + b
                for c in range(4 * part, 4 * part + 4):
                    act.wait_ge(s_ct, KC * n + c + 1)
                    if c == 0 and b > 0:
                        act.wait_ge(s_l, n)
                    act.activation(cxt[:, c, :], bk[c % 2][:, 0:CTX], ACT.Identity).then_inc(s_cte, 1)

            def exponentials(g, b):
                act.wait_ge(s_lm, g * GB + b + 1)
                act.activation(sp_[0:S, 0:CTX], sp_[0:S, 0:CTX], ACT.Exp, bias=nm3[0:S, :],
                               accum_out=rs3[0:S, b:b + 1]).then_inc(s_ex3, 1)

            def x2t_hi(g, b):
                n = g * GB + b
                for j in range(2):
                    act.wait_ge(s_x2t, 2 * n + j + 1)
                    act.activation(x2t[:, 0, 4 * j:4 * j + 4, bass.ds(n * S, S)],
                                   bk[2 + j][:, 0:TG].rearrange("p (a t) -> p a t", a=4),
                                   ACT.Identity, scale=XS).then_inc(s_hi, 1)

            with act.Fori(0, NG) as g:
                transposed_rows(NG + g)
                for c in range(KC):
                    act.wait_ge(s_g, KC * g + c + 1)
                    act.activation(gt[:, c, :], bk[2 + c % 2][:, 0:TG], ACT.Identity,
                                   bias=v2[:, c:c + 1]).then_inc(s_ge, 1)
                context_t(g, 0, 0)
                context_t(g, 0, 1)
                for b in range(1, GB):
                    context_t(g, b, 0)
                    exponentials(g, b - 1)
                    context_t(g, b, 1)
                    if b == 3:
                        x2t_hi(g, 0)
                exponentials(g, GB - 1)
                for b in range(1, GB):
                    x2t_hi(g, b)

            def high_part(q, dst, kind):
                act.wait_ge(s_wf, q + 1)
                src = wbuf[kind]
                if kind < 2:
                    src = src.rearrange("p (j n) -> p j n", j=8)
                act.activation(dst, src, ACT.Identity).then_inc(s_wh, 1)

            def hidden(i, t):
                act.wait_ge(s_gp, 4 * i + t + 1)
                act.wait_ge(s_hf, 4 * i + t + 2)
                act.activation(g_act, bk[t % 2][:, 0:TG], ACT.Silu, scale=inv_g).then_inc(s_si, 1)
                if t % 2 == 0:
                    act.wait_ge(s_ho[t // 2], 32 * (i + 1))
                act.wait_ge(s_hf, 4 * i + t + 3)
                act.activation(h_st[:, 0, t * TG:(t + 1) * TG], h_f, ACT.Identity).then_inc(s_hh, 1)

            def chunk(i, s, more):
                hidden(i, 0)
                if more:
                    high_part(3 * i + 2, wgu[1 - s][0][:, 0, :, :], 0)
                hidden(i, 1)
                if more:
                    high_part(3 * i + 3, wgu[1 - s][1][:, 0, :, :], 1)
                hidden(i, 2)
                high_part(down_no(i) if more else NGATHER - 1, wd_parts(i)[0], 2)
                hidden(i, 3)

            for m in range(2):
                high_part(m, wgu[0][m][:, 0, :, :], m)
            with act.Fori(0, NI // 2 - 1) as e:
                for s in range(2):
                    chunk(2 * e + s, s, True)
            chunk(NI - 2, 0, True)
            chunk(NI - 1, 1, False)

        @block.tensor
        def _(pe):
            def transposed_rows(gg):
                for b in range(GB):
                    pe.wait_ge(s_xs[b], 16 * (gg + 1))
                for c in range(KC):
                    if c >= 2:
                        pe.wait_ge(s_xte, KC * gg + c - 1)
                    for b in range(GB):
                        mm = pe.transpose(bk[c % 2][:, b * S:(b + 1) * S], xs_chunk(b, c, gg), ident[0:S, 0:S])
                    mm.then_inc(s_xt, 1)

            stage = [1]

            def xs_chunk(b, c, gg):
                return xs[0:S, b, c::KC] if stage[0] == 1 else xs[0:S, b, c * P:(c + 1) * P]

            def product(out, pairs, last=None):
                for k, (a, r) in enumerate(pairs):
                    mm = pe.matmul(out, a, r, start=(k == 0), stop=(k == len(pairs) - 1))
                return mm

            pe.wait_ge(s_const, 4)
            with pe.Fori(0, NG) as g:
                transposed_rows(g)
                pe.wait_ge(s_w1, 32)
                for f in range(2 * HC):
                    if f == 0:
                        pe.wait_ge(s_xte, KC * (g + 1))
                    if f >= 2:
                        pe.wait_ge(s_qke, 2 * HC * g + f - 1)
                    product(bk[2 + f % 2][:, 0:TG], [(wqkv[:, c, f * P:(f + 1) * P], xt[:, c, :])
                                                     for c in range(KC)]).then_inc(s_qk, 1)
                pe.wait_ge(s_qke, 2 * HC * (g + 1))
                for b in range(GB):
                    t = slice(b * S, (b + 1) * S)
                    mm = product(bk[2][0:S, t], [(qkt[:, c, t], qkt[:, HC + c, t]) for c in range(HC)])
                mm.then_inc(s_s, 1)
                for b in range(GB):
                    t = slice(b * S, (b + 1) * S)
                    mm = product(bk[4 + b // 2][0:S, (b % 2) * HD:(b % 2 + 1) * HD],
                                 [(xt[:, c, t], wqkv[:, c, 2 * HD:3 * HD]) for c in range(KC)])
                    if b % 2:
                        mm.then_inc(s_v, 1)
                pe.wait_ge(s_p, g + 1)
                for b in range(GB):
                    mm = pe.transpose(bk[0][0:S, b * S:(b + 1) * S], pr[0:S, b, :], ident[0:S, 0:S])
                mm.then_inc(s_pt, 1)
                pe.wait_ge(s_pte, g + 1)
                pe.wait_ge(s_ve, 2 * (g + 1))
                for c in range(HC):
                    for b in range(GB):
                        mm = product(bk[3 - c][:, b * S:(b + 1) * S],
                                     [(v_sb[0:S, b, c * P:(c + 1) * P], pt[0:S, b, :])])
                    mm.then_inc(s_o, 1)
                pe.wait_ge(s_oe, HC * (g + 1))
                for b in range(GB):
                    for h in range(2):
                        if b > 0:
                            pe.wait_ge(s_y, 2 * (g * GB + b - 1) + h + 1)
                        product(bk[6 + h][0:S, :], [(ot[:, c, b * S:(b + 1) * S], wo[:, c, h * HALF:(h + 1) * HALF])
                                                    for c in range(HC)]).then_inc(s_w, 1)

            pe.wait_ge(s_wk, 48)
            with pe.Fori(0, KC // 2) as e:
                for i in range(2):
                    pe.wait_ge(s_wq[i], 16 * (e + 1))
                    pe.wait_ge(s_me, 2 * e + i + 1)
                    for h in range(2):
                        product(bk[2 * i + h], [(wq[i][:, c, :], wk[:, c, h * HALF:(h + 1) * HALF])
                                                for c in range(KC)])
                    product(bk[4 + i][:, 0:1], [(wq[i][:, c, :], bkc[:, c:c + 1]) for c in range(KC)]).then_inc(s_m, 1)
            pe.wait_ge(s_y, 2 * NB)
            for y in range(KC):
                product(bk[6][:, y:y + 1], [(wk[:, c, y * P:(y + 1) * P], bqc[:, c:c + 1]) for c in range(KC)])
            product(bk[6][0:S, KC:KC + 1], [(bqc[:, c:c + 1].to_broadcast([P, S]), bkc[:, c:c + 1])
                                            for c in range(KC)]).then_inc(s_v2, 1)

            stage[0] = 3
            pe.wait_ge(s_v2e, 1)
            pe.wait_ge(s_me, KC + 2)
            pe.wait_ge(s_t, T["tab2"])
            pe.wait_ge(s_tabo, 32)

            def context_t(g, b):
                n = g * GB + b
                pe.wait_ge(s_cx[b % 2], 16 * (CC + 1) * (2 * g + b // 2 + 1))
                for c in range(KC):
                    if c >= 2:
                        pe.wait_ge(s_cte, KC * n + c - 1)
                    for r in range(CC):
                        mm = pe.transpose(bk[c % 2][:, r * P:r * P + CP[r]],
                                          cx[b % 2][0:CP[r], r, c * P:(c + 1) * P], ident[0:CP[r], 0:CP[r]])
                    mm.then_inc(s_ct, 1)

            def logits(g, b):
                n = g * GB + b
                pe.wait_ge(s_cte, KC * (n + 1))
                if b > 0:
                    pe.wait_ge(s_le, n)
                product(bk[5][0:S, 0:CTX], [(gt[:, c, b * S:(b + 1) * S], cxt[:, c, :])
                                            for c in range(KC)]).then_inc(s_l, 1)

            def probs_t(g, b):
                n = g * GB + b
                pe.wait_ge(s_ex3, n + 1)
                for r in range(CC):
                    mm = pe.transpose(bk[4][0:CP[r], r * P:r * P + S], sp_[0:S, r * P:r * P + CP[r]],
                                      ident[0:S, 0:S])
                mm.then_inc(s_pt3, 1)

            def attended(g, b):
                n = g * GB + b
                pe.wait_ge(s_pt3e, n + 1)
                for h in range(2):
                    if b > 0:
                        pe.wait_ge(s_y3, 2 * (n - 1) + h + 1)
                    product(bk[6 + h][0:S, :], [(pt3[0:CP[r], r, :], cx[b % 2][0:CP[r], r, h * HALF:(h + 1) * HALF])
                                                for r in range(CC)]).then_inc(s_at, 1)

            def x2_transposed(g, b):
                n = g * GB + b
                pe.wait_ge(s_n, NB + n + 1)
                if b > 0:
                    pe.wait_ge(s_lo, 2 * n + 1)
                for j in range(2):
                    for a in range(4):
                        mm = pe.transpose(bk[2 + j][:, a * S:(a + 1) * S], yo[0:S, b % 2, 4 * j + a::KC],
                                          ident[0:S, 0:S])
                    mm.then_inc(s_x2t, 1)

            with pe.Fori(0, NG) as g:
                transposed_rows(NG + g)
                pe.wait_ge(s_xte, KC * (NG + g + 1))
                pe.wait_ge(s_lo, 2 * GB * g + 1)
                for y in range(KC):
                    if y >= 2:
                        pe.wait_ge(s_ge, KC * g + y - 1)
                    product(bk[2 + y % 2][:, 0:TG], [(m_sb[:, c, y * P:(y + 1) * P], xt[:, c, :])
                                                     for c in range(KC)]).then_inc(s_g, 1)
                for b in range(GB):
                    mm = product(bk[4][0:S, b:b + 1], [(xt[:, c, b * S:(b + 1) * S], u_c[:, c:c + 1])
                                                       for c in range(KC)])
                mm.then_inc(s_r, 1)
                context_t(g, 0)
                pe.wait_ge(s_ge, KC * (g + 1))
                logits(g, 0)
                context_t(g, 1)
                pe.wait_ge(s_re, g + 1)
                probs_t(g, 0)
                logits(g, 1)
                attended(g, 0)
                context_t(g, 2)
                probs_t(g, 1)
                logits(g, 2)
                attended(g, 1)
                x2_transposed(g, 0)
                context_t(g, 3)
                probs_t(g, 2)
                logits(g, 3)
                attended(g, 2)
                probs_t(g, 3)
                x2_transposed(g, 1)
                attended(g, 3)
                x2_transposed(g, 2)
                x2_transposed(g, 3)

            def gather(q, parts):
                if not isinstance(q, int) or q > 0:
                    pe.wait_ge(s_wf, q)
                for base, pieces in ((2048, parts[0]), (3072, parts[1])):
                    for k, (a, r) in enumerate(pieces):
                        w = 1024 // len(pieces)
                        mm = pe.matmul(psum[:, base + k * w:base + (k + 1) * w], a, r, start=True, stop=True)
                mm.then_inc(s_ga, 1)

            def gather_gu(q, m, s, e):
                pe.wait_ge(s_tc[s], 16 * (e + 1))
                gather(q, [[(sel[m][:, j, :], tabc[s][:, m, :]) for j in range(8)] for sel in (sel_s, sel_z)])

            def gather_down(q, i):
                one = sel_d[:, i, :] if isinstance(i, int) else \
                    sel_d[:, bass.ds(i, 1), :].rearrange("p a b -> p (a b)")
                gather(q, [[(one, t[:, h * HALF:(h + 1) * HALF]) for h in range(2)] for t in (tab_ds, tab_dz)])

            def chunk(i, s, e, more):
                pe.wait_ge(s_wl, 3 * i + 1)
                for t in range(4):
                    cols = slice(t * TG, (t + 1) * TG)
                    pe.wait_ge(s_hf, 4 * i + t + 1)
                    for m, done in ((0, s_gp), (1, s_up)):
                        product(bk[2 * m + t % 2][:, 0:TG],
                                [(wgu[s][m][:, w, c, :], x2t[:, a, c, cols])
                                 for c in range(KC) for w, a in PASSES]).then_inc(done, 1)
                    if t == 0 and more:
                        gather_gu(3 * i + 2, 0, 1 - s, e + s)
                    if t == 1 and more:
                        gather_gu(3 * i + 3, 1, 1 - s, e + s)
                    if t == 2:
                        gather_down(down_no(i) if more else NGATHER - 1, i)

            pe.wait_ge(s_y3, 2 * NB)
            pe.wait_ge(s_lo, 2 * NB + 1)
            for m in range(2):
                gather_gu(m, m, 0, 0)
            pe.wait_ge(s_wl, 2)
            with pe.Fori(0, NI // 2 - 1) as e:
                for s in range(2):
                    chunk(2 * e + s, s, e, True)
            chunk(NI - 2, 0, NI // 2 - 1, True)
            chunk(NI - 1, 1, NI // 2 - 1, False)

            pe.wait_ge(s_hf, 4 * NI + 2)
            pe.wait_ge(s_wl, NGATHER)
            with pe.Fori(0, TT // 2) as e:
                for s in range(2):
                    tile = 2 * e + s
                    pe.wait_ge(s_ht[s], 16 * (e + 1))
                    for c in range(2):
                        pe.wait_ge(s_y5, 2 * tile + c + 1)
                        product(bk[2 * s + c], [(ht[s][:, i, a, :], wd[:, i, w, c * HALF:(c + 1) * HALF])
                                                for i in range(NI) for w, a in PASSES]).then_inc(s_d, 1)

        @block.sync
        def _(sp):
            wqkv_v = t_in["L0_attn_Wqkv"].rearrange("(p c) f -> p c f", c=KC)
            for b in range(GB):
                sp.dma_start(xs[0:S, b, :], rows(x_rows, b)).then_inc(s_xs[b], 16)
            sp.dma_start(wqkv, wqkv_v).then_inc(s_w1, 16)
            with nc.allow_non_contiguous_dma(reason="short bias columns"):
                sp.dma_start(bqk, t_in["L0_attn_bqkv"][0:2 * HD].rearrange("(c p) -> p c", p=P)).then_inc(s_bias, 16)
            sp.dma_start(vb_b, t_in["L0_attn_bqkv"][2 * HD:3 * HD].partition_broadcast(P)).then_inc(s_bias, 16)
            sp.dma_start(wo, t_in["L0_attn_Wo"].rearrange("(c p) n -> p c n", p=P)).then_inc(s_w1, 16)
            sp.dma_start(bo_b, t_in["L0_attn_bo"].partition_broadcast(P)).then_inc(s_bo, 16)
            for n in range(2):
                sp.dma_start(xr[0:S, n, :], rows(x_rows, n)).then_inc(s_xr[n], 16)
            sp.dma_start(bqc, t_in["L0_xattn_bq"].rearrange("(p c) -> p c", c=KC)).then_inc(s_wk, 16)
            sp.dma_start(bkc, t_in["L0_xattn_bk"].rearrange("(p c) -> p c", c=KC)).then_inc(s_wk, 16)
            sp.dma_start(wk, t_in["L0_xattn_Wk"].rearrange("(p c) y -> p c y", c=KC)).then_inc(s_wk, 16)
            wq_v = t_in["L0_xattn_Wq"].rearrange("(p c) x -> p c x", c=KC)
            for i in range(2):
                sp.dma_start(wq[i], wq_v[:, :, i * P:(i + 1) * P]).then_inc(s_wq[i], 16)

            def self_attention(g, more):
                if more:
                    sp.wait_ge(s_xt, KC * (g + 1))
                    for b in range(GB):
                        sp.dma_start(xs[0:S, b, :], rows(x_rows, g * GB + GB + b)).then_inc(s_xs[b], 16)
                for b in range(GB):
                    if more or b + 2 < GB:
                        sp.wait_ge(s_y, 2 * (g * GB + b + 1))
                        sp.dma_start(xr[0:S, b % 2, :], rows(x_rows, g * GB + b + 2)).then_inc(s_xr[b % 2], 16)
                    sp.wait_ge(s_n, g * GB + b + 1)
                    sp.dma_start(rows(x1_d, g * GB + b), yo[0:S, b % 2, :]).then_inc(s_yout[b % 2], 16)

            with sp.Fori(0, NG - 1) as g:
                self_attention(g, True)
            self_attention(NG - 1, False)

            for m, name in enumerate(("gate", "up", "down")):
                sp.dma_start(s_flat[m], t_in[f"L0_ffn_{name}_scales"].rearrange("g n -> (g n)").rearrange(
                    "(p c) -> p c", p=P)).then_inc(s_tin[0], 16)
            with sp.Fori(0, KC // 2 - 1) as e:
                for i in range(2):
                    sp.wait_ge(s_m, 2 * e + i + 1)
                    sp.dma_start(wq[i], wq_v[:, :, bass.ds((2 * e + 2 + i) * P, P)]).then_inc(s_wq[i], 16)

            for m, name in enumerate(("gate", "up", "down")):
                if m > 0:
                    sp.wait_ge(s_t, T[f"idx{m - 1}"])
                idx = t_in[f"L0_ffn_{name}_g_idx"]
                sp.dma_start(tmp_i[:, 0:idx.shape[0]], idx.partition_broadcast(P)).then_inc(s_tin[1], 16)
            for m, name in enumerate(("gate", "up", "down")):
                sp.wait_ge(s_t, T[f"tab{m - 1}"] if m else T["idx2"])
                scales, zeros = t_in[f"L0_ffn_{name}_scales"], t_in[f"L0_ffn_{name}_qzeros"]
                groups = scales.shape[0]
                sp.dma_start(tmp[0:groups, 0:scales.shape[1]], scales).then_inc(s_tin[2], 16)
                sp.dma_start(qz[96:96 + groups, 0:zeros.shape[1]], zeros.bitcast(U32)).then_inc(s_tin[3], 16)
                if m in (1, 2):
                    sp.dma_start(tab_d[:, :, m - 1, :].rearrange("i p c -> p i c"),
                                 tab.rearrange("p (i c) -> p i c", c=P)).then_inc(s_tabo, 16)
            for i in range(2):
                sp.wait_ge(s_yout[i], 16 * (NB // 2 + 1))
            sp.wait_ge(s_t, T["idx2"])
            for b in range(GB):
                sp.dma_start(xs[0:S, b, :], rows(x1_d, b)).then_inc(s_xs[b], 16)
            for i in range(2):
                sp.dma_start(xr[0:S, i, :], rows(x1_d, i)).then_inc(s_xr[i], 16)

            def load_ctx(n, i):
                base = n * CTX
                for c in range(CC - 1):
                    sp.dma_start(cx[i][:, c, :], ctx_rows[bass.ds(base + c * P, P), :]).then_inc(s_cx[i], 16)
                even = CP[-1] // 16 * 16
                last = (CC - 1) * P
                sp.dma_start(cx[i][0:even, CC - 1, :],
                             ctx_rows[bass.ds(base + last, even), :]).then_inc(s_cx[i], 16)
                sp.dma_start(cx[i][even:CP[-1], CC - 1, :],
                             ctx_rows[bass.ds(base + last + even, CP[-1] - even), :]).then_inc(s_cx[i], 16)

            ctx_rows = ctx_d.rearrange("b s d -> (b s) d")
            load_ctx(0, 0)
            sp.wait_ge(s_t, T["tab2"])
            sp.wait_ge(s_tabo, 32)
            load_ctx(1, 1)

            def cross_attention(g, more):
                if more:
                    sp.wait_ge(s_xt, KC * (g + NG + 1))
                    for b in range(GB):
                        sp.dma_start(xs[0:S, b, :], rows(x1_d, g * GB + GB + b)).then_inc(s_xs[b], 16)
                for b in range(GB):
                    n = g * GB + b
                    if more or b + 2 < GB:
                        sp.wait_ge(s_at, 2 * (n + 1))
                        load_ctx(n + 2, b % 2)
                        sp.wait_ge(s_y3, 2 * (n + 1))
                        sp.dma_start(xr[0:S, b % 2, :], rows(x1_d, n + 2)).then_inc(s_xr[b % 2], 16)
                    sp.wait_ge(s_n, NB + n + 1)
                    sp.dma_start(rows(x2_d, n), yo[0:S, b % 2, :]).then_inc(s_yout[b % 2], 16)

            with sp.Fori(0, NG - 1) as g:
                cross_attention(g, True)
            cross_attention(NG - 1, False)

            def load_chunk(i, s, w):
                for m, name in enumerate(("gate", "up")):
                    sp.dma_start(qw[s][m][:, 0:w], t_in[f"L0_ffn_{name}_qweight"][:, bass.ds(i * P, w)].bitcast(
                        U32)).then_inc(s_qw[s], 16)
                sp.dma_start(tabc[s], tab_d[bass.ds(i, 1)].rearrange("o p m c -> p (o m) c")).then_inc(s_tc[s], 16)

            def load_down(i, w):
                rows8 = t_in["L0_ffn_down_qweight"][bass.ds(i * (P // 8), w // 8), :]
                sp.dma_start(wbuf[2].bitcast(I32)[0:w, :], rows8.unsqueeze(1).to_broadcast([w // 8, 8, D])).then_inc(s_qd, 16)

            def chunk(i, s, w_down, w_next):
                sp.wait_ge(s_wf, 3 * i + 2)
                sp.wait_ge(s_wh, 3 * i + 2)
                sp.wait_ge(s_wl, 3 * i + 2)
                load_down(i, w_down)
                if w_next:
                    load_chunk(i + 2, s, w_next)
                for u in range(2):
                    sp.wait_ge(s_hh, 4 * i + 2 * u + 3)
                    sp.wait_ge(s_hl, 4 * i + 2 * u + 3)
                    half = slice(u * TT // 2, (u + 1) * TT // 2)
                    for l in range(2):
                        sp.dma_start(h_d[half, :, bass.ds(i, 1), l, :].rearrange("t p o c -> p t (o c)"),
                                     h_st[:, l, u * NT // 2:(u + 1) * NT // 2].rearrange("p (t c) -> p t c", c=P)
                                     ).then_inc(s_ho[u], 16)

            sp.wait_ge(s_lo, 2 * NB + 1)
            for i in range(2):
                sp.wait_ge(s_yout[i], 16 * (NB + 1))
            load_chunk(0, 0, P)
            load_chunk(1, 1, P)
            with sp.Fori(0, NI // 2 - 2) as e:
                for s in range(2):
                    chunk(2 * e + s, s, P, P)
            chunk(NI - 4, 0, P, P)
            chunk(NI - 3, 1, P, LASTC)
            chunk(NI - 2, 0, P, 0)
            chunk(NI - 1, 1, LASTC, 0)

            sp.wait_ge(s_up, 4 * NI)
            sp.wait_ge(s_wl, NGATHER)
            sp.wait_ge(s_wh, NGATHER)
            for u in range(2):
                sp.wait_ge(s_ho[u], 32 * (NI + 1))

            def load_tile(tile, s):
                sp.dma_start(ht[s].rearrange("p i l c -> p (i l c)"),
                             h_d[bass.ds(tile, 1)].rearrange("o p i l c -> p (o i l c)")).then_inc(s_ht[s], 16)

            def load_x2(tile, s):
                sp.dma_start(xf[s], x2_d[bass.ds(tile * P, P), :]).then_inc(s_xf[s], 16)

            out_rows = out.rearrange("b s d -> (b s) d")
            for s in range(2):
                load_tile(s, s)
            for s in range(2):
                load_x2(s, s)

            def down_tile(tile, s, more):
                if more:
                    sp.wait_ge(s_d, 2 * tile + 2)
                    load_tile(tile + 2, s)
                    sp.wait_ge(s_y5, 2 * tile + 2 + 4)
                    load_x2(tile + 2, s)
                sp.wait_ge(s_n5, tile + 1)
                sp.dma_start(out_rows[bass.ds(tile * P, P), :], yf[s]).then_inc(s_fin[s], 16)

            with sp.Fori(0, TT // 2 - 1) as e:
                for s in range(2):
                    down_tile(2 * e + s, s, True)
            for s in range(2):
                down_tile(TT - 2 + s, s, False)
            for s in range(2):
                sp.wait_ge(s_fin[s], 16 * (TT // 2 + 1))


_INS = ["x", "ctx_4096", "L0_attn_Wqkv", "L0_attn_bqkv", "L0_attn_Wo", "L0_attn_bo",
        "L0_xattn_Wq", "L0_xattn_bq", "L0_xattn_Wk", "L0_xattn_bk"] + [
    f"L0_ffn_{m}_{p}" for m in ("gate", "up", "down") for p in ("qweight", "scales", "qzeros", "g_idx")]


def kernel(**inputs):
    import numpy as _np
    import concourse.bacc as _bacc
    from concourse import mybir as _mybir
    from concourse.bass_utils import run_bass_kernel_spmd as _run

    nc = _bacc.Bacc("TRN2", target_bir_lowering=False, num_devices=1)
    arrays, t_in = {}, {}
    for name in _INS:
        a = _np.ascontiguousarray(inputs[name])
        arrays[f"in_{name}"] = a
        t_in[name] = nc.dram_tensor(f"in_{name}", a.shape, _mybir.dt.from_np(a.dtype), kind="ExternalInput").ap()
    out = nc.dram_tensor("out_0", inputs["x"].shape, _mybir.dt.float32, kind="ExternalOutput").ap()
    decoder_layer(nc, t_in, out)
    r = _run(nc, [arrays], core_ids=[0])
    return r.results[0]["out_0"]
```

```python
from contextlib import ExitStack

import numpy as np

import concourse.bass as bass
from concourse import mybir

F32 = mybir.dt.float32
F16 = mybir.dt.float16
BF16 = mybir.dt.bfloat16
I32 = mybir.dt.int32
U32 = mybir.dt.uint32
ALU = mybir.AluOpType
ACT = mybir.ActivationFunctionType
AX = mybir.AxisListType
RMAX = bass.bass_isa.ReduceOp.max

P = 128
EPS = 1e-5
PASSES = ((0, 0), (0, 1), (1, 0))


def decoder_layer(nc, t_in, out):
    x_d, ctx_d = t_in["x"], t_in["ctx_4096"]
    NB, S, D = x_d.shape
    CTX = ctx_d.shape[1]
    HD = t_in["L0_attn_Wo"].shape[0]
    FF = t_in["L0_ffn_gate_qweight"].shape[1]
    GU = t_in["L0_ffn_gate_scales"].shape[0]
    GD = t_in["L0_ffn_down_scales"].shape[0]
    KC = D // P
    HC = HD // P
    GB = 4
    NG = NB // GB
    TG = GB * S
    NT = NB * S
    NI = -(-FF // P)
    FP = NI * P
    LASTC = FF - (NI - 1) * P
    TT = NT // P
    HALF = 512
    CP = [min(P, CTX - c * P) for c in range(-(-CTX // P))]
    CC = len(CP)
    XS = 1024.0
    assert NB % GB == 0 and TG <= 512 and D == 2 * HALF and NI % 2 == 0 and TT % 2 == 0 and KC == 8

    x1_d = nc.dram_tensor("x1_scratch", (NT, D), F32).ap()
    x2_d = nc.dram_tensor("x2_scratch", (NT, D), F32).ap()
    h_d = nc.dram_tensor("h_scratch", (TT, P, NI, 2, P), F16).ap()
    down_d = nc.dram_tensor("down_table_scratch", (P, NI * P + 2 * D), BF16).ap()
    tab_d = nc.dram_tensor("table_scratch", (NI, P, 2, P), BF16).ap()

    with ExitStack() as ctx:
        def sem(name):
            return ctx.enter_context(nc.semaphore(name))

        def sb(name, shape, dt):
            return ctx.enter_context(nc.sbuf_tensor(name, shape, dt))

        ARENA = 203 * 1024
        arena = sb("arena", [P, ARENA // 4], F32)

        def carve(byte, shape, dt):
            size = {F32: 4, I32: 4, U32: 4, F16: 2, BF16: 2}[dt]
            n = int(np.prod(shape)) * size
            assert byte % 4 == 0 and n % 4 == 0 and byte + n <= ARENA, (byte, n)
            v = arena[:, byte // 4:(byte + n) // 4]
            if dt is not F32:
                v = v.bitcast(dt)
            if len(shape) == 2:
                v = v.rearrange("p (a b) -> p a b", b=shape[1])
            elif len(shape) == 3:
                v = v.rearrange("p (a b c) -> p a b c", b=shape[1], c=shape[2])
            elif len(shape) == 4:
                v = v.rearrange("p (a b c d) -> p a b c d", b=shape[1], c=shape[2], d=shape[3])
            return v

        at_x2t = 0
        at_tab = at_x2t + KC * NT * 4
        at_rest = at_tab + 4 * 2 * D + 2 * FP + 2 * 2 * D
        at_xs = at_rest
        at_xt = at_xs + 2 * D * 4
        at_yo = at_xt + KC * TG * 4
        at_gt = at_yo + 2 * D * 4
        at_m = at_gt + KC * TG * 4
        at_ctx = at_m + KC * D * 4
        at_ctxt = at_ctx + 3 * CC * D * 4
        at_pt3 = at_ctxt + KC * CTX * 4
        at_ub = at_pt3 + CC * S * 4

        x2t = carve(at_x2t, [2, KC, NT], F16)
        wk = carve(at_x2t, [KC, D], F32)
        wq = [carve(at_x2t + KC * D * 4 + i * KC * P * 4, [KC, P], F32) for i in range(2)]
        sel_s = [carve(at_tab + m * 2 * D, [KC, P], BF16) for m in range(2)]
        sel_z = [carve(at_tab + (2 + m) * 2 * D, [KC, P], BF16) for m in range(2)]
        n_down = FP + 2 * D
        down_tabs = carve(at_tab + 8 * D, [n_down], BF16)
        sel_d = carve(at_tab + 8 * D, [NI, P], BF16)
        tab_ds = carve(at_tab + 8 * D + 2 * FP, [D], BF16)
        tab_dz = carve(at_tab + 8 * D + 2 * FP + 2 * D, [D], BF16)
        xr3 = carve(at_tab + 8 * D, [2, D], F32)
        g_f = carve(at_tab + 16 * D, [2 * S], F32)
        assert 8 * D + 8 * S <= 2 * n_down

        xt = carve(at_xt, [KC, TG], F32)
        yo = carve(at_yo, [2, D], F32)
        xtp = carve(at_xt, [2, KC, TG], F16)
        gtp = carve(at_gt, [2, KC, TG], F16)
        acc_u = carve(at_xt, [D], F32)
        part = carve(at_xt + 4 * D, [D], F32)
        acc_v = carve(at_ub, [D], F32)
        qkt = carve(at_gt, [2 * HC, TG], F32)
        pr = carve(at_gt + 2 * HC * TG * 4, [GB, S], F32)
        pt = carve(at_gt + (2 * HC + 1) * TG * 4, [GB, S], F32)
        ot = carve(at_gt + (2 * HC + 2) * TG * 4, [HC, TG], F32)
        m32 = carve(at_m - 4 * D, [KC, D], F32)
        mp = carve(at_m, [KC, 2, D], F16)
        wqkv = carve(at_m, [KC, 3 * HD], F32)
        wo = carve(at_m + KC * 3 * HD * 4, [HC, D], F32)
        xs = carve(at_ctx, [GB, D], F32)
        v_sb = carve(at_ctx + GB * D * 4, [GB, HD], F32)
        bo_b = carve(at_ctx + (GB + 1) * D * 4, [D], F32)
        vb_b = carve(at_ctx + (GB + 2) * D * 4, [HD], F32)
        xr = carve(at_ctxt, [2, D], F32)
        xs3 = carve(at_xs, [2, D], F32)
        cx = carve(at_ctx, [CC, D], F32)
        cxp = [carve(at_ctx + (1 + i) * CC * D * 4, [2, CC, D], F16) for i in range(2)]
        cxt = carve(at_ctxt, [2, KC, CTX], F16)
        pt3 = carve(at_pt3, [2, CC, S], F16)
        u_b = carve(at_ub, [D], F32)
        at_tmp = at_ctx + (GB + 2) * D * 4 + HD * 4
        tmp = carve(at_tmp, [FP], F32)
        tmp_i = carve(at_tmp, [FP], I32)
        assert at_tmp + 4 * FP <= at_ctxt
        at_low = at_x2t + (KC * D + 2 * KC * P) * 4
        tab = carve(at_low, [FP], BF16)
        mid = carve(at_low + 2 * FP, [FP], BF16)
        qz = carve(at_low + 4 * FP, [FF // 8], U32)
        flat = [t_in[f"L0_ffn_{m}_scales"].shape[0] * t_in[f"L0_ffn_{m}_scales"].shape[1] // P
                for m in ("gate", "up", "down")]
        s_flat = [carve(at_low + 4 * FP + FF // 2 + 4 * sum(flat[:m]), [flat[m]], F32) for m in range(3)]
        assert at_low + 4 * FP + FF // 2 + 4 * sum(flat) <= at_tab
        wd = carve(at_rest, [NI, 2, D], F16)
        at_b = at_rest + NI * 2 * D * 2
        wgu = [[carve(at_b + (s * 2 + m) * 4 * D, [2, KC, P], F16) for m in range(2)] for s in range(2)]
        at_b += 16 * D
        wbuf = [carve(at_b + i * 4 * D, [D], F32) for i in range(3)]
        at_b += 12 * D
        qw = [[carve(at_b + (s * 2 + m) * 4 * P, [P], U32) for m in range(2)] for s in range(2)]
        at_b += 16 * P
        tabc = [carve(at_b + s * 4 * P, [2, P], BF16) for s in range(2)]
        at_b += 8 * P
        h_st = carve(at_b, [2, NT], F16)
        at_b += NT * 4
        g_act = carve(at_b, [TG], F32)
        h_f = carve(at_b + TG * 4, [TG], F32)
        at_c = at_rest + NI * 2 * D * 2
        ht = [carve(at_c + i * NI * 4 * P, [NI, 2, P], F16) for i in range(2)]
        xf = [carve(at_x2t + i * D * 4, [D], F32) for i in range(2)]
        yf = [carve(at_x2t + (2 + i) * D * 4, [D], F32) for i in range(2)]

        ident = sb("ident", [P, P], F32)
        ones = sb("ones", [P, 1], F32)
        ident_h = sb("ident_f16", [P, P], F16)
        sp_ = sb("logits", [P, CTX + 1], F32)
        small = sb("small", [P, 160], F32)
        small_i = small[:].bitcast(I32)
        c_ = {}
        used = [0]

        def col(name, n=1):
            c_[name] = small[:, used[0]:used[0] + n]
            used[0] += n
            return c_[name]

        bqk = col("bqk", 2 * HC)
        mx1, nm1, rs1, rc1 = col("mx1", GB), col("nm1", GB), col("rs1", GB), col("rc1", GB)
        st, mv, ve, rstd, mhalf = col("st", 12), col("mv", 2), col("ve"), col("rstd"), col("mhalf")
        bqc, bkc, v2, v2s, c0 = col("bqc", KC), col("bkc", KC), col("v2", KC), col("v2s", KC), col("c0")
        rr, nm3, rs3, rc3 = col("rr", GB), col("nm3"), col("rs3", GB), col("rc3", GB)
        amx, amr, pw, fac = col("amx", 3), col("amr", 3), col("pw", 4), col("fac", 3)
        inv_g, sc_u, inv_d, ghu = col("inv_g"), col("sc_u"), col("inv_d"), col("ghu")
        rowid, rowid_f, nib, four = col("rowid", 1), col("rowid_f"), col("nib", 3), col("masks", KC)
        mgp, mag, magr, pwg, fm, kg, ig = col("mgp", 3), col("mag", 2), col("magr", 2), col("pwg", 2), col("fm"), col("kg"), col("ig")
        cmx, cmr, pwc = col("cmx", 2), col("cmr", 2), col("pwc")
        fc, il, ia = col("fc", GB), col("il", GB), col("ia", GB)
        pc = col("pc", KC)
        assert used[0] <= 160

        psum = ctx.enter_context(nc.psum_tensor("psum", [P, 8 * 512], F32))
        bk = [psum[:, i * 512:(i + 1) * 512] for i in range(8)]
        bkh = [b.bitcast(F16).rearrange("p (l c) -> p l c", l=2) for b in bk]
        ct_bank = (0, 1, 6, 7)
        CT_ACT, CT_DVE = (0, 1, 2, 3, 4, 6), (5, 7)
        NA, ND = len(CT_ACT), len(CT_DVE)
        LOW = 1e-25

        s_const = sem("constants"); s_cc = sem("constant_step")
        s_w1 = sem("weights_stage1_in"); s_bias = sem("biases_in"); s_bo = sem("bo_in")
        s_xs = [sem(f"xs_in{b}") for b in range(GB)]
        s_xr = [sem(f"residual_in{i}") for i in range(2)]
        s_yout = [sem(f"rows_out{i}") for i in range(2)]
        s_xt = sem("xT_in_psum"); s_xta = sem("xT_even_copied"); s_xtd = sem("xT_odd_copied")
        s_x1t = sem("x1T_in_psum"); s_x1h = sem("x1T_hi_ready"); s_x1l = sem("x1T_lo_ready")
        s_xs3 = [sem(f"x1_rows_in{i}") for i in range(2)]; s_xr3 = [sem(f"x1_residual_in{i}") for i in range(2)]
        s_ch = sem("ctx_hi_ready"); s_cl = sem("ctx_lo_ready"); s_cm = sem("ctx_max_ready"); s_cr = sem("ctx_max_all"); s_cf = sem("ctx_factor_step"); s_stash = sem("down_tables_out"); s_unstash = sem("down_tables_in")
        s_ub = sem("u_rows_in_psum"); s_pv = sem("bqbk_parts"); s_pu = sem("bqWk_parts"); s_uc = sem("Wqbk_parts"); s_mm = sem("m_max_step"); s_mf = sem("m_max_all"); s_fs = sem("m_factor_step"); s_mh = sem("m_hi_ready"); s_ml = sem("m_lo_ready"); s_gh = sem("g_hi_ready"); s_gl = sem("g_lo_ready"); s_ih = sem("f16_identity"); s_seen2 = sem("wait_seen"); s_ube = sem("u_rows_copied")
        s_qk = sem("qk_in_psum"); s_qke = sem("qk_copied")
        s_s = sem("scores_in_psum"); s_v = sem("v_in_psum"); s_ve = sem("v_copied")
        s_mx = sem("max_ready"); s_nm = sem("neg_max_ready"); s_exp = sem("exp_done")
        s_rc = sem("recip_ready"); s_p = sem("probs_ready"); s_pt = sem("probsT_in_psum")
        s_pte = sem("probsT_copied"); s_o = sem("oT_in_psum"); s_oe = sem("oT_copied")
        s_w = sem("attn_in_psum"); s_xb = sem("residual_plus_bo"); s_y = sem("sum_ready")
        s_st = sem("stats_ready"); s_seen = sem("stats_seen"); s_ag = sem("mean_var_ready"); s_eps = sem("var_eps_ready")
        s_rstd = sem("rstd_ready"); s_n = sem("rows_normalised")
        s_wk = sem("wk_in"); s_wq = [sem(f"wq_in{i}") for i in range(2)]
        s_m = sem("m_in_psum"); s_me = sem("m_copied"); s_v2 = sem("v2_in_psum"); s_v2e = sem("v2_copied")
        s_tin = [sem(f"table_input{i}_in") for i in range(6)]; s_t = sem("table_step"); s_amx = sem("scale_max_all")
        s_tabo = sem("tables_out")
        s_cx = sem("ctx_in")
        s_ct = sem("ctxT_in_psum"); s_cta = sem("ctxT_even_copied"); s_ctd = sem("ctxT_odd_copied")
        s_g = sem("g_in_psum"); s_ge = sem("g_copied"); s_re = sem("row_term_ready")
        s_l = sem("logits_in_psum"); s_le = sem("logits_copied"); s_rb = sem("row_term_with_biases"); s_lm = sem("logit_max")
        s_ex3 = sem("exp3_done"); s_rc3 = sem("recip3_ready")
        s_pt3 = sem("p3T_in_psum"); s_ph = sem("p3T_hi_ready"); s_pl = sem("p3T_lo_ready"); s_at = sem("attended_in_psum")
        s_y3 = sem("sum3_ready"); s_x2t = sem("x2T_in_psum"); s_hi = sem("x2T_hi_ready"); s_lo = sem("x2T_lo_ready")
        s_qw = [sem(f"qw_in{i}") for i in range(2)]; s_tc = [sem(f"tabc_in{i}") for i in range(2)]
        s_qd = sem("qw_down_in")
        s_ga = sem("gather_in_psum"); s_wf = sem("weights_f32_ready"); s_dq = sem("dequant_step")
        s_wh = sem("weights_hi_ready"); s_wl = sem("weights_lo_ready")
        s_gp = sem("gate_in_psum"); s_up = sem("up_in_psum")
        s_si = sem("silu_ready"); s_hf = sem("h_f32_ready"); s_hh = sem("h_hi_ready"); s_hl = sem("h_lo_ready")
        s_ho = [sem(f"h_out{i}") for i in range(2)]
        s_ht = [sem(f"hT_in{i}") for i in range(2)]; s_xf = [sem(f"x2_in{i}") for i in range(2)]
        s_d = sem("down_in_psum"); s_y5 = sem("sum5_ready"); s_n5 = sem("rows5_normalised")
        s_fin = [sem(f"final_out{i}") for i in range(2)]

        block = ctx.enter_context(nc.Block())

        def rows(ap, n):
            return ap[bass.ds(n * S, S), :]

        x_rows = x_d.rearrange("b s d -> (b s) d")
        NLN = 2 * NB
        NGATHER = 3 * NI

        def down_no(i):
            return 3 * i + 4

        def ctx_pieces(n):
            return 16 * (CC + 1) * n + 16 * (CC + 1)

        def known(n, limit):
            return isinstance(n, int) and n < limit

        def batches(g, has):
            for b in range(GB):
                n = g * GB + b
                yield b, n, (lambda k, b=b: has or b + k < GB)

        def wd_parts(i):
            if isinstance(i, int):
                return [wd[:, i, l, :] for l in range(2)]
            return [wd[:, bass.ds(i, 1), l, :].rearrange("p o c -> p (o c)") for l in range(2)]

        T = {}

        @block.vector
        def _(dve):
            for i in range(2):
                dve.sem_inc(s_yout[i], 16)
                dve.sem_inc(s_ho[i], 32)
                dve.sem_inc(s_fin[i], 16)
            dve.sem_inc(s_hf, 2)
            dve.sem_inc(s_hl, 1)
            dve.sem_inc(s_hh, 1)
            dve.sem_inc(s_lo, 1)
            dve.sem_inc(s_y5, 4)

            def norm_stats(y, k, summed, first):
                n = y.shape[0]
                for h in range(2):
                    dve.wait_ge(summed, first + h)
                    dve.bn_stats(st[0:n, 6 * h:6 * h + 6], y[:, h * HALF:(h + 1) * HALF]).then_inc(s_st, 1)
                dve.wait_ge(s_st, 2 * k + 2)
                dve.sem_inc(s_seen, 1)
                dve.bn_aggr(mv[0:n, :], st[0:n, :]).then_inc(s_ag, 1)
                dve.wait_ge(s_ag, k + 1)
                dve.tensor_scalar(ve[0:n, :], mv[0:n, 1:2], EPS, None, ALU.add).then_inc(s_eps, 1)

            def norm_apply(y, k, done):
                n = y.shape[0]
                dve.wait_ge(s_rstd, k + 1)
                dve.tensor_scalar(y, y, mv[0:n, 0:1], rstd[0:n, :], ALU.subtract, ALU.mult).then_inc(done, 1)

            def transposed_rows(g, chunks):
                for c in chunks:
                    dve.wait_ge(s_xt, KC * g + c + 1)
                    dve.tensor_copy(xt[:, c, :], bk[1][:, 0:TG]).then_inc(s_xtd, 1)

            def self_attention(g, more):
                dve.wait_ge(s_s, g + 1)
                dve.tensor_reduce(mx1[0:S, :], bk[2][0:S, 0:TG].rearrange("p (b k) -> p b k", b=GB), AX.X,
                                  ALU.max, negate=True).then_inc(s_mx, 1)
                dve.wait_ge(s_mx, g + 1)
                dve.tensor_scalar(nm1[0:S, :], mx1[0:S, :], HD ** -0.5, None, ALU.mult).then_inc(s_nm, 1)
                dve.wait_ge(s_exp, GB * g + GB)
                dve.reciprocal(rc1[0:S, :], rs1[0:S, :]).then_inc(s_rc, 1)
                dve.wait_ge(s_rc, g + 1)
                dve.tensor_tensor(pr[0:S, :, :], pr[0:S, :, :], rc1[0:S, :].unsqueeze(2).to_broadcast([S, GB, S]),
                                  ALU.mult).then_inc(s_p, 1)
                dve.wait_ge(s_bias, 32)
                for p in range(2):
                    dve.wait_ge(s_v, 2 * g + p + 1)
                    dve.tensor_tensor(v_sb[0:S, 2 * p:2 * p + 2, :],
                                      bk[4 + p][0:S, :].rearrange("p (b d) -> p b d", b=2),
                                      vb_b[0:S, :].unsqueeze(1).to_broadcast([S, 2, HD]), ALU.add).then_inc(s_ve, 1)
                dve.wait_ge(s_pt, g + 1)
                dve.tensor_copy(pt[0:S, :, :], bk[4][0:S, 0:TG].rearrange("p (b k) -> p b k", b=GB)).then_inc(s_pte, 1)
                if more:
                    transposed_rows(g + 1, (1, 3))
                    transposed_rows(g + 1, (5, 7))
                for b in range(GB):
                    n = g * GB + b
                    dve.wait_ge(s_xb, n + 1)
                    dve.wait_ge(s_yout[b % 2], 16 * (2 * g + b // 2 + 1))
                    for h in range(2):
                        cols = slice(h * HALF, (h + 1) * HALF)
                        dve.wait_ge(s_w, 2 * n + h + 1)
                        dve.tensor_tensor(yo[0:S, b % 2, cols], bk[6 + h][0:S, :], xr[0:S, b % 2, cols],
                                          ALU.add).then_inc(s_y, 1)
                    norm_stats(yo[0:S, b % 2, :], n, s_y, 2 * n + 1)
                    norm_apply(yo[0:S, b % 2, :], n, s_n)

            transposed_rows(0, (1, 3, 5, 7))
            with dve.Fori(0, NG - 1) as g:
                self_attention(g, True)
            self_attention(NG - 1, False)

            steps = [0]

            def step(ins):
                ins.then_inc(s_t, 1)
                steps[0] += 1
                dve.wait_ge(s_t, steps[0])

            dve.wait_ge(s_tin[0], 48)
            for m in range(3):
                step(dve.tensor_reduce(amx[:, m:m + 1], s_flat[m], AX.X, ALU.max, apply_absolute_value=True))
            T["amx"] = steps[0]
            dve.wait_ge(s_amx, 1)
            step(dve.tensor_scalar(amr, amr, 1e-15, None, ALU.max))
            step(dve.tensor_tensor(ghu, amr[:, 0:1], amr[:, 1:2], ALU.mult))
            step(dve.tensor_scalar(pw[:, 0:3].bitcast(I32), amr.bitcast(I32), 0x7F800000, None, ALU.bitwise_and))
            step(dve.tensor_scalar(pw[:, 3:4].bitcast(I32), ghu.bitcast(I32), 0x7F800000, None, ALU.bitwise_and))
            step(dve.reciprocal(fac, pw[:, 0:3]))
            step(dve.tensor_scalar(fac, fac, 1024.0, None, ALU.mult))
            step(dve.tensor_scalar(inv_g, pw[:, 0:1], 2.0 ** -10 / XS, None, ALU.mult))
            step(dve.reciprocal(sc_u, pw[:, 3:4]))
            step(dve.tensor_tensor(sc_u, sc_u, pw[:, 1:2], ALU.mult))
            step(dve.tensor_scalar(sc_u, sc_u, 2.0 ** -24 / XS, None, ALU.mult))
            step(dve.tensor_tensor(inv_d, pw[:, 3:4], pw[:, 2:3], ALU.mult))
            step(dve.tensor_scalar(inv_d, inv_d, 2.0 ** 4, None, ALU.mult))
            dve.wait_ge(s_const, 4)
            step(dve.tensor_scalar(nib[:, 0:1].bitcast(I32), rowid.bitcast(I32), 31, None, ALU.bitwise_and))
            step(dve.tensor_copy(rowid_f, nib[:, 0:1].bitcast(I32)))
            step(dve.memset(nib[:, 1:2].bitcast(U32), 15))
            step(dve.tensor_scalar(nib[:, 0:1].bitcast(I32), rowid.bitcast(I32), 7, 2, ALU.bitwise_and,
                                   ALU.arith_shift_left))
            step(dve.tensor_tensor(nib[:, 2:3].bitcast(U32), nib[:, 1:2].bitcast(U32), nib[:, 0:1].bitcast(U32),
                                   ALU.logical_shift_left))
            for j in range(8):
                step(dve.memset(four[:, j:j + 1].bitcast(U32), 15 << (4 * j)))

            def selection(idx, groups, width, put):
                step(dve.tensor_scalar(neg[:, 0:width], idx, 0, groups, ALU.is_lt, ALU.mult))
                step(dve.tensor_tensor(tmp[:, 0:width], idx, neg[:, 0:width], ALU.add))
                step(dve.tensor_scalar(tmp[:, 0:width], tmp[:, 0:width], 0, groups - 1, ALU.max, ALU.min))
                for j in range(8):
                    put(slice(0, 96), j, 2.0 ** (-4 * j), tmp[0:96, j:width:8])
                    put(slice(96, 128), j, 2.0 ** (4 * j), tmp[96:128, j:width:8])

            neg = mid
            for m in range(2):
                step(dve.memset(sel_s[m].rearrange("p a b -> p (a b)").bitcast(U32), 0))
                step(dve.memset(sel_z[m].rearrange("p a b -> p (a b)").bitcast(U32), 0))
            step(dve.memset(sel_d.rearrange("p a b -> p (a b)").bitcast(U32), 0))
            step(dve.memset(tab_ds.bitcast(U32), 0))
            step(dve.memset(tab_dz.bitcast(U32), 0))
            for m, groups in enumerate((GU, GU, GD)):
                width = D if m < 2 else FF

                def put(r, j, factor, in0):
                    if m == 2:
                        dst = sel_d.rearrange("p a b -> p (a b)")[r, j:width:8]
                    else:
                        dst = (sel_s if r.start == 0 else sel_z)[m][r, j, :]
                    step(dve.tensor_scalar(dst, in0, rowid_f[r, :], factor, ALU.is_equal, ALU.mult))

                dve.wait_ge(s_tin[1], 16 * (m + 1))
                selection(tmp_i[:, 0:width], groups, width, put)
                T[f"idx{m}"] = steps[0]

            for m, groups in enumerate((GU, GU, GD)):
                width = FF if m < 2 else D
                s_to = tab if m < 2 else tab_ds
                z_to = tab if m < 2 else tab_dz
                if m == 0:
                    step(dve.memset(tab.bitcast(U32), 0))
                dve.wait_ge(s_tin[2], 16 * (m + 1))
                if m == 1:
                    dve.wait_ge(s_tabo, 16)
                s = tmp[0:groups, 0:width]
                step(dve.tensor_scalar(s, s, fac[0:groups, m:m + 1], None, ALU.mult))
                step(dve.tensor_copy(s_to[0:groups, 0:width], s))
                step(dve.tensor_tensor(s, s, s_to[0:groups, 0:width], ALU.subtract))
                step(dve.tensor_copy(mid[0:groups, 0:width], s))
                step(dve.tensor_copy(s_to[32:32 + groups, 0:width], s))
                step(dve.tensor_tensor(s, s, mid[0:groups, 0:width], ALU.subtract))
                step(dve.tensor_copy(s_to[64:64 + groups, 0:width], s))
                dve.wait_ge(s_tin[3], 16 * (m + 1))
                z = tmp_i[96:96 + groups, 0:width]
                for j in range(8):
                    step(dve.tensor_scalar(z[:, j:width:8].bitcast(U32), qz[96:96 + groups, 0:width // 8], 4 * j, 15,
                                           ALU.logical_shift_right, ALU.bitwise_and))
                step(dve.tensor_scalar(z_to[96:96 + groups, 0:width], z, 1, None, ALU.add))
                T[f"tab{m}"] = steps[0]
                lo, hi = ((0, 4), (4, 6), (6, KC))[m]
                dve.wait_ge(s_me, 2 + hi)
                step(dve.tensor_reduce(mgp[:, m:m + 1], m32[:, lo:hi, :].rearrange("p a b -> p (a b)"), AX.X, ALU.max,
                                       apply_absolute_value=True))
            dve.tensor_reduce(mag[:, 0:1], mgp, AX.X, ALU.max).then_inc(s_mm, 1)
            dve.wait_ge(s_v2e, 1)
            dve.tensor_reduce(mag[:, 1:2], v2, AX.X, ALU.max, apply_absolute_value=True).then_inc(s_mm, 1)

            def x1t_lo(m, b):
                cols = slice(b * S, (b + 1) * S)
                for j in range(2):
                    dve.wait_ge(s_x1h, 2 * m + j + 1)
                    dve.scalar_tensor_tensor(xtp[:, 1, 4 * j:4 * j + 4, cols],
                                             bk[2 + j][:, 0:TG].rearrange("p (a t) -> p a t", a=4), XS,
                                             xtp[:, 0, 4 * j:4 * j + 4, cols], ALU.mult, ALU.subtract).then_inc(s_x1l, 1)

            def slot_fills(n, b):
                return 8 * (n - b % 2) + 16

            def row_term(n, b):
                dve.wait_ge(s_xr3[b % 2], slot_fills(n, b))
                dve.wait_ge(s_yout[b % 2], 16 * NB // 2 + slot_fills(n, b))
                dve.tensor_tensor_reduce(yo[0:S, b % 2, :], xr3[0:S, b % 2, :], u_b[0:S, :], 1.0, 0.0,
                                         ALU.mult, ALU.add, rr[0:S, b:b + 1]).then_inc(s_re, 1)

            def softmax_in(n, b):
                dve.wait_ge(s_re, n + 1)
                dve.tensor_scalar(rr[0:S, b:b + 1], rr[0:S, b:b + 1], c0[0:S, :], D ** -0.5, ALU.add,
                                  ALU.mult).then_inc(s_rb, 1)
                dve.wait_ge(s_l, n + 1)
                dve.wait_ge(s_rb, n + 1)
                dve.tensor_scalar(sp_[0:S, 0:CTX], bk[5][0:S, 0:CTX], il[0:S, b:b + 1], rr[0:S, b:b + 1],
                                  ALU.mult, ALU.add).then_inc(s_le, 1)
                dve.wait_ge(s_le, n + 1)
                dve.tensor_reduce(nm3[0:S, :], sp_[0:S, 0:CTX], AX.X, ALU.max, negate=True).then_inc(s_lm, 1)

            def context_t(n):
                for c in CT_DVE:
                    dve.wait_ge(s_ct, KC * n + c + 1)
                    dve.tensor_copy(cxt[:, :, c, :], bkh[ct_bank[c % 4]][:, :, 0:CTX]).then_inc(s_ctd, 1)

            def context_max(n):
                dve.wait_ge(s_cx, ctx_pieces(n))
                dve.tensor_reduce(cmx[:, 0:1], cx[:, 0:CC - 1, :].rearrange("p c d -> p (c d)"), AX.X, ALU.max,
                                  apply_absolute_value=True)
                dve.tensor_reduce(cmx[0:CP[-1], 1:2], cx[0:CP[-1], CC - 1, :], AX.X, ALU.max,
                                  apply_absolute_value=True).then_inc(s_cm, 1)

            def context_factor(n, b):
                k = [0]

                def step(ins):
                    ins.then_inc(s_cf, 1)
                    k[0] += 1
                    dve.wait_ge(s_cf, 5 * n + k[0])

                dve.wait_ge(s_cr, n + 1)
                step(dve.tensor_reduce(pwc, cmr, AX.X, ALU.max))
                step(dve.tensor_scalar(pwc, pwc, LOW, None, ALU.max))
                step(dve.tensor_scalar(pwc.bitcast(I32), pwc.bitcast(I32), 0x7F800000, None, ALU.bitwise_and))
                dve.tensor_scalar(il[:, b:b + 1], pwc, ig, None, ALU.mult)
                dve.tensor_scalar(ia[:, b:b + 1], pwc, 2.0 ** -14 / XS, None, ALU.mult)
                step(dve.reciprocal(fc[:, b:b + 1], pwc))
                step(dve.tensor_scalar(fc[:, b:b + 1], fc[:, b:b + 1], 2.0 ** 14, None, ALU.mult))

            def context_lo(n, b, c):
                dve.wait_ge(s_ch, CC * n + c + 1)
                dve.scalar_tensor_tensor(cxp[b % 2][0:CP[c], 1, c, :], cx[0:CP[c], c, :], fc[0:CP[c], b:b + 1],
                                         cxp[b % 2][0:CP[c], 0, c, :], ALU.mult, ALU.subtract).then_inc(s_cl, 1)

            def probs_lo(n):
                dve.wait_ge(s_ph, n + 1)
                for c in range(CC):
                    ins = dve.scalar_tensor_tensor(pt3[0:CP[c], 1, c, :], bk[4][0:CP[c], c * P:c * P + S], XS,
                                                   pt3[0:CP[c], 0, c, :], ALU.mult, ALU.subtract)
                ins.then_inc(s_pl, 1)

            def x2t_lo(n):
                for j in range(2):
                    dve.wait_ge(s_hi, 2 * n + j + 1)
                    dve.scalar_tensor_tensor(x2t[:, 1, 4 * j:4 * j + 4, bass.ds(n * S, S)],
                                             bk[j][:, 0:TG].rearrange("p (a t) -> p a t", a=4), XS,
                                             x2t[:, 0, 4 * j:4 * j + 4, bass.ds(n * S, S)],
                                             ALU.mult, ALU.subtract).then_inc(s_lo, 1)

            def add_attended(n, b):
                y = yo[0:S, b % 2, :]
                dve.wait_ge(s_ex3, n + 1)
                dve.reciprocal(rc3[0:S, b:b + 1], rs3[0:S, b:b + 1]).then_inc(s_rc3, 1)
                dve.wait_ge(s_rc3, 2 * n + 1)
                dve.tensor_scalar(rc3[0:S, b:b + 1], rc3[0:S, b:b + 1], ia[0:S, b:b + 1], None,
                                  ALU.mult).then_inc(s_rc3, 1)
                dve.wait_ge(s_rc3, 2 * n + 2)
                for h in range(2):
                    cols = slice(h * HALF, (h + 1) * HALF)
                    dve.wait_ge(s_at, 2 * n + h + 1)
                    dve.scalar_tensor_tensor(y[:, cols], bk[6 + h][0:S, :], rc3[0:S, b:b + 1],
                                             xr3[0:S, b % 2, cols], ALU.mult, ALU.add).then_inc(s_y3, 1)

            def cross_attention(g, more):
                for b, n, has in batches(g, more):
                    y = yo[0:S, b % 2, :]
                    softmax_in(n, b)
                    if has(1):
                        context_t(n + 1)
                    if has(2):
                        context_max(n + 2)
                        context_factor(n + 2, (b + 2) % GB)
                    probs_lo(n)
                    add_attended(n, b)
                    if has(2):
                        context_lo(n + 2, (b + 2) % GB, 0)
                    norm_stats(y, NB + n, s_y3, 2 * n + 1)
                    if has(2):
                        for c in range(1, CC):
                            context_lo(n + 2, (b + 2) % GB, c)
                    if not known(n, 1):
                        x2t_lo(n - 1)
                    if more:
                        x1t_lo(n + GB, b)
                    if has(1):
                        row_term(n + 1, (b + 1) % GB)
                    norm_apply(y, NB + n, s_n)

            k = [0]

            def factor_step(ins):
                ins.then_inc(s_fs, 1)
                k[0] += 1
                dve.wait_ge(s_fs, k[0])

            factor_step(dve.memset(cmx, 0.0))
            context_max(0)
            dve.wait_ge(s_mf, 1)
            factor_step(dve.tensor_scalar(magr[:, 0:1], magr[:, 0:1], LOW, None, ALU.max))
            factor_step(dve.scalar_tensor_tensor(magr[:, 1:2], magr[:, 0:1], 1024.0, magr[:, 1:2], ALU.mult, ALU.add))
            factor_step(dve.tensor_scalar(pwg.bitcast(I32), magr.bitcast(I32), 0x7F800000, None, ALU.bitwise_and))
            factor_step(dve.reciprocal(mag, pwg))
            factor_step(dve.tensor_scalar(fm, mag[:, 0:1], 2.0 ** 14, None, ALU.mult))
            FM = k[0]
            factor_step(dve.tensor_scalar(kg, pwg[:, 0:1], mag[:, 1:2], 1 / XS, ALU.mult, ALU.mult))
            factor_step(dve.tensor_scalar(v2s, v2, mag[:, 1:2], 2.0 ** 14, ALU.mult, ALU.mult))
            factor_step(dve.tensor_scalar(ig, pwg[:, 1:2], 2.0 ** -28 * D ** -0.5, None, ALU.mult))
            T["fm"], T["g"] = FM, k[0]
            context_factor(0, 0)
            x1t_lo(0, 0)
            x1t_lo(1, 1)
            for c in range(CC):
                context_lo(0, 0, c)
            x1t_lo(2, 2)
            x1t_lo(3, 3)
            dve.wait_ge(s_ub, 1)
            dve.tensor_copy(u_b[0:S, :], psum[0:S, 2048:3072]).then_inc(s_ube, 1)
            for c in reversed(range(KC)):
                dve.wait_ge(s_mh, KC - c)
                dve.scalar_tensor_tensor(mp[:, c, 1, :], m32[:, c, :], fm, mp[:, c, 0, :], ALU.mult,
                                         ALU.subtract).then_inc(s_ml, 1)
            context_t(0)
            context_max(1)
            context_factor(1, 1)
            for c in range(CC):
                context_lo(1, 1, c)
            dve.wait_ge(s_ube, 1)
            row_term(0, 0)
            cross_attention(0, True)
            with dve.Fori(1, NG - 1) as g:
                cross_attention(g, True)
            cross_attention(NG - 1, False)
            x2t_lo(NB - 1)

            def dequant(q, kind, s, e):
                w = wbuf[kind]
                if kind < 2:
                    dve.wait_ge(s_qw[s], 32 * (e + 1))
                    if not isinstance(q, int) or q >= 2:
                        dve.wait_ge(s_wh, q - 1)
                        dve.wait_ge(s_wl, q - 1)
                    dve.tensor_tensor(w.bitcast(U32).rearrange("p (j n) -> p j n", j=8),
                                      qw[s][kind].unsqueeze(1).to_broadcast([P, 8, P]),
                                      four.bitcast(U32).unsqueeze(2).to_broadcast([P, 8, P]),
                                      ALU.bitwise_and).then_inc(s_dq, 1)
                else:
                    dve.wait_ge(s_qd, 16 * (e + 1))
                    dve.tensor_scalar(w.bitcast(U32), w.bitcast(U32), nib[:, 2:3].bitcast(U32), None,
                                      ALU.bitwise_and).then_inc(s_dq, 1)
                dve.wait_ge(s_ga, q + 1)
                dve.wait_ge(s_dq, 2 * q + 1)
                dve.tensor_tensor(w, w.bitcast(U32), psum[:, 3072:4096], ALU.subtract).then_inc(s_dq, 1)
                dve.wait_ge(s_dq, 2 * q + 2)
                dve.tensor_tensor(w, w, psum[:, 2048:3072], ALU.mult).then_inc(s_wf, 1)

            def hidden(i, t):
                dve.wait_ge(s_si, 4 * i + t + 1)
                dve.wait_ge(s_up, 4 * i + t + 1)
                dve.wait_ge(s_hh, 4 * i + t + 1)
                dve.wait_ge(s_hl, 4 * i + t + 1)
                dve.scalar_tensor_tensor(h_f, bk[2 + t % 2][:, 0:TG], sc_u, g_act, ALU.mult, ALU.mult).then_inc(s_hf, 1)
                if t % 2 == 0:
                    dve.wait_ge(s_ho[t // 2], 32 * (i + 1))
                dve.wait_ge(s_hh, 4 * i + t + 2)
                cols = slice(t * TG, (t + 1) * TG)
                dve.tensor_tensor(h_st[:, 1, cols], h_f, h_st[:, 0, cols], ALU.subtract).then_inc(s_hl, 1)

            def chunk(i, s, e, more):
                hidden(i, 0)
                if more:
                    dequant(3 * i + 2, 0, 1 - s, e + s)
                hidden(i, 1)
                if more:
                    dequant(3 * i + 3, 1, 1 - s, e + s)
                hidden(i, 2)
                dequant(down_no(i) if more else NGATHER - 1, 2, s, i)
                hidden(i, 3)

            for m in range(2):
                dequant(m, m, 0, 0)
            with dve.Fori(0, NI // 2 - 1) as e:
                for s in range(2):
                    chunk(2 * e + s, s, e, True)
            chunk(NI - 2, 0, NI // 2 - 1, True)
            chunk(NI - 1, 1, NI // 2 - 1, False)

            with dve.Fori(0, TT // 2) as e:
                for s in range(2):
                    tile = 2 * e + s
                    dve.wait_ge(s_xf[s], 16 * (e + 1))
                    dve.wait_ge(s_fin[s], 16 * (e + 1))
                    for c in range(2):
                        cols = slice(c * HALF, (c + 1) * HALF)
                        dve.wait_ge(s_d, 2 * tile + c + 1)
                        dve.scalar_tensor_tensor(yf[s][:, cols], bk[2 * s + c], inv_d, xf[s][:, cols],
                                                 ALU.mult, ALU.add).then_inc(s_y5, 1)
                    norm_stats(yf[s], NLN + tile, s_y5, 2 * tile + 1 + 4)
                    norm_apply(yf[s], NLN + tile, s_n5)

        @block.gpsimd
        def _(pool):
            pool.memset(ident[:], 1.0).then_inc(s_cc, 1)
            pool.memset(mhalf, -0.5).then_inc(s_const, 1)
            pool.iota(rowid.bitcast(I32), pattern=[[0, 1]], base=0, channel_multiplier=1).then_inc(s_const, 1)
            pool.memset(ones[:], 1.0).then_inc(s_const, 1)
            pool.wait_ge(s_cc, 1)
            pool.affine_select(out=ident[:], in_=ident[:], compare_op=ALU.is_equal, fill=0.0, base=0,
                               pattern=[[-1, P]], channel_multiplier=1).then_inc(s_const, 1)
            pool.wait_ge(s_const, 4)
            pool.tensor_copy(ident_h[:], ident[:]).then_inc(s_ih, 1)
            pool.wait_ge(s_bo, 16)

            def inverse_std(k, n):
                pool.wait_ge(s_eps, k + 1)
                pool.tensor_tensor(rstd[0:n, :], ve[0:n, :], mhalf[0:n, :], ALU.pow).then_inc(s_rstd, 1)

            def add_bo(g, b):
                pool.wait_ge(s_xr[b % 2], 16 * (2 * g + b // 2 + 1))
                pool.tensor_tensor(xr[0:S, b % 2, :], xr[0:S, b % 2, :], bo_b[0:S, :], ALU.add).then_inc(s_xb, 1)

            def self_attention(g, more):
                for b in range(GB):
                    if b + 1 < GB:
                        add_bo(g, b + 1)
                    elif more:
                        add_bo(g + 1, 0)
                    inverse_std(g * GB + b, S)

            add_bo(0, 0)
            with pool.Fori(0, NG - 1) as g:
                self_attention(g, True)
            self_attention(NG - 1, False)
            pool.wait_ge(s_t, T["amx"])
            pool.partition_all_reduce(amr, amx, P, RMAX).then_inc(s_amx, 1)

            pool.wait_ge(s_wk, 48)
            pool.memset(acc_v, 0.0).then_inc(s_pv, 1)
            pool.tensor_tensor(pc, bqc, bkc, ALU.mult).then_inc(s_pv, 1)
            for k, w in enumerate((KC // 2, KC // 4, KC // 8)):
                pool.wait_ge(s_pv, k + 2)
                pool.tensor_tensor(pc[:, 0:w], pc[:, 0:w], pc[:, w:2 * w], ALU.add).then_inc(s_pv, 1)
            pool.wait_ge(s_pv, 5)

            def m_chunk(e, i):
                m = 2 * e + i
                pool.wait_ge(s_wq[i], 16 * (e + 1))
                pool.tensor_tensor(part.rearrange("p (c x) -> p c x", c=KC), wq[i],
                                   bkc.unsqueeze(2).to_broadcast([P, KC, P]), ALU.mult).then_inc(s_uc, 1)
                for k, w in enumerate((D // 2, D // 4, D // 8)):
                    pool.wait_ge(s_uc, 4 * m + k + 1)
                    to = part[:, 0:w] if w > P else acc_u[:, bass.ds(m * P, P)]
                    pool.tensor_tensor(to, part[:, 0:w], part[:, w:2 * w], ALU.add).then_inc(s_uc, 1)
                pool.wait_ge(s_uc, 4 * m + 4)
                pool.tensor_tensor(part, wk[:, bass.ds(m, 1), :].rearrange("p o d -> p (o d)"),
                                   bqc[:, bass.ds(m, 1)].to_broadcast([P, D]), ALU.mult).then_inc(s_pu, 1)
                pool.wait_ge(s_pu, 2 * m + 1)
                pool.tensor_tensor(acc_v, acc_v, part, ALU.add).then_inc(s_pu, 1)
                pool.wait_ge(s_pu, 2 * m + 2)
                pool.sem_inc(s_seen2, 1)

            with pool.Fori(0, KC // 2) as e:
                for i in range(2):
                    m_chunk(e, i)
            pool.wait_ge(s_mm, 2)
            pool.partition_all_reduce(magr, mag, P, RMAX).then_inc(s_mf, 1)

            def context_max(n):
                pool.wait_ge(s_cm, n + 1)
                pool.sem_inc(s_seen2, 1)
                pool.partition_all_reduce(cmr, cmx, P, RMAX).then_inc(s_cr, 1)

            def g_split(k, y, q):
                t = slice(q * 2 * S, (q + 1) * 2 * S)
                pool.wait_ge(s_ge, k + 1)
                pool.sem_inc(s_seen2, 1)
                pool.tensor_copy(gtp[:, 0, y, t], g_f).then_inc(s_gh, 1)
                pool.wait_ge(s_gh, k + 1)
                pool.tensor_tensor(gtp[:, 1, y, t], g_f, gtp[:, 0, y, t], ALU.subtract).then_inc(s_gl, 1)

            def cross_attention(g, more):
                for b, n, has in batches(g, more):
                    if has(2):
                        for k in range(4):
                            g_split(KC + 4 * n + k, 4 * (b % 2) + k, 1 - b // 2)
                            if k == 0:
                                context_max(n + 2)
                    inverse_std(NB + n, S)

            context_max(0)
            for y in range(KC):
                g_split(y, y, 0)
            context_max(1)
            cross_attention(0, True)
            with pool.Fori(1, NG - 1) as g:
                cross_attention(g, True)
            cross_attention(NG - 1, False)

            def low_part(q, dst, kind):
                pool.wait_ge(s_wh, q + 1)
                src = wbuf[kind]
                if kind < 2:
                    src = src.rearrange("p (j n) -> p j n", j=8)
                pool.tensor_tensor(dst[1], src, dst[0], ALU.subtract).then_inc(s_wl, 1)

            for m in range(2):
                low_part(m, [wgu[0][m][:, l, :, :] for l in range(2)], m)

            def chunk(i, s, more):
                if more:
                    for m in range(2):
                        low_part(3 * i + 2 + m, [wgu[1 - s][m][:, l, :, :] for l in range(2)], m)
                low_part(down_no(i) if more else NGATHER - 1, wd_parts(i), 2)

            with pool.Fori(0, NI // 2 - 1) as e:
                for s in range(2):
                    chunk(2 * e + s, s, True)
            chunk(NI - 2, 0, True)
            chunk(NI - 1, 1, False)
            with pool.Fori(NLN, NLN + TT) as k:
                inverse_std(k, P)

        @block.scalar
        def _(act):
            act.sem_inc(s_me, 2)

            def transposed_rows(g, chunks):
                for c in chunks:
                    act.wait_ge(s_xt, KC * g + c + 1)
                    act.activation(xt[:, c, :], bk[0][:, 0:TG], ACT.Identity).then_inc(s_xta, 1)

            def self_attention(g, more):
                for f in range(2 * HC):
                    act.wait_ge(s_qk, 2 * HC * g + f + 1)
                    act.activation(qkt[:, f, :], bk[2 + f % 2][:, 0:TG], ACT.Identity,
                                   bias=bqk[:, f:f + 1]).then_inc(s_qke, 1)
                act.wait_ge(s_nm, g + 1)
                for b in range(GB):
                    act.activation(pr[0:S, b, :], bk[2][0:S, b * S:(b + 1) * S], ACT.Exp, scale=HD ** -0.5,
                                   bias=nm1[0:S, b:b + 1], accum_out=rs1[0:S, b:b + 1]).then_inc(s_exp, 1)
                if more:
                    transposed_rows(g + 1, (0, 2))
                for c in range(HC):
                    act.wait_ge(s_o, HC * g + c + 1)
                    act.activation(ot[:, c, :], bk[3 - c][:, 0:TG], ACT.Identity).then_inc(s_oe, 1)
                if more:
                    transposed_rows(g + 1, (4, 6))

            transposed_rows(0, (0, 2, 4, 6))
            act.wait_ge(s_bias, 32)
            with act.Fori(0, NG - 1) as g:
                self_attention(g, True)
            self_attention(NG - 1, False)

            wq_v = t_in["L0_xattn_Wq"].rearrange("(p c) x -> p c x", c=KC)

            def m_chunk(e, i, more):
                act.wait_ge(s_m, 2 * e + i + 1)
                if more:
                    act.wait_ge(s_uc, 4 * (2 * e + i) + 1)
                    act.dma_start(wq[i], wq_v[:, :, bass.ds((2 * e + 2 + i) * P, P)]).then_inc(s_wq[i], 16)
                act.activation(m32[:, bass.ds(2 * e + i, 1), :].rearrange("p a b -> p (a b)"),
                               psum[:, i * 1024:(i + 1) * 1024], ACT.Identity).then_inc(s_me, 1)

            with act.Fori(0, KC // 2 - 1) as e:
                for i in range(2):
                    m_chunk(e, i, True)
            for i in range(2):
                m_chunk(KC // 2 - 1, i, False)

            def x1t_hi(m, b):
                for j in range(2):
                    act.wait_ge(s_x1t, 2 * m + j + 1)
                    act.activation(xtp[:, 0, 4 * j:4 * j + 4, b * S:(b + 1) * S],
                                   bk[2 + j][:, 0:TG].rearrange("p (a t) -> p a t", a=4),
                                   ACT.Identity, scale=XS).then_inc(s_x1h, 1)

            def g_out(k, y):
                act.wait_ge(s_g, k + 1)
                if not known(k, 1):
                    act.wait_ge(s_gl, k)
                act.activation(g_f, bk[2 + y % 2][:, 0:2 * S], ACT.Identity, scale=kg,
                               bias=v2s[:, y:y + 1]).then_inc(s_ge, 1)

            def context_t(n, chunks):
                for c in chunks:
                    act.wait_ge(s_ct, KC * n + c + 1)
                    act.activation(cxt[:, :, c, :], bkh[ct_bank[c % 4]][:, :, 0:CTX], ACT.Identity).then_inc(s_cta, 1)

            def context_hi(n, b, c):
                if c == 0:
                    act.wait_ge(s_cf, 5 * n + 5)
                act.activation(cxp[b % 2][0:CP[c], 0, c, :], cx[0:CP[c], c, :], ACT.Identity,
                               scale=fc[0:CP[c], b:b + 1]).then_inc(s_ch, 1)

            def x2t_hi(n):
                for j in range(2):
                    act.wait_ge(s_x2t, 2 * n + j + 1)
                    act.activation(x2t[:, 0, 4 * j:4 * j + 4, bass.ds(n * S, S)],
                                   bk[j][:, 0:TG].rearrange("p (a t) -> p a t", a=4),
                                   ACT.Identity, scale=XS).then_inc(s_hi, 1)

            def probs_hi(n):
                act.wait_ge(s_pt3, n + 1)
                for c in range(CC):
                    ins = act.activation(pt3[0:CP[c], 0, c, :], bk[4][0:CP[c], c * P:c * P + S], ACT.Identity, scale=XS)
                ins.then_inc(s_ph, 1)

            def cross_attention(g, more):
                for b, n, has in batches(g, more):
                    if has(1):
                        context_t(n + 1, CT_ACT[:4])
                    act.wait_ge(s_lm, n + 1)
                    act.activation(sp_[0:S, 0:CTX], sp_[0:S, 0:CTX], ACT.Exp, bias=nm3[0:S, :],
                                   accum_out=rs3[0:S, b:b + 1]).then_inc(s_ex3, 1)
                    if has(1):
                        context_t(n + 1, CT_ACT[4:])
                    if has(2):
                        for k in range(2):
                            g_out(KC + 4 * n + k, 4 * (b % 2) + k)
                    probs_hi(n)
                    if has(2):
                        g_out(KC + 4 * n + 2, 4 * (b % 2) + 2)
                        act.wait_ge(s_at, 2 * n + 2)
                        context_hi(n + 2, (b + 2) % GB, 0)
                        g_out(KC + 4 * n + 3, 4 * (b % 2) + 3)
                        for c in range(1, CC):
                            context_hi(n + 2, (b + 2) % GB, c)
                    if not known(n, 1):
                        x2t_hi(n - 1)
                    if more:
                        x1t_hi(n + GB, b)

            act.wait_ge(s_v2, 1)
            act.activation(v2, bk[6][:, 0:KC], ACT.Identity)
            act.activation(c0[0:S, :], bk[6][0:S, KC:KC + 1], ACT.Identity).then_inc(s_v2e, 1)
            x1t_hi(0, 0)
            x1t_hi(1, 1)
            for c in range(CC):
                context_hi(0, 0, c)
            x1t_hi(2, 2)
            x1t_hi(3, 3)
            act.wait_ge(s_fs, T["fm"])
            act.wait_ge(s_me, KC + 2)
            for c in reversed(range(KC)):
                if c < KC - 1:
                    act.wait_ge(s_ml, KC - 1 - c)
                act.activation(mp[:, c, 0, :], m32[:, c, :], ACT.Identity, scale=fm).then_inc(s_mh, 1)
                context_t(0, [a for a in CT_ACT if a == KC - 1 - c])
            act.wait_ge(s_fs, T["g"])
            act.wait_ge(s_stash, 16)
            for y in range(KC):
                g_out(y, y)
            act.wait_ge(s_t, T["tab2"])
            for c in range(CC):
                context_hi(1, 1, c)
            cross_attention(0, True)
            with act.Fori(1, NG - 1) as g:
                cross_attention(g, True)
            cross_attention(NG - 1, False)
            x2t_hi(NB - 1)

            def high_part(q, dst, kind):
                act.wait_ge(s_wf, q + 1)
                src = wbuf[kind]
                if kind < 2:
                    src = src.rearrange("p (j n) -> p j n", j=8)
                act.activation(dst, src, ACT.Identity).then_inc(s_wh, 1)

            def hidden(i, t):
                act.wait_ge(s_gp, 4 * i + t + 1)
                act.wait_ge(s_hf, 4 * i + t + 2)
                act.activation(g_act, bk[t % 2][:, 0:TG], ACT.Silu, scale=inv_g).then_inc(s_si, 1)
                if t % 2 == 0:
                    act.wait_ge(s_ho[t // 2], 32 * (i + 1))
                act.wait_ge(s_hf, 4 * i + t + 3)
                act.activation(h_st[:, 0, t * TG:(t + 1) * TG], h_f, ACT.Identity).then_inc(s_hh, 1)

            def chunk(i, s, more):
                hidden(i, 0)
                if more:
                    high_part(3 * i + 2, wgu[1 - s][0][:, 0, :, :], 0)
                hidden(i, 1)
                if more:
                    high_part(3 * i + 3, wgu[1 - s][1][:, 0, :, :], 1)
                hidden(i, 2)
                high_part(down_no(i) if more else NGATHER - 1, wd_parts(i)[0], 2)
                hidden(i, 3)

            for m in range(2):
                high_part(m, wgu[0][m][:, 0, :, :], m)
            with act.Fori(0, NI // 2 - 1) as e:
                for s in range(2):
                    chunk(2 * e + s, s, True)
            chunk(NI - 2, 0, True)
            chunk(NI - 1, 1, False)

        @block.tensor
        def _(pe):
            def transposed_rows(g, chunks):
                for c in chunks:
                    if c == 0:
                        for b in range(GB):
                            pe.wait_ge(s_xs[b], 16 * (g + 1))
                    if c >= 2:
                        pe.wait_ge(s_xtd if c % 2 else s_xta, KC // 2 * g + c // 2)
                    for b in range(GB):
                        mm = pe.transpose(bk[c % 2][:, b * S:(b + 1) * S], xs[0:S, b, c::KC], ident[0:S, 0:S])
                    mm.then_inc(s_xt, 1)

            def product(out, pairs, last=None):
                for k, (a, r) in enumerate(pairs):
                    mm = pe.matmul(out, a, r, start=(k == 0), stop=(k == len(pairs) - 1))
                return mm

            pe.wait_ge(s_const, 4)
            def self_attention(g, more):
                pe.wait_ge(s_xta, KC // 2 * (g + 1))
                pe.wait_ge(s_xtd, KC // 2 * (g + 1))
                for f in range(2 * HC):
                    if f >= 2:
                        pe.wait_ge(s_qke, 2 * HC * g + f - 1)
                    product(bk[2 + f % 2][:, 0:TG], [(wqkv[:, c, f * P:(f + 1) * P], xt[:, c, :])
                                                     for c in range(KC)]).then_inc(s_qk, 1)
                def v_rows(b):
                    t = slice(b * S, (b + 1) * S)
                    return product(bk[4 + b // 2][0:S, (b % 2) * HD:(b % 2 + 1) * HD],
                                   [(xt[:, c, t], wqkv[:, c, 2 * HD:3 * HD]) for c in range(KC)])

                v_rows(0)
                pe.wait_ge(s_qke, 2 * HC * (g + 1))
                for b in range(GB):
                    t = slice(b * S, (b + 1) * S)
                    mm = product(bk[2][0:S, t], [(qkt[:, c, t], qkt[:, HC + c, t]) for c in range(HC)])
                mm.then_inc(s_s, 1)
                for b in range(1, GB):
                    mm = v_rows(b)
                    if b % 2:
                        mm.then_inc(s_v, 1)
                pe.wait_ge(s_p, g + 1)
                pe.wait_ge(s_ve, 2 * g + 1)
                for b in range(GB):
                    mm = pe.transpose(bk[4][0:S, b * S:(b + 1) * S], pr[0:S, b, :], ident[0:S, 0:S])
                mm.then_inc(s_pt, 1)
                if more:
                    transposed_rows(g + 1, range(4))
                pe.wait_ge(s_pte, g + 1)
                pe.wait_ge(s_ve, 2 * (g + 1))
                for c in range(HC):
                    for b in range(GB):
                        mm = product(bk[3 - c][:, b * S:(b + 1) * S],
                                     [(v_sb[0:S, b, c * P:(c + 1) * P], pt[0:S, b, :])])
                    mm.then_inc(s_o, 1)
                if more:
                    transposed_rows(g + 1, range(4, KC))
                pe.wait_ge(s_oe, HC * (g + 1))
                for b in range(GB):
                    for h in range(2):
                        if b > 0:
                            pe.wait_ge(s_y, 2 * (g * GB + b - 1) + h + 1)
                        product(bk[6 + h][0:S, :], [(ot[:, c, b * S:(b + 1) * S], wo[:, c, h * HALF:(h + 1) * HALF])
                                                    for c in range(HC)]).then_inc(s_w, 1)

            transposed_rows(0, range(KC))
            pe.wait_ge(s_w1, 32)
            with pe.Fori(0, NG - 1) as g:
                self_attention(g, True)
            self_attention(NG - 1, False)

            pe.wait_ge(s_wk, 48)
            with pe.Fori(0, KC // 2) as e:
                for i in range(2):
                    pe.wait_ge(s_wq[i], 16 * (e + 1))
                    pe.wait_ge(s_me, 2 * e + i + 1)
                    for h in range(2):
                        mm = product(bk[2 * i + h], [(wq[i][:, c, :], wk[:, c, h * HALF:(h + 1) * HALF])
                                                     for c in range(KC)])
                    mm.then_inc(s_m, 1)
            pe.wait_ge(s_pv, 5)
            pe.wait_ge(s_pu, 2 * KC)
            for y in range(KC):
                pe.matmul(bk[6][:, y:y + 1], acc_v[:, y * P:(y + 1) * P], ones[:], start=True, stop=True)
            pe.matmul(bk[6][0:S, KC:KC + 1], pc[:, 0:1].to_broadcast([P, S]), ones[:], start=True, stop=True).then_inc(s_v2, 1)
            pe.wait_ge(s_uc, 4 * KC)
            for h in range(2):
                mm = pe.matmul(psum[0:S, 2048 + h * HALF:2048 + (h + 1) * HALF], ones[:].to_broadcast([P, S]),
                               acc_u[:, h * HALF:(h + 1) * HALF], start=True, stop=True)
            mm.then_inc(s_ub, 1)

            def x1_transposed(m, b):
                pe.wait_ge(s_xs3[b % 2], 8 * (m - b % 2) + 16)
                for j in range(2):
                    for a in range(4):
                        mm = pe.transpose(bk[2 + j][:, a * S:(a + 1) * S],
                                          xs3[0:S, b % 2, (4 * j + a) * P:(4 * j + a + 1) * P], ident[0:S, 0:S])
                    mm.then_inc(s_x1t, 1)

            def g_chunk(y, q):
                product(bk[2 + y % 2][:, 0:2 * S],
                        [(mp[:, c, w, y * P:(y + 1) * P], xtp[:, a, c, q * 2 * S:(q + 1) * 2 * S])
                         for c in range(KC) for w, a in PASSES]).then_inc(s_g, 1)

            def context_t(n, b):
                pe.wait_ge(s_cl, CC * (n + 1))
                for c in range(KC):
                    if c == 2 and known(n, 1):
                        pe.wait_ge(s_v2e, 1)
                    elif c == 2 and not known(n, 2):
                        pe.wait_ge(s_y3, 2 * (n - 1))
                    if c == 0 and not known(n, 2):
                        pe.wait_ge(s_lo, 2 * (n - 1) - 1)
                    if c in (4, 5, 6, 7):
                        if c - 4 in CT_ACT:
                            pe.wait_ge(s_cta, NA * n + CT_ACT.index(c - 4) + 1)
                        else:
                            pe.wait_ge(s_ctd, ND * n + CT_DVE.index(c - 4) + 1)
                    for l in range(2):
                        for r in range(CC):
                            mm = pe.transpose(bkh[ct_bank[c % 4]][:, l, r * P:r * P + CP[r]],
                                              cxp[b % 2][0:CP[r], l, r, c * P:(c + 1) * P], ident_h[0:CP[r], 0:CP[r]])
                    mm.then_inc(s_ct, 1)

            def context_t_out(n):
                pe.wait_ge(s_cta, NA * (n + 1))
                pe.wait_ge(s_ctd, ND * (n + 1))

            def logits(n, b):
                if b % 2 == 0:
                    pe.wait_ge(s_gl, KC + 4 * n)
                product(bk[5][0:S, 0:CTX], [(gtp[:, w, c, b * S:(b + 1) * S], cxt[:, a, c, :])
                                            for c in range(KC) for w, a in PASSES]).then_inc(s_l, 1)

            def probs_t(n):
                pe.wait_ge(s_ex3, n + 1)
                for r in range(CC):
                    mm = pe.transpose(bk[4][0:CP[r], r * P:r * P + S], sp_[0:S, r * P:r * P + CP[r]],
                                      ident[0:S, 0:S])
                mm.then_inc(s_pt3, 1)

            def attended(n, b):
                pe.wait_ge(s_pl, n + 1)
                for h in range(2):
                    product(bk[6 + h][0:S, :], [(pt3[0:CP[r], w, r, :], cxp[b % 2][0:CP[r], a, r, h * HALF:(h + 1) * HALF])
                                                for r in range(CC) for w, a in PASSES]).then_inc(s_at, 1)

            def x2_transposed(n, b):
                pe.wait_ge(s_n, NB + n + 1)
                for j in range(2):
                    for a in range(4):
                        mm = pe.transpose(bk[j][:, a * S:(a + 1) * S], yo[0:S, b % 2, 4 * j + a::KC],
                                          ident[0:S, 0:S])
                    mm.then_inc(s_x2t, 1)

            def cross_attention(g, more):
                for b, n, has in batches(g, more):
                    if known(n, 1):
                        context_t_out(0)
                    logits(n, b)
                    if has(1):
                        context_t(n + 1, (b + 1) % GB)
                    if has(2):
                        pe.wait_ge(s_x1l, 2 * (n + GB) if more else 2 * NB)
                        for k in range(2):
                            g_chunk(4 * (b % 2) + k, 1 - b // 2)
                    probs_t(n)
                    if has(2):
                        pe.wait_ge(s_ge, KC + 4 * n + 1)
                        g_chunk(4 * (b % 2) + 2, 1 - b // 2)
                    if has(1):
                        context_t_out(n + 1)
                    attended(n, b)
                    if has(2):
                        pe.wait_ge(s_ge, KC + 4 * n + 2)
                        g_chunk(4 * (b % 2) + 3, 1 - b // 2)
                    if not known(n, 1):
                        if not known(n, 2):
                            pe.wait_ge(s_lo, 2 * (n - 1) + 1)
                        x2_transposed(n - 1, (b + 1) % 2)
                    if more:
                        pe.wait_ge(s_ge, KC + 4 * n + 4)
                        x1_transposed(n + GB, b)

            pe.wait_ge(s_me, KC + 2)
            for b in range(GB):
                if b > 0:
                    pe.wait_ge(s_x1l, 2 * b)
                x1_transposed(b, b)
            pe.wait_ge(s_ih, 1)
            context_t(0, 0)
            pe.wait_ge(s_ml, KC)
            pe.wait_ge(s_x1l, 2 * GB)
            for y in range(KC):
                if y >= 2:
                    pe.wait_ge(s_ge, y - 1)
                g_chunk(y, 0)
            pe.wait_ge(s_ube, 1)
            cross_attention(0, True)
            with pe.Fori(1, NG - 1) as g:
                cross_attention(g, True)
            cross_attention(NG - 1, False)
            pe.wait_ge(s_lo, 2 * (NB - 1) + 1)
            x2_transposed(NB - 1, 1)

            def gather(q, parts):
                if not isinstance(q, int) or q > 0:
                    pe.wait_ge(s_wf, q)
                for base, pieces in ((2048, parts[0]), (3072, parts[1])):
                    for k, (a, r) in enumerate(pieces):
                        w = 1024 // len(pieces)
                        mm = pe.matmul(psum[:, base + k * w:base + (k + 1) * w], a, r, start=True, stop=True)
                mm.then_inc(s_ga, 1)

            def gather_gu(q, m, s, e):
                pe.wait_ge(s_tc[s], 16 * (e + 1))
                gather(q, [[(sel[m][:, j, :], tabc[s][:, m, :]) for j in range(8)] for sel in (sel_s, sel_z)])

            def gather_down(q, i):
                pe.wait_ge(s_unstash, 16)
                one = sel_d[:, i, :] if isinstance(i, int) else \
                    sel_d[:, bass.ds(i, 1), :].rearrange("p a b -> p (a b)")
                gather(q, [[(one, t[:, h * HALF:(h + 1) * HALF]) for h in range(2)] for t in (tab_ds, tab_dz)])

            def chunk(i, s, e, more):
                pe.wait_ge(s_wl, 3 * i + 1)
                for t in range(4):
                    cols = slice(t * TG, (t + 1) * TG)
                    pe.wait_ge(s_hf, 4 * i + t + 1)
                    for m, done in ((0, s_gp), (1, s_up)):
                        product(bk[2 * m + t % 2][:, 0:TG],
                                [(wgu[s][m][:, w, c, :], x2t[:, a, c, cols])
                                 for c in range(KC) for w, a in PASSES]).then_inc(done, 1)
                    if t == 0 and more:
                        gather_gu(3 * i + 2, 0, 1 - s, e + s)
                    if t == 1 and more:
                        gather_gu(3 * i + 3, 1, 1 - s, e + s)
                    if t == 2:
                        gather_down(down_no(i) if more else NGATHER - 1, i)

            pe.wait_ge(s_y3, 2 * NB)
            pe.wait_ge(s_lo, 2 * NB + 1)
            for m in range(2):
                gather_gu(m, m, 0, 0)
            pe.wait_ge(s_wl, 2)
            with pe.Fori(0, NI // 2 - 1) as e:
                for s in range(2):
                    chunk(2 * e + s, s, e, True)
            chunk(NI - 2, 0, NI // 2 - 1, True)
            chunk(NI - 1, 1, NI // 2 - 1, False)

            pe.wait_ge(s_hf, 4 * NI + 2)
            pe.wait_ge(s_wl, NGATHER)
            with pe.Fori(0, TT // 2) as e:
                for s in range(2):
                    tile = 2 * e + s
                    pe.wait_ge(s_ht[s], 16 * (e + 1))
                    for c in range(2):
                        pe.wait_ge(s_y5, 2 * tile + c + 1)
                        product(bk[2 * s + c], [(ht[s][:, i, a, :], wd[:, i, w, c * HALF:(c + 1) * HALF])
                                                for i in range(NI) for w, a in PASSES]).then_inc(s_d, 1)

        @block.sync
        def _(sp):
            wqkv_v = t_in["L0_attn_Wqkv"].rearrange("(p c) f -> p c f", c=KC)
            for b in range(GB):
                sp.dma_start(xs[0:S, b, :], rows(x_rows, b)).then_inc(s_xs[b], 16)
            sp.dma_start(wqkv, wqkv_v).then_inc(s_w1, 16)
            with nc.allow_non_contiguous_dma(reason="short bias columns"):
                sp.dma_start(bqk, t_in["L0_attn_bqkv"][0:2 * HD].rearrange("(c p) -> p c", p=P)).then_inc(s_bias, 16)
            sp.dma_start(vb_b, t_in["L0_attn_bqkv"][2 * HD:3 * HD].partition_broadcast(P)).then_inc(s_bias, 16)
            sp.dma_start(wo, t_in["L0_attn_Wo"].rearrange("(c p) n -> p c n", p=P)).then_inc(s_w1, 16)
            sp.dma_start(bo_b, t_in["L0_attn_bo"].partition_broadcast(P)).then_inc(s_bo, 16)
            for n in range(2):
                sp.dma_start(xr[0:S, n, :], rows(x_rows, n)).then_inc(s_xr[n], 16)
            sp.dma_start(bqc, t_in["L0_xattn_bq"].rearrange("(p c) -> p c", c=KC)).then_inc(s_wk, 16)
            sp.dma_start(bkc, t_in["L0_xattn_bk"].rearrange("(p c) -> p c", c=KC)).then_inc(s_wk, 16)
            sp.dma_start(wk, t_in["L0_xattn_Wk"].rearrange("(p c) y -> p c y", c=KC)).then_inc(s_wk, 16)
            wq_v = t_in["L0_xattn_Wq"].rearrange("(p c) x -> p c x", c=KC)
            for i in range(2):
                sp.dma_start(wq[i], wq_v[:, :, i * P:(i + 1) * P]).then_inc(s_wq[i], 16)

            def load_group(g):
                sp.wait_ge(s_xt, KC * g)
                for b in range(GB):
                    sp.dma_start(xs[0:S, b, :], rows(x_rows, g * GB + b)).then_inc(s_xs[b], 16)

            def self_attention(g, rows_next, more):
                if rows_next:
                    load_group(g + 2)
                for b in range(GB):
                    if more or b + 2 < GB:
                        sp.wait_ge(s_y, 2 * (g * GB + b + 1))
                        sp.dma_start(xr[0:S, b % 2, :], rows(x_rows, g * GB + b + 2)).then_inc(s_xr[b % 2], 16)
                    sp.wait_ge(s_n, g * GB + b + 1)
                    sp.dma_start(rows(x1_d, g * GB + b), yo[0:S, b % 2, :]).then_inc(s_yout[b % 2], 16)

            load_group(1)
            with sp.Fori(0, NG - 2) as g:
                self_attention(g, True, True)
            self_attention(NG - 2, False, True)
            self_attention(NG - 1, False, False)

            for i in range(2):
                sp.wait_ge(s_yout[i], 16 * (NB // 2 + 1))

            def load_rows(m, b):
                sp.dma_start(xs3[0:S, b % 2, :], rows(x1_d, m)).then_inc(s_xs3[b % 2], 16)

            def load_residual(n, b):
                sp.dma_start(xr3[0:S, b % 2, :], rows(x1_d, n)).then_inc(s_xr3[b % 2], 16)

            ctx_rows = ctx_d.rearrange("b s d -> (b s) d")

            def load_ctx(n):
                base = n * CTX
                last = (CC - 1) * P
                even = CP[-1] // 16 * 16
                for c in range(CC - 1):
                    sp.dma_start(cx[:, c, :], ctx_rows[bass.ds(base + c * P, P), :]).then_inc(s_cx, 16)
                sp.dma_start(cx[0:even, CC - 1, :],
                             ctx_rows[bass.ds(base + last, even), :]).then_inc(s_cx, 16)
                sp.dma_start(cx[even:CP[-1], CC - 1, :],
                             ctx_rows[bass.ds(base + last + even, CP[-1] - even), :]).then_inc(s_cx, 16)

            for m in range(2):
                load_rows(m, m)

            for m, name in enumerate(("gate", "up", "down")):
                sp.dma_start(s_flat[m], t_in[f"L0_ffn_{name}_scales"].rearrange("g n -> (g n)").rearrange(
                    "(p c) -> p c", p=P)).then_inc(s_tin[0], 16)
            for m, name in enumerate(("gate", "up", "down")):
                if m > 0:
                    sp.wait_ge(s_t, T[f"idx{m - 1}"])
                idx = t_in[f"L0_ffn_{name}_g_idx"]
                sp.dma_start(tmp_i[:, 0:idx.shape[0]], idx.partition_broadcast(P)).then_inc(s_tin[1], 16)
            load_ctx(0)
            for m, name in enumerate(("gate", "up", "down")):
                sp.wait_ge(s_t, T[f"tab{m - 1}"] if m else T["idx2"])
                scales, zeros = t_in[f"L0_ffn_{name}_scales"], t_in[f"L0_ffn_{name}_qzeros"]
                groups = scales.shape[0]
                sp.dma_start(tmp[0:groups, 0:scales.shape[1]], scales).then_inc(s_tin[2], 16)
                sp.dma_start(qz[96:96 + groups, 0:zeros.shape[1]], zeros.bitcast(U32)).then_inc(s_tin[3], 16)
                if m in (1, 2):
                    sp.dma_start(tab_d[:, :, m - 1, :].rearrange("i p c -> p i c"),
                                 tab.rearrange("p (i c) -> p i c", c=P)).then_inc(s_tabo, 16)
            sp.wait_ge(s_t, T["tab2"])
            sp.dma_start(down_d, down_tabs).then_inc(s_stash, 16)
            for m in range(2, 4):
                sp.wait_ge(s_x1t, 2 * m - 2)
                load_rows(m, m % 2)
            sp.wait_ge(s_stash, 16)
            for n in range(2):
                load_residual(n, n)
            sp.wait_ge(s_cl, CC)
            load_ctx(1)
            for m in range(4, 6):
                sp.wait_ge(s_x1t, 2 * m - 2)
                load_rows(m, m % 2)
            sp.wait_ge(s_cl, 2 * CC)
            load_ctx(2)

            def cross_attention(g, loop):
                for b in range(GB):
                    n = g * GB + b
                    if loop or n + 2 < NB:
                        sp.wait_ge(s_y3, 2 * (n + 1))
                        load_residual(n + 2, (b + 2) % GB)
                    if loop or n + 3 < NB:
                        sp.wait_ge(s_cl, CC * (n + 3))
                        load_ctx(n + 3)
                    if loop or n + 6 < NB:
                        sp.wait_ge(s_x1t, 2 * n + 10)
                        load_rows(n + 6, (b + 2) % GB)
                    sp.wait_ge(s_n, NB + n + 1)
                    sp.dma_start(rows(x2_d, n), yo[0:S, b % 2, :]).then_inc(s_yout[b % 2], 16)

            with sp.Fori(0, NG - 2) as g:
                cross_attention(g, True)
            cross_attention(NG - 2, False)
            cross_attention(NG - 1, False)

            def load_chunk(i, s, w):
                for m, name in enumerate(("gate", "up")):
                    sp.dma_start(qw[s][m][:, 0:w], t_in[f"L0_ffn_{name}_qweight"][:, bass.ds(i * P, w)].bitcast(
                        U32)).then_inc(s_qw[s], 16)
                sp.dma_start(tabc[s], tab_d[bass.ds(i, 1)].rearrange("o p m c -> p (o m) c")).then_inc(s_tc[s], 16)

            def load_down(i, w):
                rows8 = t_in["L0_ffn_down_qweight"][bass.ds(i * (P // 8), w // 8), :]
                sp.dma_start(wbuf[2].bitcast(I32)[0:w, :], rows8.unsqueeze(1).to_broadcast([w // 8, 8, D])).then_inc(s_qd, 16)

            def chunk(i, s, w_down, w_next):
                sp.wait_ge(s_wf, 3 * i + 2)
                sp.wait_ge(s_wh, 3 * i + 2)
                sp.wait_ge(s_wl, 3 * i + 2)
                load_down(i, w_down)
                if w_next:
                    load_chunk(i + 2, s, w_next)
                for u in range(2):
                    sp.wait_ge(s_hh, 4 * i + 2 * u + 3)
                    sp.wait_ge(s_hl, 4 * i + 2 * u + 3)
                    half = slice(u * TT // 2, (u + 1) * TT // 2)
                    for l in range(2):
                        sp.dma_start(h_d[half, :, bass.ds(i, 1), l, :].rearrange("t p o c -> p t (o c)"),
                                     h_st[:, l, u * NT // 2:(u + 1) * NT // 2].rearrange("p (t c) -> p t c", c=P)
                                     ).then_inc(s_ho[u], 16)

            sp.dma_start(down_tabs, down_d).then_inc(s_unstash, 16)
            sp.wait_ge(s_lo, 2 * NB + 1)
            for i in range(2):
                sp.wait_ge(s_yout[i], 16 * (NB + 1))
            load_chunk(0, 0, P)
            load_chunk(1, 1, P)
            with sp.Fori(0, NI // 2 - 2) as e:
                for s in range(2):
                    chunk(2 * e + s, s, P, P)
            chunk(NI - 4, 0, P, P)
            chunk(NI - 3, 1, P, LASTC)
            chunk(NI - 2, 0, P, 0)
            chunk(NI - 1, 1, LASTC, 0)

            sp.wait_ge(s_up, 4 * NI)
            sp.wait_ge(s_wl, NGATHER)
            sp.wait_ge(s_wh, NGATHER)
            for u in range(2):
                sp.wait_ge(s_ho[u], 32 * (NI + 1))

            def load_tile(tile, s):
                sp.dma_start(ht[s].rearrange("p i l c -> p (i l c)"),
                             h_d[bass.ds(tile, 1)].rearrange("o p i l c -> p (o i l c)")).then_inc(s_ht[s], 16)

            def load_x2(tile, s):
                sp.dma_start(xf[s], x2_d[bass.ds(tile * P, P), :]).then_inc(s_xf[s], 16)

            out_rows = out.rearrange("b s d -> (b s) d")
            for s in range(2):
                load_tile(s, s)
            for s in range(2):
                load_x2(s, s)

            def down_tile(tile, s, more):
                if more:
                    sp.wait_ge(s_d, 2 * tile + 2)
                    load_tile(tile + 2, s)
                    sp.wait_ge(s_y5, 2 * tile + 2 + 4)
                    load_x2(tile + 2, s)
                sp.wait_ge(s_n5, tile + 1)
                sp.dma_start(out_rows[bass.ds(tile * P, P), :], yf[s]).then_inc(s_fin[s], 16)

            with sp.Fori(0, TT // 2 - 1) as e:
                for s in range(2):
                    down_tile(2 * e + s, s, True)
            for s in range(2):
                down_tile(TT - 2 + s, s, False)
            for s in range(2):
                sp.wait_ge(s_fin[s], 16 * (TT // 2 + 1))


_INS = ["x", "ctx_4096", "L0_attn_Wqkv", "L0_attn_bqkv", "L0_attn_Wo", "L0_attn_bo",
        "L0_xattn_Wq", "L0_xattn_bq", "L0_xattn_Wk", "L0_xattn_bk"] + [
    f"L0_ffn_{m}_{p}" for m in ("gate", "up", "down") for p in ("qweight", "scales", "qzeros", "g_idx")]


def kernel(**inputs):
    import numpy as _np
    import concourse.bacc as _bacc
    from concourse import mybir as _mybir
    from concourse.bass_utils import run_bass_kernel_spmd as _run

    nc = _bacc.Bacc("TRN2", target_bir_lowering=False, num_devices=1)
    arrays, t_in = {}, {}
    for name in _INS:
        a = _np.ascontiguousarray(inputs[name])
        arrays[f"in_{name}"] = a
        t_in[name] = nc.dram_tensor(f"in_{name}", a.shape, _mybir.dt.from_np(a.dtype), kind="ExternalInput").ap()
    out = nc.dram_tensor("out_0", inputs["x"].shape, _mybir.dt.float32, kind="ExternalOutput").ap()
    decoder_layer(nc, t_in, out)
    r = _run(nc, [arrays], core_ids=[0])
    return r.results[0]["out_0"]
```

```python
from contextlib import ExitStack

import numpy as np

import concourse.bass as bass
from concourse import mybir

F32 = mybir.dt.float32
F16 = mybir.dt.float16
BF16 = mybir.dt.bfloat16
I32 = mybir.dt.int32
U32 = mybir.dt.uint32
ALU = mybir.AluOpType
ACT = mybir.ActivationFunctionType
AX = mybir.AxisListType
RMAX = bass.bass_isa.ReduceOp.max

P = 128
EPS = 1e-5
PASSES = ((0, 0), (0, 1), (1, 0))


def decoder_layer(nc, t_in, out):
    x_d, ctx_d = t_in["x"], t_in["ctx_4096"]
    NB, S, D = x_d.shape
    CTX = ctx_d.shape[1]
    HD = t_in["L0_attn_Wo"].shape[0]
    FF = t_in["L0_ffn_gate_qweight"].shape[1]
    GU = t_in["L0_ffn_gate_scales"].shape[0]
    GD = t_in["L0_ffn_down_scales"].shape[0]
    KC = D // P
    HC = HD // P
    GB = 4
    NG = NB // GB
    TG = GB * S
    NT = NB * S
    NI = -(-FF // P)
    FP = NI * P
    LASTC = FF - (NI - 1) * P
    TT = NT // P
    HALF = 512
    CP = [min(P, CTX - c * P) for c in range(-(-CTX // P))]
    CC = len(CP)
    XS = 1024.0
    assert NB % GB == 0 and TG <= 512 and D == 2 * HALF and NI % 2 == 0 and TT % 2 == 0 and KC == 8 and LASTC == P // 2

    x1_d = nc.dram_tensor("x1_scratch", (NT, D), F32).ap()
    x2_d = nc.dram_tensor("x2_scratch", (NT, D), F32).ap()
    h_d = nc.dram_tensor("h_scratch", (TT, P, NI, 2, P), F16).ap()
    down_d = nc.dram_tensor("down_table_scratch", (P, NI * P + 2 * D), BF16).ap()
    tab_d = nc.dram_tensor("table_scratch", (NI, P, 2, P), BF16).ap()

    with ExitStack() as ctx:
        def sem(name):
            return ctx.enter_context(nc.semaphore(name))

        def sb(name, shape, dt):
            return ctx.enter_context(nc.sbuf_tensor(name, shape, dt))

        ARENA = 203 * 1024
        arena = sb("arena", [P, ARENA // 4], F32)

        def carve(byte, shape, dt):
            size = {F32: 4, I32: 4, U32: 4, F16: 2, BF16: 2}[dt]
            n = int(np.prod(shape)) * size
            assert byte % 4 == 0 and n % 4 == 0 and byte + n <= ARENA, (byte, n)
            v = arena[:, byte // 4:(byte + n) // 4]
            if dt is not F32:
                v = v.bitcast(dt)
            if len(shape) == 2:
                v = v.rearrange("p (a b) -> p a b", b=shape[1])
            elif len(shape) == 3:
                v = v.rearrange("p (a b c) -> p a b c", b=shape[1], c=shape[2])
            elif len(shape) == 4:
                v = v.rearrange("p (a b c d) -> p a b c d", b=shape[1], c=shape[2], d=shape[3])
            return v

        at_x2t = 0
        at_tab = at_x2t + KC * NT * 4
        at_rest = at_tab + 4 * 2 * D + 2 * FP + 2 * 2 * D
        at_xs = at_rest
        at_xt = at_xs + 2 * D * 4
        at_yo = at_xt + KC * TG * 4
        at_gt = at_yo + 2 * D * 4
        at_m = at_gt + KC * TG * 4
        at_ctx = at_m + KC * D * 4
        at_ctxt = at_ctx + 3 * CC * D * 4
        at_pt3 = at_ctxt + KC * CTX * 4
        at_ub = at_pt3 + CC * S * 4

        x2t = carve(at_x2t, [2, KC, NT], F16)
        wk = carve(at_x2t, [KC, D], F32)
        wq = [carve(at_x2t + KC * D * 4 + i * KC * P * 4, [KC, P], F32) for i in range(2)]
        sel_s = [carve(at_tab + m * 2 * D, [KC, P], BF16) for m in range(2)]
        sel_z = [carve(at_tab + (2 + m) * 2 * D, [KC, P], BF16) for m in range(2)]
        n_down = FP + 2 * D
        down_tabs = carve(at_tab + 8 * D, [n_down], BF16)
        sel_d = carve(at_tab + 8 * D, [NI, P], BF16)
        tab_ds = carve(at_tab + 8 * D + 2 * FP, [D], BF16)
        tab_dz = carve(at_tab + 8 * D + 2 * FP + 2 * D, [D], BF16)
        xr3 = carve(at_tab + 8 * D, [2, D], F32)
        g_f = carve(at_tab + 16 * D, [2 * S], F32)
        assert 8 * D + 8 * S <= 2 * n_down

        yo = carve(at_yo, [2, D], F32)
        xtp = carve(at_xt, [2, KC, TG], F16)
        gtp = carve(at_gt, [2, KC, TG], F16)
        acc_u = carve(at_ctxt, [D], F32)
        part = carve(at_ctxt + 4 * D, [D], F32)
        acc_v = carve(at_ub, [D], F32)
        qkt = carve(at_gt, [2 * HC, TG], F32)
        pr = carve(at_gt + 2 * HC * TG * 4, [GB, S], F32)
        pt = carve(at_gt + (2 * HC + 1) * TG * 4, [GB, S], F32)
        otp = carve(at_gt + (2 * HC + 2) * TG * 4, [2, HC, TG], F16)
        m32 = carve(at_m - 8 * D, [KC, D], F32)
        mp = carve(at_m, [KC, 2, D], F16)
        wqkv = carve(at_m - 2 * 3 * HD * 4, [KC, 3 * HD], F32)
        wqp = carve(at_m, [KC, 2, 3 * HD], F16)
        wo = carve(at_xs, [HC, D], F32)
        wop = carve(at_m + KC * 3 * HD * 4, [HC, 2, D], F16)
        xs = carve(at_ctx, [GB, D], F32)
        v_sb = carve(at_ctx + GB * D * 4, [GB, HD], F32)
        bo_b = carve(at_ctx + (GB + 1) * D * 4, [D], F32)
        vb_b = carve(at_ctx + (GB + 2) * D * 4, [HD], F32)
        xr = carve(at_ctxt, [2, D], F32)
        xs3 = carve(at_xs, [2, D], F32)
        cx = carve(at_ctx, [CC, D], F32)
        cxp = [carve(at_ctx + (1 + i) * CC * D * 4, [2, CC, D], F16) for i in range(2)]
        cxt = carve(at_ctxt, [2, KC, CTX], F16)
        pt3 = carve(at_pt3, [2, CC, S], F16)
        u_b = carve(at_ub, [D], F32)
        at_tmp = at_ctx + (GB + 2) * D * 4 + HD * 4
        tmp = carve(at_tmp, [FP], F32)
        tmp_i = carve(at_tmp, [FP], I32)
        assert at_tmp + 4 * FP <= at_ctxt
        at_low = at_x2t + (KC * D + 2 * KC * P) * 4
        tab = carve(at_low, [FP], BF16)
        mid = carve(at_low + 2 * FP, [FP], BF16)
        qz = carve(at_low + 4 * FP, [FF // 8], U32)
        flat = [t_in[f"L0_ffn_{m}_scales"].shape[0] * t_in[f"L0_ffn_{m}_scales"].shape[1] // P
                for m in ("gate", "up", "down")]
        s_flat = [carve(at_low + 4 * FP + FF // 2 + 4 * sum(flat[:m]), [flat[m]], F32) for m in range(3)]
        assert at_low + 4 * FP + FF // 2 + 4 * sum(flat) <= at_tab
        wd = carve(at_rest, [NI, 2, D], F16)
        at_b = at_rest + NI * 2 * D * 2
        wgu = [[carve(at_b + ((1 - s) * 2 + m) * 4 * D, [2, KC, P], F16) for m in range(2)] for s in range(2)]
        at_b += 16 * D
        wbuf = [carve(at_b + i * 4 * D, [D], F32) for i in range(3)]
        at_b += 12 * D
        qw = [[carve(at_b + (s * 2 + m) * 4 * P, [P], U32) for m in range(2)] for s in range(2)]
        at_b += 16 * P
        tabc = [carve(at_b + s * 4 * P, [2, P], BF16) for s in range(2)]
        at_b += 8 * P
        h_st = carve(at_b, [2, NT], F16)
        at_b += NT * 4
        up_c = wbuf[1][:, 0:TG]
        g_act = carve(at_b, [TG], F32)
        h_f = carve(at_b + TG * 4, [TG], F32)
        at_c = at_rest + NI * 2 * D * 2
        ht = [carve(at_c + 8 * D + i * NI * 4 * P, [NI, 2, P], F16) for i in range(2)]
        assert NI * 4 * P <= 12 * D
        xf = [carve(at_x2t + i * D * 4, [D], F32) for i in range(2)]
        yf = [carve(at_x2t + (2 + i) * D * 4, [D], F32) for i in range(2)]

        ident = sb("ident", [P, P], F32)
        ones = sb("ones", [P, 1], F32)
        ident_h = sb("ident_f16", [P, P], F16)
        sp_ = sb("logits", [P, CTX + 1], F32)
        small = sb("small", [P, 192], F32)
        used = [0]

        def col(name, n=1):
            used[0] += n
            return small[:, used[0] - n:used[0]]

        bqk = col("bqk", 2 * HC)
        mx1, nm1, rs1, rc1 = col("mx1", GB), col("nm1", GB), col("rs1", GB), col("rc1", GB)
        st, mv, ve, rstd, mhalf = col("st", 12), col("mv", 2), col("ve"), col("rstd"), col("mhalf")
        bqc, bkc, v2, v2s, c0 = col("bqc", KC), col("bkc", KC), col("v2", KC), col("v2s", KC), col("c0")
        rr, nm3, rs3, rc3 = col("rr", GB), col("nm3"), col("rs3", GB), col("rc3", GB)
        amx, amr, pw, fac = col("amx", 3), col("amr", 3), col("pw", 4), col("fac", 3)
        inv_g, sc_u, inv_d, ghu = col("inv_g"), col("sc_u"), col("inv_d"), col("ghu")
        rowid, rowid_f, nib, four = col("rowid", 1), col("rowid_f"), col("nib", 3), col("masks", KC)
        mgp, mag, magr, pwg = col("mgp", 3), col("mag", 2), col("magr", 2), col("pwg", 2)
        fm, kg, ig = col("fm"), col("kg"), col("ig")
        cmx, cmr, pwc = col("cmx", 2), col("cmr", 2), col("pwc")
        fc, il, ia = col("fc", GB), col("il", GB), col("ia", GB)
        pc = col("pc", KC)
        wmx, wmr, pww, fww = col("wmx", 3), col("wmr", 3), col("pww", 2), col("fww", 2)
        kw, kwo, k4 = col("kw"), col("kwo"), col("k4")
        xmx, xmr, pwx, fx, abv, pwb, fo, ko, kq = [col(a) for a in ("xmx", "xmr", "pwx", "fx", "abv", "pwb", "fo", "ko", "kq")]
        assert used[0] <= 192

        psum = ctx.enter_context(nc.psum_tensor("psum", [P, 8 * 512], F32))
        bk = [psum[:, i * 512:(i + 1) * 512] for i in range(8)]
        bkh = [b.bitcast(F16).rearrange("p (l c) -> p l c", l=2) for b in bk]
        xt_bank = (0, 1, 6, 7)
        ct_bank = (0, 1, 6, 7)
        CT_ACT, CT_DVE = (0, 1, 2, 3, 4, 6), (5, 7)
        NA, ND = len(CT_ACT), len(CT_DVE)
        LOW = 1e-25
        LOW1 = 1e-18

        s_const = sem("constants"); s_cc = sem("constant_step")
        s_w0 = sem("wqkv_low_chunks_in"); s_w1 = sem("wqkv_high_chunks_in"); s_wo = sem("wo_in")
        s_bias = sem("biases_in"); s_bo = sem("bo_in")
        s_xs = [sem(f"xs_in{b}") for b in range(GB)]
        s_xr = [sem(f"residual_in{i}") for i in range(2)]
        s_yout = [sem(f"rows_out{i}") for i in range(2)]
        s_xt = sem("xT_in_psum"); s_xh = sem("xT_hi_ready"); s_xl = sem("xT_lo_ready")
        s_wm = sem("weight_max_step"); s_wr = sem("weight_max_all"); s_wf1 = sem("weight_factor_step")
        s_wph = sem("wqkv_hi_ready"); s_wpl = sem("wqkv_lo_ready"); s_woh = sem("wo_hi_ready")
        s_wol = sem("wo_lo_ready")
        s_xm = sem("x_max_ready"); s_xr1 = sem("x_max_all"); s_xf1 = sem("x_factor_step")
        s_gf = sem("group_factor_step"); s_ko = sem("output_factor")
        s_x1t = sem("x1T_in_psum"); s_x1h = sem("x1T_hi_ready"); s_x1l = sem("x1T_lo_ready")
        s_xs3 = [sem(f"x1_rows_in{i}") for i in range(2)]; s_xr3 = [sem(f"x1_residual_in{i}") for i in range(2)]
        s_ch = sem("ctx_hi_ready"); s_cl = sem("ctx_lo_ready"); s_cm = sem("ctx_max_ready")
        s_cr = sem("ctx_max_all"); s_cf = sem("ctx_factor_step"); s_stash = sem("down_tables_out")
        s_unstash = sem("down_tables_in")
        s_ub = sem("u_rows_in_psum"); s_pv = sem("bqbk_parts"); s_pu = sem("bqWk_parts"); s_uc = sem("Wqbk_parts")
        s_mm = sem("m_max_step"); s_mf = sem("m_max_all"); s_fs = sem("m_factor_step"); s_mh = sem("m_hi_ready")
        s_ml = sem("m_lo_ready"); s_gl = sem("g_lo_ready"); s_ih = sem("f16_identity"); s_seen2 = sem("wait_seen")
        s_ube = sem("u_rows_copied")
        s_qk = sem("qk_in_psum"); s_qke = sem("qk_copied")
        s_s = sem("scores_in_psum"); s_v = sem("v_in_psum"); s_ve = sem("v_copied")
        s_mx = sem("max_ready"); s_nm = sem("neg_max_ready"); s_exp = sem("exp_done")
        s_rc = sem("recip_ready"); s_p = sem("probs_ready"); s_pt = sem("probsT_in_psum")
        s_pte = sem("probsT_copied"); s_o = sem("oT_in_psum"); s_oh = sem("oT_hi_ready"); s_ol = sem("oT_lo_ready")
        s_w = sem("attn_in_psum"); s_xb = sem("residual_plus_bo"); s_y = sem("sum_ready")
        s_st = sem("stats_ready"); s_seen = sem("stats_seen"); s_ag = sem("mean_var_ready")
        s_eps = sem("var_eps_ready")
        s_rstd = sem("rstd_ready"); s_n = sem("rows_normalised")
        s_wk = sem("wk_in"); s_wq = [sem(f"wq_in{i}") for i in range(2)]
        s_m = sem("m_in_psum"); s_me = sem("m_copied"); s_v2 = sem("v2_in_psum"); s_v2e = sem("v2_copied")
        s_tin = [sem(f"table_input{i}_in") for i in range(6)]; s_t = sem("table_step"); s_amx = sem("scale_max_all")
        s_tabo = sem("tables_out")
        s_cx = sem("ctx_in")
        s_ct = sem("ctxT_in_psum"); s_cta = sem("ctxT_even_copied"); s_ctd = sem("ctxT_odd_copied")
        s_g = sem("g_in_psum"); s_ge = sem("g_copied"); s_re = sem("row_term_ready")
        s_l = sem("logits_in_psum"); s_le = sem("logits_copied"); s_rb = sem("row_term_with_biases")
        s_lm = sem("logit_max")
        s_ex3 = sem("exp3_done"); s_rc3 = sem("recip3_ready")
        s_pt3 = sem("p3T_in_psum"); s_ph = sem("p3T_hi_ready"); s_pl = sem("p3T_lo_ready")
        s_at = sem("attended_in_psum")
        s_y3 = sem("sum3_ready"); s_x2t = sem("x2T_in_psum"); s_hi = sem("x2T_hi_ready"); s_lo = sem("x2T_lo_ready")
        s_qw = [sem(f"qw_in{i}") for i in range(2)]; s_tc = [sem(f"tabc_in{i}") for i in range(2)]
        s_qd = sem("qw_down_in")
        s_ga = sem("gather_in_psum"); s_wf = sem("weights_f32_ready"); s_dq = sem("dequant_step")
        s_wh = sem("weights_hi_ready"); s_wl = sem("weights_lo_ready")
        s_uo = sem("last_up_copied"); s_gp = sem("gate_in_psum"); s_up = sem("up_in_psum")
        s_si = sem("silu_ready"); s_hf = sem("h_f32_ready"); s_hh = sem("h_hi_ready"); s_hl = sem("h_lo_ready")
        s_ho = [sem(f"h_out{i}") for i in range(2)]
        s_ht = [sem(f"hT_in{i}") for i in range(2)]; s_h0 = sem("hT_of_tile0_in")
        s_xf = [sem(f"x2_in{i}") for i in range(2)]
        s_d = sem("down_in_psum"); s_y5 = sem("sum5_ready"); s_n5 = sem("rows5_normalised")
        s_fin = [sem(f"final_out{i}") for i in range(2)]

        block = ctx.enter_context(nc.Block())

        def rows(ap, n):
            return ap[bass.ds(n * S, S), :]

        x_rows = x_d.rearrange("b s d -> (b s) d")
        NLN = 2 * NB
        NGATHER = 3 * NI - 1

        def down_no(i):
            if isinstance(i, int) and i >= NI - 2:
                return NGATHER - NI + i
            return 3 * i + 4

        def is_last(i):
            return isinstance(i, int) and i == NI - 1

        def ctx_pieces(n):
            return 16 * (CC + 1) * n + 16 * (CC + 1)

        def known(n, limit):
            return isinstance(n, int) and n < limit

        def batches(g, has):
            for b in range(GB):
                n = g * GB + b
                yield b, n, (lambda k, b=b: has or b + k < GB)

        def wd_parts(i):
            if isinstance(i, int):
                return [wd[:, i, l, :] for l in range(2)]
            return [wd[:, bass.ds(i, 1), l, :].rearrange("p o c -> p (o c)") for l in range(2)]

        T = {}

        @block.vector
        def _(dve):
            for i in range(2):
                dve.sem_inc(s_yout[i], 16)
                dve.sem_inc(s_ho[i], 32)
                dve.sem_inc(s_fin[i], 16)
            dve.sem_inc(s_hf, 2)
            dve.sem_inc(s_hl, 1)
            dve.sem_inc(s_hh, 1)
            dve.sem_inc(s_lo, 1)

            def norm_stats(y, k, summed, first):
                n = y.shape[0]
                for h in range(2):
                    dve.wait_ge(summed, first + h)
                    dve.bn_stats(st[0:n, 6 * h:6 * h + 6], y[:, h * HALF:(h + 1) * HALF]).then_inc(s_st, 1)
                dve.wait_ge(s_st, 2 * k + 2)
                dve.sem_inc(s_seen, 1)
                dve.bn_aggr(mv[0:n, :], st[0:n, :]).then_inc(s_ag, 1)
                dve.wait_ge(s_ag, k + 1)
                dve.tensor_scalar(ve[0:n, :], mv[0:n, 1:2], EPS, None, ALU.add).then_inc(s_eps, 1)

            def norm_apply(y, k, done):
                n = y.shape[0]
                dve.wait_ge(s_rstd, k + 1)
                dve.tensor_scalar(y, y, mv[0:n, 0:1], rstd[0:n, :], ALU.subtract, ALU.mult).then_inc(done, 1)

            def x_lo(g, places):
                for k in places:
                    c = KC - 1 - k
                    dve.wait_ge(s_xh, KC * g + k + 1)
                    dve.scalar_tensor_tensor(xtp[:, 1, c, :], bk[xt_bank[k % 4]][:, 0:TG], fx, xtp[:, 0, c, :],
                                             ALU.mult, ALU.subtract).then_inc(s_xl, 1)

            def x_max(g):
                for b in range(GB):
                    dve.wait_ge(s_xs[b], 16 * g + 16)
                dve.tensor_reduce(xmx[0:S, :], xs[0:S, :, :].rearrange("p b d -> p (b d)"), AX.X, ALU.max,
                                  apply_absolute_value=True).then_inc(s_xm, 1)

            def x_factor(g):
                k = [0]

                def step(ins):
                    ins.then_inc(s_xf1, 1)
                    k[0] += 1
                    dve.wait_ge(s_xf1, 4 * g + k[0])

                dve.wait_ge(s_xr1, g + 1)
                step(dve.tensor_scalar(pwx, xmr, LOW1, None, ALU.max))
                step(dve.tensor_scalar(pwx.bitcast(I32), pwx.bitcast(I32), 0x7F800000, None, ALU.bitwise_and))
                step(dve.reciprocal(fx, pwx))
                step(dve.tensor_scalar(fx, fx, 2.0 ** 14, None, ALU.mult))

            def group_factors(g):
                k = [0]

                def step(ins):
                    ins.then_inc(s_gf, 1)
                    k[0] += 1
                    dve.wait_ge(s_gf, 5 * g + k[0])

                step(dve.tensor_scalar(kq, pwx, kw, None, ALU.mult))
                step(dve.tensor_scalar(pwb, pwx, k4, abv, ALU.mult, ALU.add))
                step(dve.tensor_scalar(pwb.bitcast(I32), pwb.bitcast(I32), 0x7F800000, None, ALU.bitwise_and))
                step(dve.reciprocal(fo, pwb))
                step(dve.tensor_scalar(fo, fo, 2.0 ** 14, None, ALU.mult))

            def self_attention(g, more, beside=()):
                if more:
                    x_max(g + 1)
                if known(g, 1):
                    wo_split()
                for work in beside:
                    work()
                dve.wait_ge(s_s, g + 1)
                dve.tensor_reduce(mx1[0:S, :], bk[2][0:S, 0:TG].rearrange("p (b k) -> p b k", b=GB), AX.X,
                                  ALU.max, negate=True).then_inc(s_mx, 1)
                dve.wait_ge(s_mx, g + 1)
                dve.tensor_scalar(nm1[0:S, :], mx1[0:S, :], HD ** -0.5, None, ALU.mult).then_inc(s_nm, 1)
                if more:
                    x_factor(g + 1)
                dve.wait_ge(s_exp, GB * g + GB)
                dve.reciprocal(rc1[0:S, :], rs1[0:S, :]).then_inc(s_rc, 1)
                dve.wait_ge(s_rc, g + 1)
                dve.tensor_tensor(pr[0:S, :, :], pr[0:S, :, :], rc1[0:S, :].unsqueeze(2).to_broadcast([S, GB, S]),
                                  ALU.mult).then_inc(s_p, 1)
                for p in range(2):
                    dve.wait_ge(s_v, 2 * g + p + 1)
                    dve.scalar_tensor_tensor(v_sb[0:S, 2 * p:2 * p + 2, :],
                                             bk[4 + p][0:S, :].rearrange("p (b d) -> p b d", b=2), kq[0:S, :],
                                             vb_b[0:S, :].unsqueeze(1).to_broadcast([S, 2, HD]), ALU.mult,
                                             ALU.add).then_inc(s_ve, 1)
                dve.wait_ge(s_pt, g + 1)
                dve.tensor_copy(pt[0:S, :, :], bk[4][0:S, 0:TG].rearrange("p (b k) -> p b k", b=GB)).then_inc(s_pte, 1)
                if more:
                    x_lo(g + 1, range(KC // 2))
                for c in range(HC):
                    dve.wait_ge(s_oh, HC * g + c + 1)
                    dve.scalar_tensor_tensor(otp[:, 1, c, :], bk[3 - c][:, 0:TG], fo, otp[:, 0, c, :], ALU.mult,
                                             ALU.subtract).then_inc(s_ol, 1)
                if more:
                    x_lo(g + 1, range(KC // 2, KC))
                dve.tensor_scalar(ko, pwb, kwo, None, ALU.mult).then_inc(s_ko, 1)
                dve.wait_ge(s_ko, g + 1)
                if more:
                    group_factors(g + 1)
                for b in range(GB):
                    n = g * GB + b
                    dve.wait_ge(s_xb, n + 1)
                    dve.wait_ge(s_yout[b % 2], 16 * (2 * g + b // 2 + 1))
                    for h in range(2):
                        cols = slice(h * HALF, (h + 1) * HALF)
                        dve.wait_ge(s_w, 2 * n + h + 1)
                        dve.scalar_tensor_tensor(yo[0:S, b % 2, cols], bk[4 + 2 * (b % 2) + h][0:S, :], ko[0:S, :],
                                                 xr[0:S, b % 2, cols], ALU.mult, ALU.add).then_inc(s_y, 1)
                    norm_stats(yo[0:S, b % 2, :], n, s_y, 2 * n + 1)
                    norm_apply(yo[0:S, b % 2, :], n, s_n)

            steps = [0]

            def step(ins):
                ins.then_inc(s_t, 1)
                steps[0] += 1
                dve.wait_ge(s_t, steps[0])

            def table_factors():
                dve.wait_ge(s_tin[0], 48)
                for m in range(3):
                    step(dve.tensor_reduce(amx[:, m:m + 1], s_flat[m], AX.X, ALU.max, apply_absolute_value=True))
                T["amx"] = steps[0]
                dve.wait_ge(s_amx, 1)
                step(dve.tensor_scalar(amr, amr, 1e-15, None, ALU.max))
                step(dve.tensor_tensor(ghu, amr[:, 0:1], amr[:, 1:2], ALU.mult))
                step(dve.tensor_scalar(pw[:, 0:3].bitcast(I32), amr.bitcast(I32), 0x7F800000, None, ALU.bitwise_and))
                step(dve.tensor_scalar(pw[:, 3:4].bitcast(I32), ghu.bitcast(I32), 0x7F800000, None, ALU.bitwise_and))
                step(dve.reciprocal(fac, pw[:, 0:3]))
                step(dve.tensor_scalar(fac, fac, 1024.0, None, ALU.mult))
                step(dve.tensor_scalar(inv_g, pw[:, 0:1], 2.0 ** -10 / XS, None, ALU.mult))
                step(dve.reciprocal(sc_u, pw[:, 3:4]))
                step(dve.tensor_tensor(sc_u, sc_u, pw[:, 1:2], ALU.mult))
                step(dve.tensor_scalar(sc_u, sc_u, 2.0 ** -24 / XS, None, ALU.mult))
                step(dve.tensor_tensor(inv_d, pw[:, 3:4], pw[:, 2:3], ALU.mult))
                step(dve.tensor_scalar(inv_d, inv_d, 2.0 ** 4, None, ALU.mult))
                dve.wait_ge(s_const, 4)
                step(dve.tensor_scalar(nib[:, 0:1].bitcast(I32), rowid.bitcast(I32), 31, None, ALU.bitwise_and))
                step(dve.tensor_copy(rowid_f, nib[:, 0:1].bitcast(I32)))
                step(dve.memset(nib[:, 1:2].bitcast(U32), 15))
                step(dve.tensor_scalar(nib[:, 0:1].bitcast(I32), rowid.bitcast(I32), 7, 2, ALU.bitwise_and,
                                       ALU.arith_shift_left))
                step(dve.tensor_tensor(nib[:, 2:3].bitcast(U32), nib[:, 1:2].bitcast(U32), nib[:, 0:1].bitcast(U32),
                                       ALU.logical_shift_left))
                for j in range(8):
                    step(dve.memset(four[:, j:j + 1].bitcast(U32), 15 << (4 * j)))

            def selection(at, groups, width, put):
                step(dve.tensor_scalar(neg[:, 0:width], tmp_i[:, at:at + width], 0, groups, ALU.is_lt, ALU.mult))
                step(dve.tensor_tensor(tmp[:, at:at + width], tmp_i[:, at:at + width], neg[:, 0:width], ALU.add))
                step(dve.tensor_scalar(tmp[:, at:at + width], tmp[:, at:at + width], 0, groups - 1, ALU.max, ALU.min))
                for j in range(8):
                    put(slice(0, 96), j, 2.0 ** (-4 * j), tmp[0:96, at + j:at + width:8])
                    put(slice(96, 128), j, 2.0 ** (4 * j), tmp[96:128, at + j:at + width:8])

            neg = mid

            def clear_tables():
                for m in range(2):
                    step(dve.memset(sel_s[m].rearrange("p a b -> p (a b)").bitcast(U32), 0))
                    step(dve.memset(sel_z[m].rearrange("p a b -> p (a b)").bitcast(U32), 0))
                step(dve.memset(sel_d.rearrange("p a b -> p (a b)").bitcast(U32), 0))
                step(dve.memset(tab_ds.bitcast(U32), 0))
                step(dve.memset(tab_dz.bitcast(U32), 0))

            def select(m):
                groups, width = (GU, GU, GD)[m], (D, D, FF)[m]

                def put(r, j, factor, in0):
                    if m == 2:
                        dst = sel_d.rearrange("p a b -> p (a b)")[r, j:width:8]
                    else:
                        dst = (sel_s if r.start == 0 else sel_z)[m][r, j, :]
                    step(dve.tensor_scalar(dst, in0, rowid_f[r, :], factor, ALU.is_equal, ALU.mult))

                dve.wait_ge(s_tin[1], 16 * max(m + 1, 2))
                selection(D if m == 1 else 0, groups, width, put)
                T[f"idx{m}"] = steps[0]

            w_steps = [0]

            def w_step(ins):
                ins.then_inc(s_wf1, 1)
                w_steps[0] += 1
                dve.wait_ge(s_wf1, w_steps[0])

            def w_factor(m, waited):
                dve.wait_ge(s_wr, waited)
                w_step(dve.tensor_scalar(pww[:, m:m + 1].bitcast(I32), pww[:, m:m + 1].bitcast(I32), 0x7F800000, None,
                                         ALU.bitwise_and))
                w_step(dve.reciprocal(fww[:, m:m + 1], pww[:, m:m + 1]))
                w_step(dve.tensor_scalar(fww[:, m:m + 1], fww[:, m:m + 1], 2.0 ** 14, None, ALU.mult))

            def wo_split():
                dve.wait_ge(s_wo, 16)
                dve.tensor_reduce(wmx[:, 2:3], wo.rearrange("p c n -> p (c n)"), AX.X, ALU.max,
                                  apply_absolute_value=True).then_inc(s_wm, 1)
                dve.wait_ge(s_wr, 2)
                w_step(dve.tensor_scalar(pww[:, 1:2], wmr[:, 2:3], LOW1, None, ALU.max))
                w_factor(1, 2)
                w_step(dve.tensor_scalar(kwo, pww[:, 1:2], 2.0 ** -28, None, ALU.mult))
                for c in range(HC):
                    dve.wait_ge(s_woh, c + 1)
                    dve.scalar_tensor_tensor(wop[:, c, 1, :], wo[:, c, :], fww[:, 1:2], wop[:, c, 0, :], ALU.mult,
                                             ALU.subtract).then_inc(s_wol, 1)

            w_step(dve.memset(xmx, 0.0))
            x_max(0)
            for h, landed in enumerate((s_w0, s_w1)):
                if h:
                    x_factor(0)
                    x_lo(0, range(KC))
                dve.wait_ge(landed, 16)
                dve.tensor_reduce(wmx[:, h:h + 1], wqkv[:, h * KC // 2:(h + 1) * KC // 2, :].rearrange("p c f -> p (c f)"),
                                  AX.X, ALU.max, apply_absolute_value=True).then_inc(s_wm, 1)
            dve.wait_ge(s_wr, 1)
            w_step(dve.tensor_scalar(pww[:, 0:1], wmr[:, 0:1], wmr[:, 1:2], LOW1, ALU.max, ALU.max))
            w_factor(0, 1)
            T["fw"] = w_steps[0]
            for k in range(KC):
                c = KC - 1 - k
                dve.wait_ge(s_wph, k + 1)
                dve.scalar_tensor_tensor(wqp[:, c, 1, :], wqkv[:, c, :], fww[:, 0:1], wqp[:, c, 0, :], ALU.mult,
                                         ALU.subtract).then_inc(s_wpl, 1)
            w_step(dve.tensor_scalar(kw, pww[:, 0:1], 2.0 ** -28, None, ALU.mult))
            w_step(dve.tensor_scalar(k4, pww[:, 0:1], 4096.0, None, ALU.mult))
            dve.wait_ge(s_bias, 32)
            w_step(dve.tensor_reduce(abv, vb_b, AX.X, ALU.max, apply_absolute_value=True))
            T["fwo"] = w_steps[0] + 4
            group_factors(0)
            self_attention(0, True)
            self_attention(1, True, (table_factors, clear_tables))
            with dve.Fori(2, NG - 1) as g:
                self_attention(g, True)
            self_attention(NG - 1, False, (lambda: select(0), lambda: select(1)))
            select(2)

            for m, groups in enumerate((GU, GU, GD)):
                width = FF if m < 2 else D
                s_to = tab if m < 2 else tab_ds
                z_to = tab if m < 2 else tab_dz
                if m == 0:
                    step(dve.memset(tab.bitcast(U32), 0))
                dve.wait_ge(s_tin[2], 16 * (m + 1))
                if m == 1:
                    dve.wait_ge(s_tabo, 16)
                s = tmp[0:groups, 0:width]
                step(dve.tensor_scalar(s, s, fac[0:groups, m:m + 1], None, ALU.mult))
                step(dve.tensor_copy(s_to[0:groups, 0:width], s))
                step(dve.tensor_tensor(s, s, s_to[0:groups, 0:width], ALU.subtract))
                step(dve.tensor_copy(mid[0:groups, 0:width], s))
                step(dve.tensor_copy(s_to[32:32 + groups, 0:width], s))
                step(dve.tensor_tensor(s, s, mid[0:groups, 0:width], ALU.subtract))
                step(dve.tensor_copy(s_to[64:64 + groups, 0:width], s))
                dve.wait_ge(s_tin[3], 16 * (m + 1))
                z = tmp_i[96:96 + groups, 0:width]
                for j in range(8):
                    step(dve.tensor_scalar(z[:, j:width:8].bitcast(U32), qz[96:96 + groups, 0:width // 8], 4 * j, 15,
                                           ALU.logical_shift_right, ALU.bitwise_and))
                step(dve.tensor_scalar(z_to[96:96 + groups, 0:width], z, 1, None, ALU.add))
                T[f"tab{m}"] = steps[0]

            def x1t_lo(m, b, bank=2):
                cols = slice(b * S, (b + 1) * S)
                for j in range(2):
                    dve.wait_ge(s_x1h, 2 * m + j + 1)
                    dve.scalar_tensor_tensor(xtp[:, 1, 4 * j:4 * j + 4, cols],
                                             bk[bank + j][:, 0:TG].rearrange("p (a t) -> p a t", a=4), XS,
                                             xtp[:, 0, 4 * j:4 * j + 4, cols], ALU.mult, ALU.subtract).then_inc(s_x1l, 1)

            def slot_fills(n, b):
                return 8 * (n - b % 2) + 16

            def row_term(n, b):
                dve.wait_ge(s_xr3[b % 2], slot_fills(n, b))
                dve.wait_ge(s_yout[b % 2], 16 * NB // 2 + slot_fills(n, b))
                dve.tensor_tensor_reduce(yo[0:S, b % 2, :], xr3[0:S, b % 2, :], u_b[0:S, :], 1.0, 0.0,
                                         ALU.mult, ALU.add, rr[0:S, b:b + 1]).then_inc(s_re, 1)

            def softmax_in(n, b):
                dve.wait_ge(s_re, n + 1)
                dve.tensor_scalar(rr[0:S, b:b + 1], rr[0:S, b:b + 1], c0[0:S, :], D ** -0.5, ALU.add,
                                  ALU.mult).then_inc(s_rb, 1)
                dve.wait_ge(s_l, n + 1)
                dve.wait_ge(s_rb, n + 1)
                dve.tensor_scalar(sp_[0:S, 0:CTX], bk[5][0:S, 0:CTX], il[0:S, b:b + 1], rr[0:S, b:b + 1],
                                  ALU.mult, ALU.add).then_inc(s_le, 1)
                dve.wait_ge(s_le, n + 1)
                dve.tensor_reduce(nm3[0:S, :], sp_[0:S, 0:CTX], AX.X, ALU.max, negate=True).then_inc(s_lm, 1)

            def context_t(n):
                for c in CT_DVE:
                    dve.wait_ge(s_ct, KC * n + c + 1)
                    dve.tensor_copy(cxt[:, :, c, :], bkh[ct_bank[c % 4]][:, :, 0:CTX]).then_inc(s_ctd, 1)

            def context_max(n):
                dve.wait_ge(s_cx, ctx_pieces(n))
                dve.tensor_reduce(cmx[:, 0:1], cx[:, 0:CC - 1, :].rearrange("p c d -> p (c d)"), AX.X, ALU.max,
                                  apply_absolute_value=True)
                dve.tensor_reduce(cmx[0:CP[-1], 1:2], cx[0:CP[-1], CC - 1, :], AX.X, ALU.max,
                                  apply_absolute_value=True).then_inc(s_cm, 1)

            def context_factor(n, b, undo=True):
                k = [0]

                def step(ins):
                    ins.then_inc(s_cf, 1)
                    k[0] += 1
                    dve.wait_ge(s_cf, 5 * n + k[0])

                dve.wait_ge(s_cr, n + 1)
                step(dve.tensor_reduce(pwc, cmr, AX.X, ALU.max))
                step(dve.tensor_scalar(pwc, pwc, LOW, None, ALU.max))
                step(dve.tensor_scalar(pwc.bitcast(I32), pwc.bitcast(I32), 0x7F800000, None, ALU.bitwise_and))
                if undo:
                    dve.tensor_scalar(il[:, b:b + 1], pwc, ig, None, ALU.mult)
                dve.tensor_scalar(ia[:, b:b + 1], pwc, 2.0 ** -14 / XS, None, ALU.mult)
                step(dve.reciprocal(fc[:, b:b + 1], pwc))
                step(dve.tensor_scalar(fc[:, b:b + 1], fc[:, b:b + 1], 2.0 ** 14, None, ALU.mult))

            def context_lo(n, b, c):
                dve.wait_ge(s_ch, CC * n + c + 1)
                dve.scalar_tensor_tensor(cxp[b % 2][0:CP[c], 1, c, :], cx[0:CP[c], c, :], fc[0:CP[c], b:b + 1],
                                         cxp[b % 2][0:CP[c], 0, c, :], ALU.mult, ALU.subtract).then_inc(s_cl, 1)

            def probs_lo(n):
                dve.wait_ge(s_ph, n + 1)
                for c in range(CC):
                    ins = dve.scalar_tensor_tensor(pt3[0:CP[c], 1, c, :], bk[4][0:CP[c], c * P:c * P + S], XS,
                                                   pt3[0:CP[c], 0, c, :], ALU.mult, ALU.subtract)
                ins.then_inc(s_pl, 1)

            def x2t_lo(n):
                for j in range(2):
                    dve.wait_ge(s_hi, 2 * n + j + 1)
                    dve.scalar_tensor_tensor(x2t[:, 1, 4 * j:4 * j + 4, bass.ds(n * S, S)],
                                             bk[j][:, 0:TG].rearrange("p (a t) -> p a t", a=4), XS,
                                             x2t[:, 0, 4 * j:4 * j + 4, bass.ds(n * S, S)],
                                             ALU.mult, ALU.subtract).then_inc(s_lo, 1)

            def add_attended(n, b):
                y = yo[0:S, b % 2, :]
                dve.wait_ge(s_ex3, n + 1)
                dve.reciprocal(rc3[0:S, b:b + 1], rs3[0:S, b:b + 1]).then_inc(s_rc3, 1)
                dve.wait_ge(s_rc3, 2 * n + 1)
                dve.tensor_scalar(rc3[0:S, b:b + 1], rc3[0:S, b:b + 1], ia[0:S, b:b + 1], None,
                                  ALU.mult).then_inc(s_rc3, 1)
                dve.wait_ge(s_rc3, 2 * n + 2)
                for h in range(2):
                    cols = slice(h * HALF, (h + 1) * HALF)
                    dve.wait_ge(s_at, 2 * n + h + 1)
                    dve.scalar_tensor_tensor(y[:, cols], bk[6 + h][0:S, :], rc3[0:S, b:b + 1],
                                             xr3[0:S, b % 2, cols], ALU.mult, ALU.add).then_inc(s_y3, 1)

            def cross_attention(g, more):
                for b, n, has in batches(g, more):
                    y = yo[0:S, b % 2, :]
                    softmax_in(n, b)
                    if has(1):
                        context_t(n + 1)
                    if has(2):
                        context_max(n + 2)
                    probs_lo(n)
                    if has(2):
                        context_factor(n + 2, (b + 2) % GB)
                    add_attended(n, b)
                    if has(2):
                        context_lo(n + 2, (b + 2) % GB, 0)
                    norm_stats(y, NB + n, s_y3, 2 * n + 1)
                    if has(2):
                        for c in range(1, CC):
                            context_lo(n + 2, (b + 2) % GB, c)
                    if not known(n, 1):
                        x2t_lo(n - 1)
                    if more:
                        x1t_lo(n + GB, b)
                    if has(1):
                        row_term(n + 1, (b + 1) % GB)
                    norm_apply(y, NB + n, s_n)

            k = [0]

            def factor_step(ins):
                ins.then_inc(s_fs, 1)
                k[0] += 1
                dve.wait_ge(s_fs, k[0])

            def largest_of_m(lo, hi, to):
                dve.wait_ge(s_me, 2 + hi)
                factor_step(dve.tensor_reduce(mgp[:, to:to + 1], m32[:, lo:hi, :].rearrange("p a b -> p (a b)"), AX.X,
                                              ALU.max, apply_absolute_value=True))

            factor_step(dve.memset(cmx, 0.0))
            context_max(0)
            x1t_lo(0, 0, 4)
            x1t_lo(1, 1, 6)
            largest_of_m(0, 5, 0)
            context_factor(0, 0, False)
            x1t_lo(2, 2, 4)
            x1t_lo(3, 3, 6)
            for c in range(CC):
                context_lo(0, 0, c)
            context_max(1)
            largest_of_m(5, 7, 1)
            largest_of_m(7, 8, 2)
            dve.tensor_reduce(mag[:, 0:1], mgp, AX.X, ALU.max).then_inc(s_mm, 1)
            dve.wait_ge(s_v2e, 1)
            dve.tensor_reduce(mag[:, 1:2], v2, AX.X, ALU.max, apply_absolute_value=True).then_inc(s_mm, 1)
            dve.wait_ge(s_mf, 1)
            factor_step(dve.tensor_scalar(magr[:, 0:1], magr[:, 0:1], LOW, None, ALU.max))
            factor_step(dve.scalar_tensor_tensor(magr[:, 1:2], magr[:, 0:1], 1024.0, magr[:, 1:2], ALU.mult, ALU.add))
            factor_step(dve.tensor_scalar(pwg.bitcast(I32), magr.bitcast(I32), 0x7F800000, None, ALU.bitwise_and))
            factor_step(dve.reciprocal(mag, pwg))
            factor_step(dve.tensor_scalar(fm, mag[:, 0:1], 2.0 ** 14, None, ALU.mult))
            FM = k[0]
            factor_step(dve.tensor_scalar(kg, pwg[:, 0:1], mag[:, 1:2], 1 / XS, ALU.mult, ALU.mult))
            factor_step(dve.tensor_scalar(v2s, v2, mag[:, 1:2], 2.0 ** 14, ALU.mult, ALU.mult))
            factor_step(dve.tensor_scalar(ig, pwg[:, 1:2], 2.0 ** -28 * D ** -0.5, None, ALU.mult))
            T["fm"], T["g"] = FM, k[0]
            dve.tensor_scalar(il[:, 0:1], ia[:, 0:1], ig, XS * 2.0 ** 14, ALU.mult, ALU.mult)
            for c in reversed(range(KC)):
                dve.wait_ge(s_mh, KC - c)
                dve.scalar_tensor_tensor(mp[:, c, 1, :], m32[:, c, :], fm, mp[:, c, 0, :], ALU.mult,
                                         ALU.subtract).then_inc(s_ml, 1)
            context_t(0)
            dve.wait_ge(s_ub, 1)
            dve.tensor_copy(u_b[0:S, :], psum[0:S, 2048:3072]).then_inc(s_ube, 1)
            context_factor(1, 1)
            for c in range(CC):
                context_lo(1, 1, c)
            dve.wait_ge(s_ube, 1)
            row_term(0, 0)
            cross_attention(0, True)
            with dve.Fori(1, NG - 1) as g:
                cross_attention(g, True)
            cross_attention(NG - 1, False)
            def dequant(q, kind, s, e):
                w = wbuf[kind]
                if kind < 2:
                    dve.wait_ge(s_qw[s], 32 * (e + 1))
                    if not isinstance(q, int) or q >= 2:
                        dve.wait_ge(s_wh, q - 1)
                        dve.wait_ge(s_wl, q - 1)
                    dve.tensor_tensor(w.bitcast(U32).rearrange("p (j n) -> p j n", j=8),
                                      qw[s][kind].unsqueeze(1).to_broadcast([P, 8, P]),
                                      four.bitcast(U32).unsqueeze(2).to_broadcast([P, 8, P]),
                                      ALU.bitwise_and).then_inc(s_dq, 1)
                else:
                    dve.wait_ge(s_qd, 16 * (e + 1))
                    dve.tensor_scalar(w.bitcast(U32), w.bitcast(U32), nib[:, 2:3].bitcast(U32), None,
                                      ALU.bitwise_and).then_inc(s_dq, 1)
                dve.wait_ge(s_ga, q + 1)
                dve.wait_ge(s_dq, 2 * q + 1)
                dve.tensor_tensor(w, w.bitcast(U32), psum[:, 3072:4096], ALU.subtract).then_inc(s_dq, 1)
                dve.wait_ge(s_dq, 2 * q + 2)
                dve.tensor_tensor(w, w, psum[:, 2048:3072], ALU.mult).then_inc(s_wf, 1)

            def hidden(i, t):
                joint = is_last(i)
                n = LASTC if joint else P
                dve.wait_ge(s_si, 4 * i + t + 1)
                if joint:
                    dve.wait_ge(s_uo, t + 1)
                else:
                    dve.wait_ge(s_up, 4 * i + t + 1)
                dve.wait_ge(s_hh, 4 * i + t + 1)
                dve.wait_ge(s_hl, 4 * i + t + 1)
                up = up_c if joint else bk[2 + t % 2][:, 0:TG]
                dve.scalar_tensor_tensor(h_f[0:n, :], up[0:n, :], sc_u[0:n, :], g_act[0:n, :], ALU.mult,
                                         ALU.mult).then_inc(s_hf, 1)
                if t % 2 == 0:
                    dve.wait_ge(s_ho[t // 2], 32 * (i + 1))
                dve.wait_ge(s_hh, 4 * i + t + 2)
                cols = slice(t * TG, (t + 1) * TG)
                dve.tensor_tensor(h_st[0:n, 1, cols], h_f[0:n, :], h_st[0:n, 0, cols], ALU.subtract).then_inc(s_hl, 1)

            def chunk(i, s, e, more):
                hidden(i, 0)
                if more:
                    dequant(3 * i + 2, 0, 1 - s, e + s)
                hidden(i, 1)
                if more and not (known(i, NI) and i == NI - 2):
                    dequant(3 * i + 3, 1, 1 - s, e + s)
                if is_last(i):
                    dequant(down_no(i), 2, s, i)
                hidden(i, 2)
                if not is_last(i):
                    dequant(down_no(i), 2, s, i)
                hidden(i, 3)

            dequant(0, 0, 0, 0)
            x2t_lo(NB - 1)
            dequant(1, 1, 0, 0)
            with dve.Fori(0, NI // 2 - 1) as e:
                for s in range(2):
                    chunk(2 * e + s, s, e, True)
            chunk(NI - 2, 0, NI // 2 - 1, True)
            chunk(NI - 1, 1, NI // 2 - 1, False)

            with dve.Fori(0, TT // 2) as e:
                for s in range(2):
                    tile = 2 * e + s
                    dve.wait_ge(s_xf[s], 16 * (e + 1))
                    dve.wait_ge(s_fin[s], 16 * (e + 1))
                    for c in range(2):
                        cols = slice(c * HALF, (c + 1) * HALF)
                        dve.wait_ge(s_d, 2 * tile + c + 1)
                        dve.scalar_tensor_tensor(yf[s][:, cols], bk[2 * s + c], inv_d, xf[s][:, cols],
                                                 ALU.mult, ALU.add).then_inc(s_y5, 1)
                    norm_stats(yf[s], NLN + tile, s_y5, 2 * tile + 1)
                    norm_apply(yf[s], NLN + tile, s_n5)

        @block.gpsimd
        def _(pool):
            pool.memset(ident[:], 1.0).then_inc(s_cc, 1)
            pool.memset(mhalf, -0.5).then_inc(s_const, 1)
            pool.iota(rowid.bitcast(I32), pattern=[[0, 1]], base=0, channel_multiplier=1).then_inc(s_const, 1)
            pool.memset(ones[:], 1.0).then_inc(s_const, 1)
            pool.wait_ge(s_cc, 1)
            pool.affine_select(out=ident[:], in_=ident[:], compare_op=ALU.is_equal, fill=0.0, base=0,
                               pattern=[[-1, P]], channel_multiplier=1).then_inc(s_const, 1)
            pool.wait_ge(s_const, 4)
            pool.tensor_copy(ident_h[:], ident[:]).then_inc(s_ih, 1)

            def inverse_std(k, n):
                pool.wait_ge(s_eps, k + 1)
                pool.tensor_tensor(rstd[0:n, :], ve[0:n, :], mhalf[0:n, :], ALU.pow).then_inc(s_rstd, 1)

            def x_largest(g):
                pool.wait_ge(s_xm, g + 1)
                pool.sem_inc(s_seen2, 1)
                pool.partition_all_reduce(xmr, xmx, P, RMAX).then_inc(s_xr1, 1)

            def add_bo(g, b):
                pool.wait_ge(s_xr[b % 2], 16 * (2 * g + b // 2 + 1))
                pool.tensor_tensor(xr[0:S, b % 2, :], xr[0:S, b % 2, :], bo_b[0:S, :], ALU.add).then_inc(s_xb, 1)

            def self_attention(g, more, largest=True):
                if more and largest:
                    x_largest(g + 1)
                for b in range(GB):
                    if b + 1 < GB:
                        add_bo(g, b + 1)
                    elif more:
                        add_bo(g + 1, 0)
                    inverse_std(g * GB + b, S)

            x_largest(0)
            pool.wait_ge(s_wm, 2)
            pool.partition_all_reduce(wmr[:, 0:2], wmx[:, 0:2], P, RMAX).then_inc(s_wr, 1)
            pool.wait_ge(s_wm, 3)
            pool.partition_all_reduce(wmr[:, 2:3], wmx[:, 2:3], P, RMAX).then_inc(s_wr, 1)
            pool.wait_ge(s_bo, 16)
            add_bo(0, 0)
            self_attention(0, True)
            x_largest(2)
            pool.wait_ge(s_t, T["amx"])
            pool.partition_all_reduce(amr, amx, P, RMAX).then_inc(s_amx, 1)
            self_attention(1, True, False)
            with pool.Fori(2, NG - 1) as g:
                self_attention(g, True)
            self_attention(NG - 1, False)

            pool.wait_ge(s_wk, 48)
            pool.memset(acc_v, 0.0).then_inc(s_pv, 1)
            pool.tensor_tensor(pc, bqc, bkc, ALU.mult).then_inc(s_pv, 1)
            for k, w in enumerate((KC // 2, KC // 4, KC // 8)):
                pool.wait_ge(s_pv, k + 2)
                pool.tensor_tensor(pc[:, 0:w], pc[:, 0:w], pc[:, w:2 * w], ALU.add).then_inc(s_pv, 1)
            pool.wait_ge(s_pv, 5)

            def m_chunk(e, i):
                m = 2 * e + i
                pool.wait_ge(s_wq[i], 16 * (e + 1))
                pool.tensor_tensor(part.rearrange("p (c x) -> p c x", c=KC), wq[i],
                                   bkc.unsqueeze(2).to_broadcast([P, KC, P]), ALU.mult).then_inc(s_uc, 1)
                for k, w in enumerate((D // 2, D // 4, D // 8)):
                    pool.wait_ge(s_uc, 4 * m + k + 1)
                    to = part[:, 0:w] if w > P else acc_u[:, bass.ds(m * P, P)]
                    pool.tensor_tensor(to, part[:, 0:w], part[:, w:2 * w], ALU.add).then_inc(s_uc, 1)
                pool.wait_ge(s_uc, 4 * m + 4)
                pool.tensor_tensor(part, wk[:, bass.ds(m, 1), :].rearrange("p o d -> p (o d)"),
                                   bqc[:, bass.ds(m, 1)].to_broadcast([P, D]), ALU.mult).then_inc(s_pu, 1)
                pool.wait_ge(s_pu, 2 * m + 1)
                pool.tensor_tensor(acc_v, acc_v, part, ALU.add).then_inc(s_pu, 1)
                pool.wait_ge(s_pu, 2 * m + 2)
                pool.sem_inc(s_seen2, 1)

            with pool.Fori(0, KC // 2) as e:
                for i in range(2):
                    m_chunk(e, i)

            def context_max(n):
                pool.wait_ge(s_cm, n + 1)
                pool.sem_inc(s_seen2, 1)
                pool.partition_all_reduce(cmr, cmx, P, RMAX).then_inc(s_cr, 1)

            def g_lo(k, y, q):
                t = slice(q * 2 * S, (q + 1) * 2 * S)
                pool.wait_ge(s_ge, k + 1)
                pool.tensor_tensor(gtp[:, 1, y, t], g_f, gtp[:, 0, y, t], ALU.subtract).then_inc(s_gl, 1)

            def cross_attention(g, more):
                for b, n, has in batches(g, more):
                    if has(2):
                        for k in range(4):
                            g_lo(KC + 4 * n + k, 4 * (b % 2) + k, 1 - b // 2)
                            if k == 0:
                                context_max(n + 2)
                    inverse_std(NB + n, S)

            context_max(0)
            context_max(1)
            pool.wait_ge(s_mm, 2)
            pool.partition_all_reduce(magr, mag, P, RMAX).then_inc(s_mf, 1)
            for y in range(KC):
                g_lo(y, y, 0)
            cross_attention(0, True)
            with pool.Fori(1, NG - 1) as g:
                cross_attention(g, True)
            cross_attention(NG - 1, False)

            def low_part(q, dst, kind):
                pool.wait_ge(s_wh, q + 1)
                src = wbuf[kind]
                if kind < 2:
                    src = src.rearrange("p (j n) -> p j n", j=8)
                pool.tensor_tensor(dst[1], src, dst[0], ALU.subtract).then_inc(s_wl, 1)

            for m in range(2):
                low_part(m, [wgu[0][m][:, l, :, :] for l in range(2)], m)

            def chunk(i, s, more):
                if more:
                    for m in range(1 if known(i, NI) and i == NI - 2 else 2):
                        low_part(3 * i + 2 + m, [wgu[1 - s][m][:, l, :, :] for l in range(2)], m)
                low_part(down_no(i), wd_parts(i), 2)

            with pool.Fori(0, NI // 2 - 1) as e:
                for s in range(2):
                    chunk(2 * e + s, s, True)
            chunk(NI - 2, 0, True)
            chunk(NI - 1, 1, False)
            with pool.Fori(NLN, NLN + TT) as k:
                inverse_std(k, P)

        @block.scalar
        def _(act):
            act.sem_inc(s_me, 2)

            def x_hi(g, places):
                for k in places:
                    act.wait_ge(s_xt, KC * g + k + 1)
                    act.activation(xtp[:, 0, KC - 1 - k, :], bk[xt_bank[k % 4]][:, 0:TG], ACT.Identity, scale=fx).then_inc(s_xh, 1)

            def self_attention(g, more):
                act.wait_ge(s_gf, 5 * g + 5)
                for f in range(2 * HC):
                    act.wait_ge(s_qk, 2 * HC * g + f + 1)
                    act.activation(qkt[:, f, :], bk[2 + f % 2][:, 0:TG], ACT.Identity, scale=kq,
                                   bias=bqk[:, f:f + 1]).then_inc(s_qke, 1)
                if known(g, 1):
                    act.wait_ge(s_wf1, T["fwo"])
                    for c in range(HC):
                        act.activation(wop[:, c, 0, :], wo[:, c, :], ACT.Identity, scale=fww[:, 1:2]).then_inc(s_woh, 1)
                act.wait_ge(s_nm, g + 1)
                for b in range(GB):
                    act.activation(pr[0:S, b, :], bk[2][0:S, b * S:(b + 1) * S], ACT.Exp, scale=HD ** -0.5,
                                   bias=nm1[0:S, b:b + 1], accum_out=rs1[0:S, b:b + 1]).then_inc(s_exp, 1)
                if more:
                    act.wait_ge(s_xf1, 4 * g + 8)
                    x_hi(g + 1, range(KC // 2))
                for c in range(HC):
                    act.wait_ge(s_o, HC * g + c + 1)
                    act.activation(otp[:, 0, c, :], bk[3 - c][:, 0:TG], ACT.Identity, scale=fo).then_inc(s_oh, 1)
                if more:
                    x_hi(g + 1, range(KC // 2, KC))

            act.wait_ge(s_xf1, 4)
            x_hi(0, range(KC))
            act.wait_ge(s_wf1, T["fw"])
            for k in range(KC):
                c = KC - 1 - k
                if k >= 2:
                    act.wait_ge(s_wpl, k - 1)
                act.activation(wqp[:, c, 0, :], wqkv[:, c, :], ACT.Identity, scale=fww[:, 0:1]).then_inc(s_wph, 1)
            act.wait_ge(s_bias, 32)
            self_attention(0, True)
            with act.Fori(1, NG - 1) as g:
                self_attention(g, True)
            self_attention(NG - 1, False)

            wq_v = t_in["L0_xattn_Wq"].rearrange("(p c) x -> p c x", c=KC)

            def m_chunk(e, i, more):
                act.wait_ge(s_m, 2 * e + i + 1)
                if more:
                    act.wait_ge(s_uc, 4 * (2 * e + i) + 1)
                    act.dma_start(wq[i], wq_v[:, :, bass.ds((2 * e + 2 + i) * P, P)]).then_inc(s_wq[i], 16)
                act.activation(m32[:, bass.ds(2 * e + i, 1), :].rearrange("p a b -> p (a b)"),
                               psum[:, i * 1024:(i + 1) * 1024], ACT.Identity).then_inc(s_me, 1)

            def x1t_hi(m, b, bank=2):
                for j in range(2):
                    act.wait_ge(s_x1t, 2 * m + j + 1)
                    act.activation(xtp[:, 0, 4 * j:4 * j + 4, b * S:(b + 1) * S],
                                   bk[bank + j][:, 0:TG].rearrange("p (a t) -> p a t", a=4),
                                   ACT.Identity, scale=XS).then_inc(s_x1h, 1)

            def g_out(k, y, q):
                act.wait_ge(s_g, k + 1)
                act.activation(gtp[:, 0, y, q * 2 * S:(q + 1) * 2 * S], bk[2 + y % 2][:, 0:2 * S], ACT.Identity,
                               scale=kg, bias=v2s[:, y:y + 1])
                if not known(k, 1):
                    act.wait_ge(s_gl, k)
                act.activation(g_f, bk[2 + y % 2][:, 0:2 * S], ACT.Identity, scale=kg,
                               bias=v2s[:, y:y + 1]).then_inc(s_ge, 1)

            def context_t(n, chunks):
                for c in chunks:
                    act.wait_ge(s_ct, KC * n + c + 1)
                    act.activation(cxt[:, :, c, :], bkh[ct_bank[c % 4]][:, :, 0:CTX], ACT.Identity).then_inc(s_cta, 1)

            def context_hi(n, b, c):
                if c == 0:
                    act.wait_ge(s_cf, 5 * n + 5)
                act.activation(cxp[b % 2][0:CP[c], 0, c, :], cx[0:CP[c], c, :], ACT.Identity,
                               scale=fc[0:CP[c], b:b + 1]).then_inc(s_ch, 1)

            def x2t_hi(n):
                for j in range(2):
                    act.wait_ge(s_x2t, 2 * n + j + 1)
                    act.activation(x2t[:, 0, 4 * j:4 * j + 4, bass.ds(n * S, S)],
                                   bk[j][:, 0:TG].rearrange("p (a t) -> p a t", a=4),
                                   ACT.Identity, scale=XS).then_inc(s_hi, 1)

            def probs_hi(n):
                act.wait_ge(s_pt3, n + 1)
                for c in range(CC):
                    ins = act.activation(pt3[0:CP[c], 0, c, :], bk[4][0:CP[c], c * P:c * P + S], ACT.Identity, scale=XS)
                ins.then_inc(s_ph, 1)

            def cross_attention(g, more):
                for b, n, has in batches(g, more):
                    if has(1):
                        context_t(n + 1, CT_ACT[:4])
                    act.wait_ge(s_lm, n + 1)
                    act.activation(sp_[0:S, 0:CTX], sp_[0:S, 0:CTX], ACT.Exp, bias=nm3[0:S, :],
                                   accum_out=rs3[0:S, b:b + 1]).then_inc(s_ex3, 1)
                    if has(2):
                        g_out(KC + 4 * n, 4 * (b % 2), 1 - b // 2)
                    if has(1):
                        context_t(n + 1, CT_ACT[4:])
                    if has(2):
                        g_out(KC + 4 * n + 1, 4 * (b % 2) + 1, 1 - b // 2)
                    probs_hi(n)
                    if has(2):
                        g_out(KC + 4 * n + 2, 4 * (b % 2) + 2, 1 - b // 2)
                        act.wait_ge(s_at, 2 * n + 2)
                        context_hi(n + 2, (b + 2) % GB, 0)
                        g_out(KC + 4 * n + 3, 4 * (b % 2) + 3, 1 - b // 2)
                        for c in range(1, CC):
                            context_hi(n + 2, (b + 2) % GB, c)
                    if not known(n, 1):
                        x2t_hi(n - 1)
                    if more:
                        x1t_hi(n + GB, b)

            with act.Fori(0, KC // 2 - 1) as e:
                for i in range(2):
                    m_chunk(e, i, True)
            x1t_hi(0, 0, 4)
            x1t_hi(1, 1, 6)
            for i in range(2):
                act.wait_ge(s_yout[i], 16 * (NB // 2 + 1))
            for m in (2, 3):
                act.dma_start(xs3[0:S, m % 2, :], x1_d[m * S:(m + 1) * S, :]).then_inc(s_xs3[m % 2], 16)
            m_chunk(KC // 2 - 1, 0, False)
            x1t_hi(2, 2, 4)
            x1t_hi(3, 3, 6)
            for c in range(CC):
                context_hi(0, 0, c)
            m_chunk(KC // 2 - 1, 1, False)
            act.wait_ge(s_v2, 1)
            act.activation(v2, bk[6][:, 0:KC], ACT.Identity)
            act.activation(c0[0:S, :], bk[6][0:S, KC:KC + 1], ACT.Identity).then_inc(s_v2e, 1)
            context_t(0, CT_ACT[:4])
            act.wait_ge(s_fs, T["fm"])
            act.wait_ge(s_me, KC + 2)
            for c in reversed(range(KC)):
                if c < KC - 2:
                    act.wait_ge(s_ml, KC - 2 - c)
                act.activation(mp[:, c, 0, :], m32[:, c, :], ACT.Identity, scale=fm).then_inc(s_mh, 1)
            context_t(0, CT_ACT[4:])
            act.wait_ge(s_fs, T["g"])
            act.wait_ge(s_stash, 16)
            for y in range(KC):
                g_out(y, y, 0)
                if y == 0:
                    act.wait_ge(s_t, T["tab2"])
                if y < CC:
                    context_hi(1, 1, y)
            cross_attention(0, True)
            with act.Fori(1, NG - 1) as g:
                cross_attention(g, True)
            cross_attention(NG - 1, False)
            x2t_hi(NB - 1)

            def high_part(q, dst, kind):
                act.wait_ge(s_wf, q + 1)
                src = wbuf[kind]
                if kind < 2:
                    src = src.rearrange("p (j n) -> p j n", j=8)
                act.activation(dst, src, ACT.Identity).then_inc(s_wh, 1)

            def hidden(i, t):
                joint = is_last(i)
                n = LASTC if joint else P
                act.wait_ge(s_gp, 4 * i + t + 1)
                act.wait_ge(s_hf, 4 * i + t + 2)
                act.activation(g_act[0:n, :], bk[t % 2][0:n, 0:TG], ACT.Silu, scale=inv_g[0:n, :]).then_inc(s_si, 1)
                if joint:
                    act.activation(up_c[0:n, :], bk[t % 2][P - n:P, 0:TG], ACT.Identity).then_inc(s_uo, 1)
                if t % 2 == 0:
                    act.wait_ge(s_ho[t // 2], 32 * (i + 1))
                act.wait_ge(s_hf, 4 * i + t + 3)
                act.activation(h_st[0:n, 0, t * TG:(t + 1) * TG], h_f[0:n, :], ACT.Identity).then_inc(s_hh, 1)

            def chunk(i, s, more):
                hidden(i, 0)
                if more:
                    high_part(3 * i + 2, wgu[1 - s][0][:, 0, :, :], 0)
                hidden(i, 1)
                if more and not (known(i, NI) and i == NI - 2):
                    high_part(3 * i + 3, wgu[1 - s][1][:, 0, :, :], 1)
                if is_last(i):
                    high_part(down_no(i), wd_parts(i)[0], 2)
                hidden(i, 2)
                if not is_last(i):
                    high_part(down_no(i), wd_parts(i)[0], 2)
                hidden(i, 3)

            for m in range(2):
                high_part(m, wgu[0][m][:, 0, :, :], m)
            with act.Fori(0, NI // 2 - 1) as e:
                for s in range(2):
                    chunk(2 * e + s, s, True)
            chunk(NI - 2, 0, True)
            chunk(NI - 1, 1, False)

        @block.tensor
        def _(pe):
            def transposed_rows(g, places):
                for k in places:
                    if k == 0:
                        for b in range(GB):
                            pe.wait_ge(s_xs[b], 16 * (g + 1))
                    if k >= 4:
                        pe.wait_ge(s_xl, KC * g + k - 3)
                    for b in range(GB):
                        mm = pe.transpose(bk[xt_bank[k % 4]][:, b * S:(b + 1) * S], xs[0:S, b, KC - 1 - k::KC],
                                          ident[0:S, 0:S])
                    mm.then_inc(s_xt, 1)

            def product(out, pairs, last=None):
                for k, (a, r) in enumerate(pairs):
                    mm = pe.matmul(out, a, r, start=(k == 0), stop=(k == len(pairs) - 1))
                return mm

            pe.wait_ge(s_const, 4)
            def self_attention(g, more):
                pe.wait_ge(s_xl, KC * (g + 1))
                if known(g, 1):
                    for c in reversed(range(KC)):
                        pe.wait_ge(s_wpl, KC - c)
                        for f in range(2):
                            for w, a in PASSES:
                                mm = pe.matmul(bk[2 + f][:, 0:TG], wqp[:, c, w, f * P:(f + 1) * P], xtp[:, a, c, :],
                                               start=(c == KC - 1 and (w, a) == PASSES[0]),
                                               stop=(c == 0 and (w, a) == PASSES[-1]))
                            if c == 0:
                                mm.then_inc(s_qk, 1)
                for f in range(2 if known(g, 1) else 0, 2 * HC):
                    if f >= 2:
                        pe.wait_ge(s_qke, 2 * HC * g + f - 1)
                    product(bk[2 + f % 2][:, 0:TG], [(wqp[:, c, w, f * P:(f + 1) * P], xtp[:, a, c, :])
                                                     for c in range(KC) for w, a in PASSES]).then_inc(s_qk, 1)
                def v_rows(b):
                    t = slice(b * S, (b + 1) * S)
                    return product(bk[4 + b // 2][0:S, (b % 2) * HD:(b % 2 + 1) * HD],
                                   [(xtp[:, a, c, t], wqp[:, c, w, 2 * HD:3 * HD]) for c in range(KC) for w, a in PASSES])

                if not known(g, 1):
                    pe.wait_ge(s_y, 2 * GB * g)
                v_rows(0)
                pe.wait_ge(s_qke, 2 * HC * (g + 1))
                for b in range(GB):
                    t = slice(b * S, (b + 1) * S)
                    mm = product(bk[2][0:S, t], [(qkt[:, c, t], qkt[:, HC + c, t]) for c in range(HC)])
                mm.then_inc(s_s, 1)
                for b in range(1, GB):
                    mm = v_rows(b)
                    if b % 2:
                        mm.then_inc(s_v, 1)
                pe.wait_ge(s_p, g + 1)
                pe.wait_ge(s_ve, 2 * g + 1)
                for b in range(GB):
                    mm = pe.transpose(bk[4][0:S, b * S:(b + 1) * S], pr[0:S, b, :], ident[0:S, 0:S])
                mm.then_inc(s_pt, 1)
                if more:
                    transposed_rows(g + 1, range(4))
                pe.wait_ge(s_pte, g + 1)
                pe.wait_ge(s_ve, 2 * (g + 1))
                for c in range(HC):
                    for b in range(GB):
                        mm = product(bk[3 - c][:, b * S:(b + 1) * S],
                                     [(v_sb[0:S, b, c * P:(c + 1) * P], pt[0:S, b, :])])
                    mm.then_inc(s_o, 1)
                if more:
                    transposed_rows(g + 1, range(4, KC))
                pe.wait_ge(s_ol, HC * (g + 1))
                for b in range(GB):
                    if b == 1 and more:
                        pe.wait_ge(s_xl, KC * (g + 2))
                    for h in range(2):
                        if b > 1:
                            pe.wait_ge(s_y, 2 * (g * GB + b - 2) + h + 1)
                        if known(g * GB + b, 1):
                            pe.wait_ge(s_wol, HC)
                        product(bk[4 + 2 * (b % 2) + h][0:S, :],
                                [(otp[:, a, c, b * S:(b + 1) * S], wop[:, c, w, h * HALF:(h + 1) * HALF])
                                 for c in range(HC) for w, a in PASSES]).then_inc(s_w, 1)

            transposed_rows(0, range(KC))
            self_attention(0, True)
            with pe.Fori(1, NG - 1) as g:
                self_attention(g, True)
            self_attention(NG - 1, False)

            pe.wait_ge(s_wk, 48)
            def x1_transposed(m, b, bank=2, g_out=None):
                pe.wait_ge(s_xs3[b % 2], 8 * (m - b % 2) + 16)
                for j in range(2):
                    if g_out is not None:
                        pe.wait_ge(s_ge, g_out - 1 + j)
                    for a in range(4):
                        mm = pe.transpose(bk[bank + j][:, a * S:(a + 1) * S],
                                          xs3[0:S, b % 2, (4 * j + a) * P:(4 * j + a + 1) * P], ident[0:S, 0:S])
                    mm.then_inc(s_x1t, 1)

            def m_chunk(e, i):
                pe.wait_ge(s_wq[i], 16 * (e + 1))
                pe.wait_ge(s_me, 2 * e + i + 1)
                for h in range(2):
                    mm = product(bk[2 * i + h], [(wq[i][:, c, :], wk[:, c, h * HALF:(h + 1) * HALF])
                                                 for c in range(KC)])
                mm.then_inc(s_m, 1)

            with pe.Fori(0, KC // 2 - 1) as e:
                for i in range(2):
                    m_chunk(e, i)
            for i in range(2):
                if i:
                    pe.wait_ge(s_x1l, 4)
                x1_transposed(2 * i, 2 * i, 4)
                x1_transposed(2 * i + 1, 2 * i + 1, 6)
                m_chunk(KC // 2 - 1, i)
            pe.wait_ge(s_x1l, 2 * GB)
            pe.wait_ge(s_pv, 5)
            pe.wait_ge(s_pu, 2 * KC)
            for y in range(KC):
                pe.matmul(bk[6][:, y:y + 1], acc_v[:, y * P:(y + 1) * P], ones[:], start=True, stop=True)
            pe.matmul(bk[6][0:S, KC:KC + 1], pc[:, 0:1].to_broadcast([P, S]), ones[:], start=True, stop=True).then_inc(s_v2, 1)
            pe.wait_ge(s_uc, 4 * KC)
            for h in range(2):
                mm = pe.matmul(psum[0:S, 2048 + h * HALF:2048 + (h + 1) * HALF], ones[:].to_broadcast([P, S]),
                               acc_u[:, h * HALF:(h + 1) * HALF], start=True, stop=True)
            mm.then_inc(s_ub, 1)

            def g_chunk(y, q):
                product(bk[2 + y % 2][:, 0:2 * S],
                        [(mp[:, c, w, y * P:(y + 1) * P], xtp[:, a, c, q * 2 * S:(q + 1) * 2 * S])
                         for c in range(KC) for w, a in PASSES]).then_inc(s_g, 1)

            def context_t(n, b, chunks=range(KC)):
                if chunks[0] == 0:
                    pe.wait_ge(s_cl, CC * (n + 1))
                for c in chunks:
                    if c == 2 and known(n, 1):
                        pe.wait_ge(s_v2e, 1)
                    elif c == 2 and not known(n, 2):
                        pe.wait_ge(s_y3, 2 * (n - 1))
                    if c == 0 and not known(n, 2):
                        pe.wait_ge(s_lo, 2 * (n - 1) - 1)
                    if c in (4, 5, 6, 7):
                        if c - 4 in CT_ACT:
                            pe.wait_ge(s_cta, NA * n + CT_ACT.index(c - 4) + 1)
                        else:
                            pe.wait_ge(s_ctd, ND * n + CT_DVE.index(c - 4) + 1)
                    for l in range(2):
                        for r in range(CC):
                            mm = pe.transpose(bkh[ct_bank[c % 4]][:, l, r * P:r * P + CP[r]],
                                              cxp[b % 2][0:CP[r], l, r, c * P:(c + 1) * P], ident_h[0:CP[r], 0:CP[r]])
                    mm.then_inc(s_ct, 1)

            def context_t_out(n):
                pe.wait_ge(s_cta, NA * (n + 1))
                pe.wait_ge(s_ctd, ND * (n + 1))

            def logits(n, b):
                if b % 2 == 0:
                    pe.wait_ge(s_gl, KC + 4 * n)
                product(bk[5][0:S, 0:CTX], [(gtp[:, w, c, b * S:(b + 1) * S], cxt[:, a, c, :])
                                            for c in range(KC) for w, a in PASSES]).then_inc(s_l, 1)

            def probs_t(n):
                pe.wait_ge(s_ex3, n + 1)
                for r in range(CC):
                    mm = pe.transpose(bk[4][0:CP[r], r * P:r * P + S], sp_[0:S, r * P:r * P + CP[r]],
                                      ident[0:S, 0:S])
                mm.then_inc(s_pt3, 1)

            def attended(n, b):
                pe.wait_ge(s_pl, n + 1)
                for h in range(2):
                    product(bk[6 + h][0:S, :], [(pt3[0:CP[r], w, r, :], cxp[b % 2][0:CP[r], a, r, h * HALF:(h + 1) * HALF])
                                                for r in range(CC) for w, a in PASSES]).then_inc(s_at, 1)

            def x2_transposed(n, b):
                pe.wait_ge(s_n, NB + n + 1)
                for j in range(2):
                    for a in range(4):
                        mm = pe.transpose(bk[j][:, a * S:(a + 1) * S], yo[0:S, b % 2, 4 * j + a::KC],
                                          ident[0:S, 0:S])
                    mm.then_inc(s_x2t, 1)

            def cross_attention(g, more):
                for b, n, has in batches(g, more):
                    if known(n, 1):
                        context_t_out(0)
                    logits(n, b)
                    if has(1):
                        context_t(n + 1, (b + 1) % GB, range(KC // 2))
                    if has(2):
                        pe.wait_ge(s_x1l, 2 * (n + GB) if more else 2 * NB)
                        g_chunk(4 * (b % 2), 1 - b // 2)
                    if has(1):
                        context_t(n + 1, (b + 1) % GB, range(KC // 2, KC))
                    if has(2):
                        g_chunk(4 * (b % 2) + 1, 1 - b // 2)
                    probs_t(n)
                    if has(2):
                        pe.wait_ge(s_ge, KC + 4 * n + 1)
                        g_chunk(4 * (b % 2) + 2, 1 - b // 2)
                    if has(1):
                        context_t_out(n + 1)
                    attended(n, b)
                    if has(2):
                        pe.wait_ge(s_ge, KC + 4 * n + 2)
                        g_chunk(4 * (b % 2) + 3, 1 - b // 2)
                    if not known(n, 1):
                        if not known(n, 2):
                            pe.wait_ge(s_lo, 2 * (n - 1) + 1)
                        x2_transposed(n - 1, (b + 1) % 2)
                    if more:
                        x1_transposed(n + GB, b, g_out=KC + 4 * n + 4)

            pe.wait_ge(s_me, KC + 2)
            pe.wait_ge(s_ih, 1)
            context_t(0, 0)
            for c in reversed(range(KC)):
                pe.wait_ge(s_ml, KC - c)
                for y in range(2):
                    for w, a in PASSES:
                        mm = pe.matmul(bk[2 + y][:, 0:2 * S], mp[:, c, w, y * P:(y + 1) * P], xtp[:, a, c, 0:2 * S],
                                       start=(c == KC - 1 and (w, a) == PASSES[0]),
                                       stop=(c == 0 and (w, a) == PASSES[-1]))
                    if c == 0:
                        mm.then_inc(s_g, 1)
            for y in range(2, KC):
                pe.wait_ge(s_ge, y - 1)
                g_chunk(y, 0)
            pe.wait_ge(s_ube, 1)
            cross_attention(0, True)
            with pe.Fori(1, NG - 1) as g:
                cross_attention(g, True)
            cross_attention(NG - 1, False)
            def gather(q, parts):
                if not isinstance(q, int) or q > 0:
                    pe.wait_ge(s_wf, q)
                for base, pieces in ((2048, parts[0]), (3072, parts[1])):
                    for k, (a, r) in enumerate(pieces):
                        w = 1024 // len(pieces)
                        mm = pe.matmul(psum[:, base + k * w:base + (k + 1) * w], a, r, start=True, stop=True)
                mm.then_inc(s_ga, 1)

            def gather_gu(q, m, s, e):
                pe.wait_ge(s_tc[s], 16 * (e + 1))
                gather(q, [[(sel[m][:, j, :], tabc[s][:, m, :]) for j in range(8)] for sel in (sel_s, sel_z)])

            def gather_last(q, s, e):
                pe.wait_ge(s_tc[s], 16 * (e + 1))
                gather(q, [[(sel[m][:, j, :], tabc[s][:, m, 0:LASTC]) for j in range(8) for m in range(2)]
                           for sel in (sel_s, sel_z)])

            def gather_down(q, i):
                pe.wait_ge(s_unstash, 16)
                one = sel_d[:, i, :] if isinstance(i, int) else \
                    sel_d[:, bass.ds(i, 1), :].rearrange("p a b -> p (a b)")
                gather(q, [[(one, t[:, h * HALF:(h + 1) * HALF]) for h in range(2)] for t in (tab_ds, tab_dz)])

            def chunk(i, s, e, more):
                pe.wait_ge(s_wl, 3 * i + 1)
                last, joint = known(i, NI) and i == NI - 2, is_last(i)
                for t in range(4):
                    cols = slice(t * TG, (t + 1) * TG)
                    pe.wait_ge(s_hf, 4 * i + t + 1)
                    for m, done in ((0, s_gp), (1, s_up))[:1 if joint else 2]:
                        if t == 0 and m == 1:
                            pe.wait_ge(s_wl, 3 * i + 2)
                        product(bk[2 * m + t % 2][:, 0:TG],
                                [(wgu[s][m][:, w, c, :], x2t[:, a, c, cols])
                                 for c in range(KC) for w, a in PASSES]).then_inc(done, 1)
                    if t == 0 and last:
                        gather_last(3 * i + 2, 1 - s, e + s)
                    elif t == 0 and more:
                        gather_gu(3 * i + 2, 0, 1 - s, e + s)
                    if t == 1 and more and not last:
                        gather_gu(3 * i + 3, 1, 1 - s, e + s)
                    if t == (1 if joint else 2):
                        gather_down(down_no(i), i)

            pe.wait_ge(s_y3, 2 * NB)
            gather_gu(0, 0, 0, 0)
            pe.wait_ge(s_lo, 2 * (NB - 1) + 1)
            x2_transposed(NB - 1, 1)
            gather_gu(1, 1, 0, 0)
            pe.wait_ge(s_lo, 2 * NB + 1)
            with pe.Fori(0, NI // 2 - 1) as e:
                for s in range(2):
                    chunk(2 * e + s, s, e, True)
            chunk(NI - 2, 0, NI // 2 - 1, True)
            chunk(NI - 1, 1, NI // 2 - 1, False)

            pe.wait_ge(s_wl, NGATHER)
            pe.wait_ge(s_h0, 32)

            def down_tile(tile, s, e):
                if known(tile, 2) and s == 1:
                    pe.wait_ge(s_ht[1], 16)
                elif not known(tile, 2):
                    pe.wait_ge(s_ht[s], 16 * (e + s))
                for c in range(2):
                    if known(tile, 2):
                        pe.wait_ge(s_hf, 4 * NI + 2 if s or c else 4 * NI + 1)
                    else:
                        pe.wait_ge(s_y5, 2 * (tile - 2) + c + 1)
                    product(bk[2 * s + c], [(ht[s][:, i, a, :], wd[:, i, w, c * HALF:(c + 1) * HALF])
                                            for i in range(NI) for w, a in PASSES]).then_inc(s_d, 1)

            for s in range(2):
                down_tile(s, s, 0)
            with pe.Fori(1, TT // 2) as e:
                for s in range(2):
                    down_tile(2 * e + s, s, e)

        @block.sync
        def _(sp):
            wqkv_v = t_in["L0_attn_Wqkv"].rearrange("(p c) f -> p c f", c=KC)
            for b in range(GB):
                sp.dma_start(xs[0:S, b, :], rows(x_rows, b)).then_inc(s_xs[b], 16)
            for h, landed in enumerate((s_w0, s_w1)):
                half = slice(h * KC // 2, (h + 1) * KC // 2)
                sp.dma_start(wqkv[:, half, :], wqkv_v[:, half, :]).then_inc(landed, 16)
            with nc.allow_non_contiguous_dma(reason="short bias columns"):
                sp.dma_start(bqk, t_in["L0_attn_bqkv"][0:2 * HD].rearrange("(c p) -> p c", p=P)).then_inc(s_bias, 16)
            sp.dma_start(vb_b, t_in["L0_attn_bqkv"][2 * HD:3 * HD].partition_broadcast(P)).then_inc(s_bias, 16)
            for m, name in enumerate(("gate", "up", "down")):
                sp.dma_start(s_flat[m], t_in[f"L0_ffn_{name}_scales"].rearrange("g n -> (g n)").rearrange(
                    "(p c) -> p c", p=P)).then_inc(s_tin[0], 16)

            def load_g_idx(m, at):
                idx = t_in[f"L0_ffn_{('gate', 'up', 'down')[m]}_g_idx"]
                sp.dma_start(tmp_i[:, at:at + idx.shape[0]], idx.partition_broadcast(P)).then_inc(s_tin[1], 16)

            load_g_idx(0, 0)
            load_g_idx(1, D)
            sp.dma_start(wo, t_in["L0_attn_Wo"].rearrange("(c p) n -> p c n", p=P)).then_inc(s_wo, 16)
            sp.dma_start(bo_b, t_in["L0_attn_bo"].partition_broadcast(P)).then_inc(s_bo, 16)
            for n in range(2):
                sp.dma_start(xr[0:S, n, :], rows(x_rows, n)).then_inc(s_xr[n], 16)
            sp.dma_start(bqc, t_in["L0_xattn_bq"].rearrange("(p c) -> p c", c=KC)).then_inc(s_wk, 16)
            sp.dma_start(bkc, t_in["L0_xattn_bk"].rearrange("(p c) -> p c", c=KC)).then_inc(s_wk, 16)
            sp.dma_start(wk, t_in["L0_xattn_Wk"].rearrange("(p c) y -> p c y", c=KC)).then_inc(s_wk, 16)
            wq_v = t_in["L0_xattn_Wq"].rearrange("(p c) x -> p c x", c=KC)
            for i in range(2):
                sp.dma_start(wq[i], wq_v[:, :, i * P:(i + 1) * P]).then_inc(s_wq[i], 16)

            def load_group(g):
                sp.wait_ge(s_xt, KC * g)
                for b in range(GB):
                    sp.dma_start(xs[0:S, b, :], rows(x_rows, g * GB + b)).then_inc(s_xs[b], 16)

            def self_attention(g, rows_next, more):
                if rows_next:
                    load_group(g + 2)
                for b in range(GB):
                    if more or b + 2 < GB:
                        sp.wait_ge(s_y, 2 * (g * GB + b + 1))
                        sp.dma_start(xr[0:S, b % 2, :], rows(x_rows, g * GB + b + 2)).then_inc(s_xr[b % 2], 16)
                    sp.wait_ge(s_n, g * GB + b + 1)
                    sp.dma_start(rows(x1_d, g * GB + b), yo[0:S, b % 2, :]).then_inc(s_yout[b % 2], 16)

            load_group(1)
            with sp.Fori(0, NG - 2) as g:
                self_attention(g, True, True)
            self_attention(NG - 2, False, True)

            def load_table(m):
                sp.wait_ge(s_t, T[f"tab{m - 1}"] if m else T["idx2"])
                name = ("gate", "up", "down")[m]
                scales, zeros = t_in[f"L0_ffn_{name}_scales"], t_in[f"L0_ffn_{name}_qzeros"]
                groups = scales.shape[0]
                sp.dma_start(tmp[0:groups, 0:scales.shape[1]], scales).then_inc(s_tin[2], 16)
                sp.dma_start(qz[96:96 + groups, 0:zeros.shape[1]], zeros.bitcast(U32)).then_inc(s_tin[3], 16)

            sp.wait_ge(s_t, T["idx1"])
            load_g_idx(2, 0)
            self_attention(NG - 1, False, False)

            for i in range(2):
                sp.wait_ge(s_yout[i], 16 * (NB // 2 + 1))

            def load_rows(m, b):
                sp.dma_start(xs3[0:S, b % 2, :], rows(x1_d, m)).then_inc(s_xs3[b % 2], 16)

            def load_residual(n, b):
                sp.dma_start(xr3[0:S, b % 2, :], rows(x1_d, n)).then_inc(s_xr3[b % 2], 16)

            ctx_rows = ctx_d.rearrange("b s d -> (b s) d")

            def load_ctx(n):
                base = n * CTX
                last = (CC - 1) * P
                even = CP[-1] // 16 * 16
                for c in range(CC - 1):
                    sp.dma_start(cx[:, c, :], ctx_rows[bass.ds(base + c * P, P), :]).then_inc(s_cx, 16)
                sp.dma_start(cx[0:even, CC - 1, :],
                             ctx_rows[bass.ds(base + last, even), :]).then_inc(s_cx, 16)
                sp.dma_start(cx[even:CP[-1], CC - 1, :],
                             ctx_rows[bass.ds(base + last + even, CP[-1] - even), :]).then_inc(s_cx, 16)

            for m in range(2):
                load_rows(m, m)

            load_ctx(0)
            load_table(0)
            for m in (1, 2):
                load_table(m)
                sp.dma_start(tab_d[:, :, m - 1, :].rearrange("i p c -> p i c"),
                             tab.rearrange("p (i c) -> p i c", c=P)).then_inc(s_tabo, 16)
            sp.wait_ge(s_t, T["tab2"])
            sp.dma_start(down_d, down_tabs).then_inc(s_stash, 16)
            sp.wait_ge(s_stash, 16)
            for n in range(2):
                load_residual(n, n)
            sp.wait_ge(s_cl, CC)
            load_ctx(1)
            for m in range(4, 6):
                sp.wait_ge(s_x1t, 2 * m - 2)
                load_rows(m, m % 2)
            sp.wait_ge(s_cl, 2 * CC)
            load_ctx(2)

            def cross_attention(g, loop):
                for b in range(GB):
                    n = g * GB + b
                    if loop or n + 2 < NB:
                        sp.wait_ge(s_y3, 2 * (n + 1))
                        load_residual(n + 2, (b + 2) % GB)
                    if loop or n + 3 < NB:
                        sp.wait_ge(s_cl, CC * (n + 3))
                        load_ctx(n + 3)
                    if loop or n + 6 < NB:
                        sp.wait_ge(s_x1t, 2 * n + 10)
                        load_rows(n + 6, (b + 2) % GB)
                    if known(n, NB) and n == NB - 1:
                        sp.wait_ge(s_l, NB)
                        load_chunk(0, 0, P)
                        load_chunk(1, 1, P)
                        sp.wait_ge(s_y3, 2 * NB)
                        sp.dma_start(down_tabs, down_d).then_inc(s_unstash, 16)
                    sp.wait_ge(s_n, NB + n + 1)
                    sp.dma_start(rows(x2_d, n), yo[0:S, b % 2, :]).then_inc(s_yout[b % 2], 16)

            def load_chunk(i, s, w):
                for m, name in enumerate(("gate", "up")):
                    to = qw[s][m][:, 0:w] if w == P else qw[s][0][:, m * w:(m + 1) * w]
                    sp.dma_start(to, t_in[f"L0_ffn_{name}_qweight"][:, bass.ds(i * P, w)].bitcast(
                        U32)).then_inc(s_qw[s], 16)
                sp.dma_start(tabc[s], tab_d[bass.ds(i, 1)].rearrange("o p m c -> p (o m) c")).then_inc(s_tc[s], 16)

            with sp.Fori(0, NG - 2) as g:
                cross_attention(g, True)
            cross_attention(NG - 2, False)
            cross_attention(NG - 1, False)

            def load_down(i, w):
                rows8 = t_in["L0_ffn_down_qweight"][bass.ds(i * (P // 8), w // 8), :]
                sp.dma_start(wbuf[2].bitcast(I32)[0:w, :], rows8.unsqueeze(1).to_broadcast([w // 8, 8, D])).then_inc(s_qd, 16)

            def load_first_tile():
                sp.wait_ge(s_up, 4 * (NI - 1))
                sp.wait_ge(s_wl, 3 * (NI - 2) + 3)
                sp.wait_ge(s_wh, 3 * (NI - 2) + 3)
                sp.wait_ge(s_ho[0], 32 * NI)
                sp.dma_start(ht[0][:, 0:NI - 1], h_d[0, :, 0:NI - 1]).then_inc(s_h0, 16)

            def chunk(i, s, w_down, w_next):
                before = NGATHER - 1 if is_last(i) else 3 * i + 2
                sp.wait_ge(s_wf, before)
                sp.wait_ge(s_wh, before)
                sp.wait_ge(s_wl, before)
                load_down(i, w_down)
                if w_next:
                    load_chunk(i + 2, s, w_next)
                if isinstance(i, int) and i == NI - 1:
                    load_first_tile()
                for u in range(2):
                    sp.wait_ge(s_hh, 4 * i + 2 * u + 3)
                    sp.wait_ge(s_hl, 4 * i + 2 * u + 3)
                    half = slice(u * TT // 2, (u + 1) * TT // 2)
                    for l in range(2):
                        sp.dma_start(h_d[half, :, bass.ds(i, 1), l, :].rearrange("t p o c -> p t (o c)"),
                                     h_st[:, l, u * NT // 2:(u + 1) * NT // 2].rearrange("p (t c) -> p t c", c=P)
                                     ).then_inc(s_ho[u], 16)
                    if u == 0 and isinstance(i, int) and i == NI - 1:
                        sp.wait_ge(s_ho[0], 32 * (NI + 1))
                        sp.dma_start(ht[0][:, NI - 1], h_d[0, :, NI - 1]).then_inc(s_h0, 16)

            sp.wait_ge(s_yout[(NB - 1) % 2], 16 * (NB + 1))
            sp.wait_ge(s_lo, 2 * NB + 1)
            with sp.Fori(0, NI // 2 - 2) as e:
                for s in range(2):
                    chunk(2 * e + s, s, P, P)
            chunk(NI - 4, 0, P, P)
            chunk(NI - 3, 1, P, LASTC)
            chunk(NI - 2, 0, P, 0)
            chunk(NI - 1, 1, LASTC, 0)

            sp.wait_ge(s_gp, 4 * NI)
            sp.wait_ge(s_hl, 4 * NI + 1)
            sp.wait_ge(s_wl, NGATHER)
            sp.wait_ge(s_wh, NGATHER)
            for u in range(2):
                sp.wait_ge(s_ho[u], 32 * (NI + 1))

            def load_tile(tile, s):
                sp.dma_start(ht[s].rearrange("p i l c -> p (i l c)"),
                             h_d[bass.ds(tile, 1)].rearrange("o p i l c -> p (o i l c)")).then_inc(s_ht[s], 16)

            def load_x2(tile, s):
                sp.dma_start(xf[s], x2_d[bass.ds(tile * P, P), :]).then_inc(s_xf[s], 16)

            out_rows = out.rearrange("b s d -> (b s) d")
            load_tile(1, 1)
            for s in range(2):
                load_x2(s, s)

            def down_tile(tile, s, more):
                if more:
                    sp.wait_ge(s_d, 2 * tile + 2)
                    load_tile(tile + 2, s)
                    sp.wait_ge(s_y5, 2 * tile + 2)
                    load_x2(tile + 2, s)
                sp.wait_ge(s_n5, tile + 1)
                sp.dma_start(out_rows[bass.ds(tile * P, P), :], yf[s]).then_inc(s_fin[s], 16)

            with sp.Fori(0, TT // 2 - 1) as e:
                for s in range(2):
                    down_tile(2 * e + s, s, True)
            for s in range(2):
                down_tile(TT - 2 + s, s, False)
            for s in range(2):
                sp.wait_ge(s_fin[s], 16 * (TT // 2 + 1))


_INS = ["x", "ctx_4096", "L0_attn_Wqkv", "L0_attn_bqkv", "L0_attn_Wo", "L0_attn_bo",
        "L0_xattn_Wq", "L0_xattn_bq", "L0_xattn_Wk", "L0_xattn_bk"] + [
    f"L0_ffn_{m}_{p}" for m in ("gate", "up", "down") for p in ("qweight", "scales", "qzeros", "g_idx")]


def kernel(**inputs):
    import numpy as _np
    import concourse.bacc as _bacc
    from concourse import mybir as _mybir
    from concourse.bass_utils import run_bass_kernel_spmd as _run

    nc = _bacc.Bacc("TRN2", target_bir_lowering=False, num_devices=1)
    arrays, t_in = {}, {}
    for name in _INS:
        a = _np.ascontiguousarray(inputs[name])
        arrays[f"in_{name}"] = a
        t_in[name] = nc.dram_tensor(f"in_{name}", a.shape, _mybir.dt.from_np(a.dtype), kind="ExternalInput").ap()
    out = nc.dram_tensor("out_0", inputs["x"].shape, _mybir.dt.float32, kind="ExternalOutput").ap()
    decoder_layer(nc, t_in, out)
    r = _run(nc, [arrays], core_ids=[0])
    return r.results[0]["out_0"]
```
